# Optimizing a Trainium2 kernel written in Bass

```python
import numpy as np
import jax
import jax.numpy as jnp

def _softmax(x, axis=-1):
    return jax.nn.softmax(x, axis=axis)

def _gelu(x):
    return jax.nn.gelu(x, approximate=True)

def _silu(x):
    return jax.nn.silu(x)

def _sigmoid(x):
    return jax.nn.sigmoid(x)

def _layernorm(x, axis=-1, eps=1e-05):
    m = jnp.mean(x, axis=axis, keepdims=True)
    v = jnp.var(x, axis=axis, keepdims=True)
    return (x - m) / jnp.sqrt(v + eps)

def _scatter_add(tgt, idx, src, axis=0):
    return tgt.at[idx].add(src)

def _segment_sum(src, seg, n):
    return jax.ops.segment_sum(src, seg, n)
kernel_name = 'mk_macaron_d2_jaxref_r8_0a67de'

def setup_inputs(seed: int=0):
    np.random.seed(seed)
    _w = jnp.asarray

    def _L0_attn_setup():
        import jax, jax.numpy as jnp
        import numpy as np
        B, T, D = (1, 256, 256)
        H, DK, DV, M = (16, 64, 128, 64)
        KEY_DIM, VALUE_DIM = (H * DK, H * DV)
        EPS = 1e-05
        CLAMP_MIN, CLAMP_MAX = (-32.0, 32.0)
        XAVIER_GAIN = 2.0 ** (-2.5)

        def _chunk_abc(q, k, v, s):
            scale = q.shape[-1] ** (-0.5)
            z = jax.lax.cumlogsumexp(s, axis=2)
            g = jnp.exp(jnp.concatenate([z[:, :, :1], z[:, :, :-1]], axis=2) - z)
            p = jnp.exp(s - z)
            tfirst = lambda x: jnp.moveaxis(x, 2, 0)
            qT, kT, vT, pT, gT = map(tfirst, (q * scale, k, v, p, g))
            b, h = (q.shape[0], q.shape[1])
            hk0 = jnp.zeros((b, h, q.shape[-1], s.shape[-1]), q.dtype)

            def step_k(hk, x):
                q_t, k_t, p_t, g_t = x
                hk = hk * g_t[:, :, None, :] + k_t[..., None] * p_t[:, :, None, :]
                return (hk, jnp.einsum('bhk,bhkm->bhm', q_t, hk))
            _, okT = jax.lax.scan(step_k, hk0, (qT, kT, pT, gT))
            pvT = jax.nn.softmax(okT, axis=-1)
            hv0 = jnp.zeros((b, h, s.shape[-1], v.shape[-1]), q.dtype)

            def step_v(hv, x):
                pv_t, v_t, p_t, g_t = x
                hv = hv * g_t[..., None] + p_t[..., None] * v_t[:, :, None, :]
                return (hv, jnp.einsum('bhm,bhmv->bhv', pv_t, hv))
            _, ovT = jax.lax.scan(step_v, hv0, (pvT, vT, pT, gT))
            return jnp.moveaxis(ovT, 0, 2)
        key = jax.random.key(seed)
        ks = jax.random.split(key, 8)

        def w(k, fan_in, fan_out):
            std = XAVIER_GAIN * np.sqrt(2.0 / (fan_in + fan_out))
            return jax.random.normal(k, (fan_in, fan_out), jnp.float32) * std
        return {'hidden_states': jax.random.normal(ks[0], (B, T, D), jnp.float32), 'Wq': w(ks[1], D, KEY_DIM), 'Wk': w(ks[2], D, KEY_DIM), 'Wv': w(ks[3], D, VALUE_DIM), 'Wg': w(ks[4], D, VALUE_DIM), 'Ws': w(ks[5], D, H * M), 'Wo': w(ks[6], VALUE_DIM, D), 'g_norm_weight': jnp.ones((DV,), jnp.float32)}
    _L0_attn_in = _L0_attn_setup()

    def _L0_ffn_setup():
        import jax, jax.numpy as jnp
        import numpy as np
        B, S, D = (2, 256, 256)
        F = 128
        E = 64
        K = 8
        C = 128
        NORM_TOPK = False

        def _moe(x, gate_w, w_gate, w_up, w_down):
            b, s, d = x.shape
            T = b * s
            x2 = x.reshape(T, d)
            logits = x2 @ gate_w.T
            probs = jax.nn.softmax(logits.astype(jnp.float32), axis=-1)
            top_w, top_i = jax.lax.top_k(probs, K)
            if NORM_TOPK:
                top_w = top_w / jnp.sum(top_w, axis=-1, keepdims=True)
            top_w = top_w.astype(x.dtype)
            flat_e = top_i.reshape(-1)
            flat_w = top_w.reshape(-1)
            tok = jnp.arange(T * K) // K
            onehot = jax.nn.one_hot(flat_e, E, dtype=jnp.int32)
            pos = jnp.sum(jnp.cumsum(onehot, axis=0) * onehot, axis=-1) - 1
            valid = pos < C
            loc = flat_e * C + jnp.minimum(pos, C - 1)
            flat_w = jnp.where(valid, flat_w, 0.0)
            safe_loc = jnp.where(valid, loc, E * C)
            xg = jnp.zeros((E * C + 1, d), dtype=x.dtype).at[safe_loc].set(x2[tok])[:E * C]
            xg = xg.reshape(E, C, d)
            h = jax.nn.silu(jnp.einsum('ecd,edf->ecf', xg, w_gate)) * jnp.einsum('ecd,edf->ecf', xg, w_up)
            y = jnp.einsum('ecf,efd->ecd', h, w_down).reshape(E * C, d)
            y_tok = y[loc] * flat_w[:, None]
            out = jnp.zeros((T, d), dtype=x.dtype).at[tok].add(y_tok)
            return out.reshape(b, s, d)
        key = jax.random.key(seed)
        ks = jax.random.split(key, 5)
        scale = 0.02
        return {'hidden_states': jax.random.normal(ks[0], (B, S, D), dtype=jnp.float32), 'gate_w': jax.random.normal(ks[1], (E, D), dtype=jnp.float32) * scale, 'w_gate': jax.random.normal(ks[2], (E, D, F), dtype=jnp.float32) * scale, 'w_up': jax.random.normal(ks[3], (E, D, F), dtype=jnp.float32) * scale, 'w_down': jax.random.normal(ks[4], (E, F, D), dtype=jnp.float32) * scale}
    _L0_ffn_in = _L0_ffn_setup()

    def _L1_attn_setup():
        import jax, jax.numpy as jnp
        import numpy as np
        EPS = 1e-05
        key = jax.random.key(seed)
        ks = jax.random.split(key, 6)
        B, T, H = (4, 256, 256)
        scale = 2 ** (-2.5) * (6.0 / (H + H)) ** 0.5
        return {'hidden_states': jax.random.normal(ks[0], (B, T, H), dtype=jnp.float32), 'Wi': jax.random.normal(ks[1], (H, H), dtype=jnp.float32) * scale, 'Wf': jax.random.normal(ks[2], (H, H), dtype=jnp.float32) * scale, 'Wg': jax.random.normal(ks[3], (H, H), dtype=jnp.float32) * scale, 'Wo': jax.random.normal(ks[4], (H, H), dtype=jnp.float32) * scale, 'gnorm_w': jnp.ones((H,), dtype=jnp.float32)}
    _L1_attn_in = _L1_attn_setup()

    def _L1_ffn_setup():
        import jax, jax.numpy as jnp
        import numpy as np
        HIDDEN = 256
        INTER = 688
        LUT_SIZE = 16

        def _ghost_linear(x, idx, lut):
            w = lut[idx]
            return jnp.einsum('bsh,oh->bso', x, w)
        key = jax.random.key(seed)
        k_x, k_lut, k_g, k_u, k_d = jax.random.split(key, 5)
        x = jax.random.normal(k_x, (2, 512, HIDDEN), dtype=jnp.float32)
        lut = jax.random.normal(k_lut, (LUT_SIZE,), dtype=jnp.float32) * 0.02
        gate_idx = jax.random.randint(k_g, (INTER, HIDDEN), 0, LUT_SIZE, dtype=jnp.int32)
        up_idx = jax.random.randint(k_u, (INTER, HIDDEN), 0, LUT_SIZE, dtype=jnp.int32)
        down_idx = jax.random.randint(k_d, (HIDDEN, INTER), 0, LUT_SIZE, dtype=jnp.int32)
        return {'x': x, 'lut': lut, 'gate_idx': gate_idx, 'up_idx': up_idx, 'down_idx': down_idx}
    _L1_ffn_in = _L1_ffn_setup()
    _d = {'L0_attn_hidden_states': _L0_attn_in['hidden_states'], 'L0_attn_Wq': _L0_attn_in['Wq'], 'L0_attn_Wk': _L0_attn_in['Wk'], 'L0_attn_Wv': _L0_attn_in['Wv'], 'L0_attn_Wg': _L0_attn_in['Wg'], 'L0_attn_Ws': _L0_attn_in['Ws'], 'L0_attn_Wo': _L0_attn_in['Wo'], 'L0_attn_g_norm_weight': _L0_attn_in['g_norm_weight'], 'L0_ffn_gate_w': _L0_ffn_in['gate_w'], 'L0_ffn_w_gate': _L0_ffn_in['w_gate'], 'L0_ffn_w_up': _L0_ffn_in['w_up'], 'L0_ffn_w_down': _L0_ffn_in['w_down'], 'L1_attn_Wi': _L1_attn_in['Wi'], 'L1_attn_Wf': _L1_attn_in['Wf'], 'L1_attn_Wg': _L1_attn_in['Wg'], 'L1_attn_Wo': _L1_attn_in['Wo'], 'L1_attn_gnorm_w': _L1_attn_in['gnorm_w'], 'L1_ffn_lut': _L1_ffn_in['lut'], 'L1_ffn_gate_idx': _L1_ffn_in['gate_idx'], 'L1_ffn_up_idx': _L1_ffn_in['up_idx'], 'L1_ffn_down_idx': _L1_ffn_in['down_idx']}
    _x0 = _d['L0_attn_hidden_states']
    _d['L0_attn_hidden_states'] = jax.random.normal(jax.random.fold_in(jax.random.key(seed), 1), (16, 256, 256), dtype=_x0.dtype)
    del _x0
    return _d

def reference(L0_attn_hidden_states, L0_attn_Wq, L0_attn_Wk, L0_attn_Wv, L0_attn_Wg, L0_attn_Ws, L0_attn_Wo, L0_attn_g_norm_weight, L0_ffn_gate_w, L0_ffn_w_gate, L0_ffn_w_up, L0_ffn_w_down, L1_attn_Wi, L1_attn_Wf, L1_attn_Wg, L1_attn_Wo, L1_attn_gnorm_w, L1_ffn_lut, L1_ffn_gate_idx, L1_ffn_up_idx, L1_ffn_down_idx):

    def _L0_attn_ref(hidden_states, Wq, Wk, Wv, Wg, Ws, Wo, g_norm_weight):
        import jax, jax.numpy as jnp
        import numpy as np
        B, T, D = (1, 256, 256)
        H, DK, DV, M = (16, 64, 128, 64)
        KEY_DIM, VALUE_DIM = (H * DK, H * DV)
        EPS = 1e-05
        CLAMP_MIN, CLAMP_MAX = (-32.0, 32.0)
        XAVIER_GAIN = 2.0 ** (-2.5)

        def _chunk_abc(q, k, v, s):
            scale = q.shape[-1] ** (-0.5)
            z = jax.lax.cumlogsumexp(s, axis=2)
            g = jnp.exp(jnp.concatenate([z[:, :, :1], z[:, :, :-1]], axis=2) - z)
            p = jnp.exp(s - z)
            tfirst = lambda x: jnp.moveaxis(x, 2, 0)
            qT, kT, vT, pT, gT = map(tfirst, (q * scale, k, v, p, g))
            b, h = (q.shape[0], q.shape[1])
            hk0 = jnp.zeros((b, h, q.shape[-1], s.shape[-1]), q.dtype)

            def step_k(hk, x):
                q_t, k_t, p_t, g_t = x
                hk = hk * g_t[:, :, None, :] + k_t[..., None] * p_t[:, :, None, :]
                return (hk, jnp.einsum('bhk,bhkm->bhm', q_t, hk))
            _, okT = jax.lax.scan(step_k, hk0, (qT, kT, pT, gT))
            pvT = jax.nn.softmax(okT, axis=-1)
            hv0 = jnp.zeros((b, h, s.shape[-1], v.shape[-1]), q.dtype)

            def step_v(hv, x):
                pv_t, v_t, p_t, g_t = x
                hv = hv * g_t[..., None] + p_t[..., None] * v_t[:, :, None, :]
                return (hv, jnp.einsum('bhm,bhmv->bhv', pv_t, hv))
            _, ovT = jax.lax.scan(step_v, hv0, (pvT, vT, pT, gT))
            return jnp.moveaxis(ovT, 0, 2)
        b, t, _ = hidden_states.shape
        to_heads = lambda x, d: jnp.transpose(x.reshape(b, t, H, d), (0, 2, 1, 3))
        q = to_heads(hidden_states @ Wq, DK)
        k = to_heads(hidden_states @ Wk, DK)
        v = to_heads(hidden_states @ Wv, DV)
        s = jnp.clip(to_heads(hidden_states @ Ws, M), CLAMP_MIN, CLAMP_MAX)
        o = jnp.transpose(_chunk_abc(q, k, v, s), (0, 2, 1, 3))
        g = (hidden_states @ Wg).reshape(b, t, H, DV)
        o = o * jax.lax.rsqrt(jnp.mean(jnp.square(o), axis=-1, keepdims=True) + EPS) * g_norm_weight
        o = o * (g * jax.nn.sigmoid(g))
        return o.reshape(b, t, VALUE_DIM) @ Wo

    def _L0_ffn_ref(hidden_states, gate_w, w_gate, w_up, w_down):
        import jax, jax.numpy as jnp
        import numpy as np
        B, S, D = (2, 256, 256)
        F = 128
        E = 64
        K = 8
        C = 128
        NORM_TOPK = False

        def _moe(x, gate_w, w_gate, w_up, w_down):
            b, s, d = x.shape
            T = b * s
            x2 = x.reshape(T, d)
            logits = x2 @ gate_w.T
            probs = jax.nn.softmax(logits.astype(jnp.float32), axis=-1)
            top_w, top_i = jax.lax.top_k(probs, K)
            if NORM_TOPK:
                top_w = top_w / jnp.sum(top_w, axis=-1, keepdims=True)
            top_w = top_w.astype(x.dtype)
            flat_e = top_i.reshape(-1)
            flat_w = top_w.reshape(-1)
            tok = jnp.arange(T * K) // K
            onehot = jax.nn.one_hot(flat_e, E, dtype=jnp.int32)
            pos = jnp.sum(jnp.cumsum(onehot, axis=0) * onehot, axis=-1) - 1
            valid = pos < C
            loc = flat_e * C + jnp.minimum(pos, C - 1)
            flat_w = jnp.where(valid, flat_w, 0.0)
            safe_loc = jnp.where(valid, loc, E * C)
            xg = jnp.zeros((E * C + 1, d), dtype=x.dtype).at[safe_loc].set(x2[tok])[:E * C]
            xg = xg.reshape(E, C, d)
            h = jax.nn.silu(jnp.einsum('ecd,edf->ecf', xg, w_gate)) * jnp.einsum('ecd,edf->ecf', xg, w_up)
            y = jnp.einsum('ecf,efd->ecd', h, w_down).reshape(E * C, d)
            y_tok = y[loc] * flat_w[:, None]
            out = jnp.zeros((T, d), dtype=x.dtype).at[tok].add(y_tok)
            return out.reshape(b, s, d)
        return _moe(hidden_states, gate_w, w_gate, w_up, w_down)

    def _L1_attn_ref(hidden_states, Wi, Wf, Wg, Wo, gnorm_w):
        import jax, jax.numpy as jnp
        import numpy as np
        EPS = 1e-05
        i = jnp.einsum('bth,dh->btd', hidden_states, Wi)
        f = jnp.einsum('bth,dh->btd', hidden_states, Wf)
        g = jnp.einsum('bth,dh->btd', hidden_states, Wg)
        gate = jax.nn.sigmoid(f)
        v = jax.nn.silu(i) * (1.0 - gate)

        def combine(c1, c2):
            a1, b1 = c1
            a2, b2 = c2
            return (a1 * a2, a2 * b1 + b2)
        _, o = jax.lax.associative_scan(combine, (gate, v), axis=1)
        rms = o * jax.lax.rsqrt(jnp.mean(o * o, axis=-1, keepdims=True) + EPS)
        o = rms * gnorm_w * g * jax.nn.sigmoid(g)
        return jnp.einsum('btd,hd->bth', o, Wo)

    def _L1_ffn_ref(x, lut, gate_idx, up_idx, down_idx):
        import jax, jax.numpy as jnp
        import numpy as np
        HIDDEN = 256
        INTER = 688
        LUT_SIZE = 16

        def _ghost_linear(x, idx, lut):
            w = lut[idx]
            return jnp.einsum('bsh,oh->bso', x, w)
        gate = _ghost_linear(x, gate_idx, lut)
        up = _ghost_linear(x, up_idx, lut)
        h = jax.nn.silu(gate) * up
        return _ghost_linear(h, down_idx, lut)
    x = L0_attn_hidden_states
    x = x + 0.5 * _L0_ffn_ref(_layernorm(x, axis=-1), L0_ffn_gate_w, L0_ffn_w_gate, L0_ffn_w_up, L0_ffn_w_down)
    x = x + _L0_attn_ref(_layernorm(x, axis=-1), L0_attn_Wq, L0_attn_Wk, L0_attn_Wv, L0_attn_Wg, L0_attn_Ws, L0_attn_Wo, L0_attn_g_norm_weight)
    x = x + 0.5 * _L0_ffn_ref(_layernorm(x, axis=-1), L0_ffn_gate_w, L0_ffn_w_gate, L0_ffn_w_up, L0_ffn_w_down)
    x = x + 0.5 * _L1_ffn_ref(_layernorm(x, axis=-1), L1_ffn_lut, L1_ffn_gate_idx, L1_ffn_up_idx, L1_ffn_down_idx)
    x = x + _L1_attn_ref(_layernorm(x, axis=-1), L1_attn_Wi, L1_attn_Wf, L1_attn_Wg, L1_attn_Wo, L1_attn_gnorm_w)
    x = x + 0.5 * _L1_ffn_ref(_layernorm(x, axis=-1), L1_ffn_lut, L1_ffn_gate_idx, L1_ffn_up_idx, L1_ffn_down_idx)
    return x

_drawn_inputs = setup_inputs


def setup_inputs(seed=0):
    import zlib

    import numpy as np

    out = dict(_drawn_inputs(seed))
    spreads = {'L0_attn_g_norm_weight': (1.0, 0.6), 'L1_attn_gnorm_w': (1.0, 0.6)}
    factors = {'L0_attn_Wq': 8.0,
     'L0_attn_Wk': 8.0,
     'L0_attn_Wv': 6.029,
     'L0_attn_Wg': 6.048,
     'L0_attn_Ws': 8.0,
     'L0_attn_Wo': 6.041,
     'L0_ffn_gate_w': 8.0,
     'L0_ffn_w_gate': 8.0,
     'L0_ffn_w_up': 8.0,
     'L0_ffn_w_down': 8.0,
     'L1_attn_Wf': 6.647}
    for name, (base, spread) in spreads.items():
        noise = np.random.default_rng([zlib.crc32(name.encode()), seed]).standard_normal(out[name].shape)
        drawn = base * np.exp(spread * noise) if base else spread * noise
        out[name] = jnp.asarray(drawn.astype(out[name].dtype))
    for name, factor in factors.items():
        out[name] = (out[name] * factor).astype(out[name].dtype)
    return out
```

```python
from contextlib import ExitStack

import concourse.bass as bass
from concourse import mybir

F32 = mybir.dt.float32
U32 = mybir.dt.uint32
I32 = mybir.dt.int32
ALU = mybir.AluOpType
ACT = mybir.ActivationFunctionType
AX = mybir.AxisListType

P = 128
D = 256
DC = D // P
B, T = 16, 256
NTOK = B * T
NTILE = NTOK // P
E, F, CAP = 64, 128, 128
H, DK, DV, M = 16, 64, 128, 64
INTER = 688
NLUT = 16
FT = -(-INTER // P)
FLAST = INTER - (FT - 1) * P
EPS = 1e-5
ROW = D + E


class Mem:

    def __init__(self, nc, ctx, tag=""):
        self.nc, self.ctx, self.tag = nc, ctx, tag
        self.sems = []

    def sb(self, name, shape, dt=F32):
        return self.ctx.enter_context(self.nc.sbuf_tensor(self.tag + name, shape, dt))

    def ps(self, name, shape):
        size = 1
        for n in shape[1:]:
            size *= n
        whole = self.ctx.enter_context(self.nc.psum_tensor(self.tag + name, [P, -(-size // 512) * 512], F32))
        part = whole[0:shape[0], 0:size]
        return part.rearrange("p (a b) -> p a b", b=shape[2]) if len(shape) == 3 else part

    def sem(self, name):
        self.sems.append(self.ctx.enter_context(self.nc.semaphore(self.tag + name)))
        return self.sems[-1]

    def sem2(self, name):
        return [self.sem(name + "0"), self.sem(name + "1")]


def clear_semaphores(nc, mem):
    with nc.Block() as block:
        @block.gpsimd
        def _(pool):
            for s in mem.sems:
                pool.sem_clear(s)


def hold(engine):
    engine.nop(nofuse=True)


def constants(nc, mem):
    c = {
        "ident": mem.sb("ident", [P, P]),
        "causal": mem.sb("causal", [P, 3, P]),
        "minus_half": mem.sb("minus_half", [P, 8]),
    }
    s_set, s_cut = mem.sem("c_set"), mem.sem("c_cut")
    with nc.Block() as block:
        @block.gpsimd
        def _(pool):
            nc.gpsimd.memset(c["ident"][:, :], 0.0).then_inc(s_set, 1)
            nc.gpsimd.memset(c["causal"][:, :, :], 1.0).then_inc(s_set, 1)
            nc.gpsimd.memset(c["minus_half"][:, :], -0.5).then_inc(s_set, 1)
            pool.wait_ge(s_set, 3)
            nc.gpsimd.affine_select(out=c["ident"][:, :], in_=c["ident"][:, :], compare_op=ALU.not_equal,
                                    fill=1.0, base=0, pattern=[[-1, P]], channel_multiplier=1).then_inc(s_cut, 1)
            for blk in (0, 2):
                nc.gpsimd.affine_select(out=c["causal"][:, blk, :], in_=c["causal"][:, blk, :],
                                        compare_op=ALU.is_ge, fill=0.0, base=0, pattern=[[1, P]],
                                        channel_multiplier=-1).then_inc(s_cut, 1)
            pool.wait_ge(s_cut, 3)
    return c


def moe_router(nc, cst, tag, x_src, gate_w, rows, stream_a, stream_b, slot_tok, lookup):
    HALF = NTILE // 2
    with ExitStack() as ctx:
        mem = Mem(nc, ctx, tag)
        lut, lut_idx, lut_row, lut_w, part = lookup
        l0, l1 = lut_columns(part)
        idx_i = mem.sb("idx_i", [P, l1 - l0], I32)
        picked = mem.sb("picked", [P, l1 - l0])
        idx_set, idx_here, picked_ok, summed = (mem.sem(n) for n in ("idx_set", "idx_here", "picked_ok", "summed"))
        gw_in = mem.sb("gw_in", [E, D])
        gwT = mem.sb("gwT", [P, DC, E])
        zeros = mem.sb("zeros", [P, (NTOK // P + 1) * D])
        xt = mem.sb("xt", [P, 2, 2, D])
        bs = mem.sb("bs", [P, 2, 2, 6])
        mv = mem.sb("mv", [P, 2, 2, 2])
        ve = mem.sb("ve", [P, 2, 2])
        rstd = mem.sb("rstd", [P, 2, 2])
        row = mem.sb("row", [P, 2, 2, ROW])
        lnT = mem.sb("lnT", [P, 2, DC, 2 * P])
        lg = mem.sb("lg", [P, 2, 2, E])
        mx = mem.sb("mx", [P, 2, 2, 8])
        nm = mem.sb("nm", [P, 2, 2])
        left = mem.sb("left", [P, 2, 2, E])
        chosen = mem.sb("chosen", [P, 2, 2, E])
        ex = mem.sb("ex", [P, 2, 2, E])
        den = mem.sb("den", [P, 2, 2])
        rden = mem.sb("rden", [P, 2, 2])
        desc_i = mem.sb("desc_i", [P, HALF * P], I32)
        desc = mem.sb("desc", [P, HALF * P])
        key = mem.sb("key", [P, HALF * P])
        cand = mem.sb("cand", [P, CAP])
        both = mem.sb("both", [E, 2, CAP])
        best = mem.sb("best", [E, CAP])
        slot_i = mem.sb("slot_i", [P, 1], I32)
        slot_n = mem.sb("slot_n", [P, 1])
        pad = mem.sb("pad", [P, E])
        tok = mem.sb("tok", [P, E])
        psT = [mem.ps(f"psT{u}", [P, DC, 2 * P]) for u in range(2)]
        psL = [mem.ps(f"psL{u}", [P, 2, E]) for u in range(2)]
        psM = [mem.ps(f"psM{u}", [P, P]) for u in range(2)]
        psG = mem.ps("psG", [P, DC, E])

        gw_here, gw_turned, gw_ready = mem.sem("gw_here"), mem.sem("gw_turned"), mem.sem("gw_ready")
        zero_set, zero_out, desc_set = mem.sem("zero_set"), mem.sem("zero_out"), mem.sem("desc_set")
        x_here, x_kept, row_out = mem.sem2("x_here"), mem.sem2("x_kept"), mem.sem2("row_out")
        stats, moments, shifted, rstd_ok = (mem.sem2(n) for n in ("stats", "moments", "shifted", "rstd_ok"))
        normed, turned, lnT_ok, logits, lg_ok = (mem.sem2(n) for n in ("normed", "turned", "lnT_ok", "logits", "lg_ok"))
        top, cut, nm_ok, chosen_ok, exps, rden_ok, weights = (
            mem.sem2(n) for n in ("top", "cut", "nm_ok", "chosen_ok", "exps", "rden_ok", "weights"))
        maskT, keyed = mem.sem2("maskT"), mem.sem2("keyed")
        found, struck, moved, found2, struck2 = (mem.sem(n) for n in ("found", "struck", "moved", "found2", "struck2"))
        bestT, padded, tokened, tabled = (mem.sem(n) for n in ("bestT", "padded", "tokened", "tabled"))

        xv = x_src.rearrange("(h j p) d -> j p h d", h=2, p=P)
        av = stream_a[0:NTOK, :].rearrange("(h j p) d -> j p h d", h=2, p=P)
        rv = rows[0:NTOK, :].rearrange("(h j p) d -> j p h d", h=2, p=P)

        with nc.Block() as block:
            @block.sync
            def _(sp):
                sp.dma_start(gw_in[:, :], gate_w).then_inc(gw_here, 16)
                sp.wait_ge(idx_set, 1)
                if part == 0:
                    for k in range(2):
                        dst = idx_i[:, k * FT * D:(k + 1) * FT * D].rearrange("p (f d) -> p f d", d=D)
                        sp.dma_start(dst[:, 0:FT - 1, :], lut_idx[k][0:(FT - 1) * P, :].rearrange("(f p) d -> p f d", p=P)).then_inc(idx_here, 16)
                        sp.dma_start(dst[0:FLAST, FT - 1, :], lut_idx[k][(FT - 1) * P:INTER, :]).then_inc(idx_here, 16)
                    sp.dma_start(lut_row[:, :], lut.partition_broadcast(P)).then_inc(idx_here, 16)
                else:
                    sp.dma_start(idx_i[:, :].rearrange("p (c o) -> p c o", c=DC),
                                 lut_idx[2].rearrange("(c p) o -> p c o", p=P)).then_inc(idx_here, 16)
                with sp.Fori(0, HALF // 2) as i:
                    for u in range(2):
                        sp.wait_ge(normed[u], 2 * i)
                        hold(sp)
                        sp.wait_ge(x_kept[u], 16 * i)
                        hold(sp)
                        sp.dma_start(xt[:, u, :, :], xv[2 * i + u]).then_inc(x_here[u], 16)
                sp.wait_ge(found, CAP // 8)
                for h in range(2):
                    sp.dma_start(both[:, h, :], cand[h * E:(h + 1) * E, :]).then_inc(moved, 16)

            @block.scalar
            def _(act):
                act.wait_ge(zero_set, 1)
                act.dma_start(stream_b.rearrange("(p r) d -> p (r d)", p=P), zeros[:, :]).then_inc(zero_out, 16)
                act.dma_start(stream_a[NTOK:NTOK + P, :], zeros[:, 0:D]).then_inc(zero_out, 16)
                act.dma_start(rows[NTOK:NTOK + P, :], zeros[:, 0:ROW]).then_inc(zero_out, 16)
                act.wait_ge(gw_turned, DC)
                nc.scalar.activation(gwT[:, :, :], psG[:, :, :], ACT.Copy).then_inc(gw_ready, 1)
                with act.Fori(0, HALF // 2) as i:
                    for u in range(2):
                        act.wait_ge(x_here[u], 16 * i + 16)
                        act.dma_start(av[2 * i + u], xt[:, u, :, :]).then_inc(x_kept[u], 16)
                    for u in range(2):
                        act.wait_ge(turned[u], 4 * i + 4)
                        act.wait_ge(logits[u], 2 * i)
                        nc.scalar.activation(lnT[:, u, :, :], psT[u][:, :, :], ACT.Copy).then_inc(lnT_ok[u], 1)
                    for u in range(2):
                        act.wait_ge(nm_ok[u], i + 1)
                        act.wait_ge(weights[u], 2 * i)
                        for h in range(2):
                            nc.scalar.activation(ex[:, u, h, :], lg[:, u, h, :], ACT.Exp, bias=nm[:, u, h:h + 1],
                                                 accum_out=den[:, u, h:h + 1]).then_inc(exps[u], 1)
                    for u in range(2):
                        act.wait_ge(weights[u], 2 * i + 2)
                        act.dma_start(rv[2 * i + u], row[:, u, :, :]).then_inc(row_out[u], 16)
                for u in range(2):
                    act.wait_ge(x_kept[u], 16 * (HALF // 2))
                    act.wait_ge(row_out[u], 16 * (HALF // 2))
                act.wait_ge(zero_out, 48)

            @block.gpsimd
            def _(pool):
                nc.gpsimd.memset(idx_i[:, :], 0).then_inc(idx_set, 1)
                nc.gpsimd.memset(lut_w[:, l0:l1], 0.0).then_inc(summed, 1)
                nc.gpsimd.memset(zeros[:, :], 0.0).then_inc(zero_set, 1)
                nc.gpsimd.iota(slot_i[:, :], pattern=[[0, 1]], base=0, channel_multiplier=1).then_inc(desc_set, 1)
                for h in range(2):
                    pool.wait_ge(desc_set, 1 + h)
                    nc.gpsimd.iota(desc_i[h * E:(h + 1) * E, :], pattern=[[-1, HALF * P]],
                                   base=NTOK - h * HALF * P, channel_multiplier=0).then_inc(desc_set, 1)
                pool.wait_ge(desc_set, 3)
                hold(pool)
                nc.gpsimd.tensor_copy(desc[:, :], desc_i[:, :]).then_inc(desc_set, 1)
                nc.gpsimd.tensor_copy(slot_n[:, :], slot_i[:, :]).then_inc(desc_set, 1)
                with pool.Fori(0, HALF // 2) as i:
                    for u in range(2):
                        pool.wait_ge(moments[u], 2 * i + 2)
                        hold(pool)
                        nc.gpsimd.tensor_scalar(ve[:, u, :], mv[:, u, :, 1], EPS, None, ALU.add).then_inc(shifted[u], 1)
                        pool.wait_ge(shifted[u], i + 1)
                        pool.wait_ge(normed[u], 2 * i)
                        nc.gpsimd.tensor_tensor(out=rstd[:, u, :], in0=ve[:, u, :], in1=cst["minus_half"][:, 0:2],
                                                op=ALU.pow).then_inc(rstd_ok[u], 1)
                pool.wait_ge(idx_here, 16 * 5 if part == 0 else 16)
                for code in range(NLUT):
                    pool.wait_ge(summed, code + 1)
                    hold(pool)
                    nc.gpsimd.tensor_scalar(picked[:, :], idx_i[:, :], float(code), lut_row[:, code:code + 1],
                                            ALU.is_equal, ALU.mult).then_inc(picked_ok, 1)
                    pool.wait_ge(picked_ok, code + 1)
                    nc.gpsimd.tensor_tensor(out=lut_w[:, l0:l1], in0=lut_w[:, l0:l1], in1=picked[:, :], op=ALU.add).then_inc(summed, 1)

            @block.vector
            def _(dve):
                dve.wait_ge(desc_set, 5)
                with dve.Fori(0, HALF // 2) as i:
                    for u in range(2):
                        dve.wait_ge(x_here[u], 16 * i + 16)
                        for h in range(2):
                            nc.vector.bn_stats(bs[:, u, h, :], xt[:, u, h, :]).then_inc(stats[u], 1)
                    for u in range(2):
                        dve.wait_ge(stats[u], 2 * i + 2)
                        dve.wait_ge(rstd_ok[u], i)
                        hold(dve)
                        for h in range(2):
                            nc.vector.bn_aggr(mv[:, u, h, :], bs[:, u, h, :]).then_inc(moments[u], 1)
                    for u in range(2):
                        dve.wait_ge(rstd_ok[u], i + 1)
                        dve.wait_ge(row_out[u], 16 * i)
                        for h in range(2):
                            nc.vector.tensor_scalar(row[:, u, h, 0:D], xt[:, u, h, :], mv[:, u, h, 0:1],
                                                    rstd[:, u, h:h + 1], ALU.subtract, ALU.mult).then_inc(normed[u], 1)
                    for u in range(2):
                        dve.wait_ge(logits[u], 2 * i + 2)
                        dve.wait_ge(exps[u], 2 * i)
                        nc.vector.tensor_copy(lg[:, u, :, :], psL[u][:, :, :]).then_inc(lg_ok[u], 1)
                    for u in range(2):
                        dve.wait_ge(lg_ok[u], i + 1)
                        hold(dve)
                        for h in range(2):
                            nc.vector.max(out=mx[:, u, h, :], in_=lg[:, u, h, :]).then_inc(top[u], 1)
                    for u in range(2):
                        dve.wait_ge(top[u], 2 * i + 2)
                        nc.vector.tensor_scalar(nm[:, u, :], mx[:, u, :, 0], -1.0, None, ALU.mult).then_inc(nm_ok[u], 1)
                        for h in range(2):
                            nc.vector.match_replace(out=left[:, u, h, :], in_to_replace=mx[:, u, h, :],
                                                    in_values=lg[:, u, h, :], imm_value=-3.0e38).then_inc(cut[u], 1)
                    for u in range(2):
                        dve.wait_ge(cut[u], 2 * i + 2)
                        dve.wait_ge(maskT[u], i)
                        nc.vector.tensor_tensor(out=chosen[:, u, :, :], in0=left[:, u, :, :], in1=lg[:, u, :, :],
                                                op=ALU.not_equal).then_inc(chosen_ok[u], 1)
                    for u in range(2):
                        dve.wait_ge(exps[u], 2 * i + 2)
                        nc.vector.reciprocal(rden[:, u, :], den[:, u, :]).then_inc(rden_ok[u], 1)
                        dve.wait_ge(rden_ok[u], i + 1)
                        for h in range(2):
                            nc.vector.tensor_scalar(row[:, u, h, D:ROW], ex[:, u, h, :], rden[:, u, h:h + 1], 0.5,
                                                    ALU.mult, ALU.mult).then_inc(weights[u], 1)
                    for u in range(2):
                        dve.wait_ge(maskT[u], i + 1)
                        at = bass.ds((2 * i + u) * P, P)
                        nc.vector.tensor_tensor(out=key[:, at], in0=psM[u][:, :], in1=desc[:, at],
                                                op=ALU.mult).then_inc(keyed[u], 1)
                for u in range(2):
                    dve.wait_ge(keyed[u], HALF // 2)
                for r in range(CAP // 8):
                    dve.wait_ge(struck, r)
                    nc.vector.max(out=cand[:, 8 * r:8 * r + 8], in_=key[:, :]).then_inc(found, 1)
                    dve.wait_ge(found, r + 1)
                    nc.vector.match_replace(out=key[:, :], in_to_replace=cand[:, 8 * r:8 * r + 8],
                                            in_values=key[:, :], imm_value=0.0).then_inc(struck, 1)
                dve.wait_ge(moved, 32)
                for r in range(CAP // 8):
                    dve.wait_ge(struck2, r)
                    nc.vector.max(out=best[:, 8 * r:8 * r + 8], in_=both[:, :, :].rearrange("e h c -> e (h c)")).then_inc(found2, 1)
                    dve.wait_ge(found2, r + 1)
                    nc.vector.match_replace(out=both[:, :, :].rearrange("e h c -> e (h c)"),
                                            in_to_replace=best[:, 8 * r:8 * r + 8],
                                            in_values=both[:, :, :].rearrange("e h c -> e (h c)"), imm_value=0.0).then_inc(struck2, 1)
                dve.wait_ge(bestT, 1)
                nc.vector.tensor_scalar(pad[:, :], psG[:, 0, :], 0.0, slot_n[:, 0:1], ALU.is_equal, ALU.mult).then_inc(padded, 1)
                dve.wait_ge(padded, 1)
                nc.vector.tensor_tensor(out=tok[:, :], in0=pad[:, :], in1=psG[:, 0, :], op=ALU.subtract).then_inc(tokened, 1)
                dve.wait_ge(tokened, 1)
                nc.vector.tensor_scalar(slot_tok[:, :], tok[:, :], float(NTOK), None, ALU.add).then_inc(tabled, 1)
                dve.wait_ge(tabled, 1)

            @block.tensor
            def _(pe):
                pe.wait_ge(gw_here, 16)
                for c in range(DC):
                    nc.tensor.transpose(psG[:, c, :], gw_in[:, c * P:(c + 1) * P], cst["ident"][0:E, 0:E]).then_inc(gw_turned, 1)
                pe.wait_ge(gw_ready, 1)
                with pe.Fori(0, HALF // 2) as i:
                    for u in range(2):
                        pe.wait_ge(normed[u], 2 * i + 2)
                        pe.wait_ge(lnT_ok[u], i)
                        for h in range(2):
                            for c in range(DC):
                                nc.tensor.transpose(psT[u][:, c, h * P:(h + 1) * P], row[:, u, h, c * P:(c + 1) * P],
                                                    cst["ident"][:, :]).then_inc(turned[u], 1)
                    for u in range(2):
                        pe.wait_ge(lnT_ok[u], i + 1)
                        pe.wait_ge(lg_ok[u], i)
                        for h in range(2):
                            for c in range(DC):
                                mm = nc.tensor.matmul(psL[u][:, h, :], lnT[:, u, c, h * P:(h + 1) * P], gwT[:, c, :],
                                                      start=(c == 0), stop=(c == DC - 1))
                            mm.then_inc(logits[u], 1)
                    for u in range(2):
                        pe.wait_ge(chosen_ok[u], i + 1)
                        pe.wait_ge(keyed[u], i)
                        nc.tensor.transpose(psM[u][:, :], chosen[:, u, :, :].rearrange("p h e -> p (h e)"),
                                            cst["ident"][:, :]).then_inc(maskT[u], 1)
                pe.wait_ge(found2, CAP // 8)
                nc.tensor.transpose(psG[:, 0, :], best[:, :], cst["ident"][0:E, 0:E]).then_inc(bestT, 1)
        clear_semaphores(nc, mem)


def moe_experts(nc, cst, tag, rows, w_gate, w_up, w_down, slot_tok, stream_a, stream_b, pool_dma, run):
    U = 4
    with ExitStack() as ctx:
        mem = Mem(nc, ctx, tag)
        wg = mem.sb("wg", [P, U, DC, F])
        wu = mem.sb("wu", [P, U, DC, F])
        wd = mem.sb("wd", [P, U, D])
        idx = mem.sb("idx", [P, U], U32)
        xg = mem.sb("xg", [P, U, ROW])
        wcol = mem.sb("wcol", [P, U])
        xgT = mem.sb("xgT", [P, 2, DC, CAP])
        sil = mem.sb("sil", [P, 2, CAP])
        hT = mem.sb("hT", [P, 2, CAP])
        y = mem.sb("y", [P, U, D])
        psX = [mem.ps(f"psX{u}", [P, DC, CAP]) for u in range(2)]
        psH = [mem.ps(f"psH{u}", [P, 2, CAP]) for u in range(2)]
        psY = [mem.ps(f"psY{u}", [P, D]) for u in range(2)]
        w_here = [mem.sem(f"w_here{k}") for k in range(U)]
        got, added = pool_dma
        got0, added0 = 16 * run * (E // U), 16 * run * (E // 2)
        idx_ok, wcol_ok = mem.sem("idx_ok"), mem.sem("wcol_ok")
        down = [mem.sem(f"down{k}") for k in range(U)]
        turned, xgT_ok, hid, silued, gated, y_ok = (
            mem.sem2(n) for n in ("turned", "xgT_ok", "hid", "silued", "gated", "y_ok"))
        streams = [stream_a, stream_b]
        wgv = w_gate.rearrange("e (c p) f -> e p c f", p=P)
        wuv = w_up.rearrange("e (c p) f -> e p c f", p=P)

        with nc.Block() as block:
            @block.sync
            def _(sp):
                with sp.Fori(0, E // U) as i:
                    for k in range(U):
                        sp.wait_ge(down[k], i)
                        hold(sp)
                        e = U * i + k
                        sp.dma_start(wg[:, k, :, :], wgv[e]).then_inc(w_here[k], 16)
                        sp.dma_start(wu[:, k, :, :], wuv[e]).then_inc(w_here[k], 16)
                        sp.dma_start(wd[:, k, :], w_down[e]).then_inc(w_here[k], 16)

            @block.gpsimd
            def _(pool):
                def fetch(i, k):
                    e = U * i + k
                    nc.gpsimd.tensor_copy(idx[:, k:k + 1], slot_tok[:, bass.ds(e, 1)]).then_inc(idx_ok, 1)
                    pool.wait_ge(idx_ok, e + 1)
                    hold(pool)
                    pool.indirect_dma_start(out=xg[:, k, :], out_offset=None, in_=rows,
                                            in_offset=bass.IndirectOffsetOnAxis(ap=idx[:, k:k + 1], axis=0)).then_inc(got[k], 16)

                def scatter(i, k):
                    u = k % 2
                    pool.wait_ge(y_ok[u], 2 * i + k // 2 + 1)
                    pool.wait_ge(added[u], added0 + 16 * (2 * i + k // 2))
                    hold(pool)
                    pool.indirect_dma_start(out=streams[u], out_offset=bass.IndirectOffsetOnAxis(ap=idx[:, k:k + 1], axis=0),
                                            in_=y[:, k, :], in_offset=None, compute_op=ALU.add).then_inc(added[u], 16)

                def weight(i, k):
                    pool.wait_ge(got[k], got0 + 16 * i + 16)
                    hold(pool)
                    nc.gpsimd.tensor_copy(wcol[:, k:k + 1], xg[:, k, bass.ds(D + U * i + k, 1)]).then_inc(wcol_ok, 1)

                for k in range(2):
                    fetch(0, k)
                with pool.Fori(0, E // U - 1) as i:
                    for k in range(U):
                        weight(i, k)
                        n, kk = (i, k + 2) if k < 2 else (i + 1, k - 2)
                        u = kk % 2
                        pool.wait_ge(added[u], added0 + (16 * (2 * (n - 1) + kk // 2 + 1) if k >= 2 else 16 * (2 * n)))
                        fetch(n, kk)
                        scatter(i, k)
                i = E // U - 1
                for k in range(U):
                    weight(i, k)
                    if k < 2:
                        pool.wait_ge(added[k % 2], added0 + 16 * (2 * i))
                        fetch(i, k + 2)
                    scatter(i, k)
                for u in range(2):
                    pool.wait_ge(added[u], added0 + 16 * (E // 2))

            @block.tensor
            def _(pe):
                with pe.Fori(0, E // U) as i:
                    for k in range(U):
                        u, n = k % 2, 2 * i + k // 2
                        pe.wait_ge(got[k], got0 + 16 * i + 16)
                        pe.wait_ge(xgT_ok[u], n)
                        for c in range(DC):
                            nc.tensor.transpose(psX[u][:, c, :], xg[:, k, c * P:(c + 1) * P], cst["ident"][:, :]).then_inc(turned[u], 1)
                        pe.wait_ge(w_here[k], 48 * i + 48)
                        pe.wait_ge(xgT_ok[u], n + 1)
                        pe.wait_ge(gated[u], n)
                        for g, w in enumerate((wg, wu)):
                            for c in range(DC):
                                mm = nc.tensor.matmul(psH[u][:, g, :], w[:, k, c, :], xgT[:, u, c, :],
                                                      start=(c == 0), stop=(c == DC - 1))
                            mm.then_inc(hid[u], 1)
                        pe.wait_ge(gated[u], n + 1)
                        pe.wait_ge(y_ok[u], n)
                        nc.tensor.matmul(psY[u][:, :], hT[:, u, :], wd[:, k, :], start=True, stop=True).then_inc(down[k], 1)

            @block.scalar
            def _(act):
                with act.Fori(0, E // U) as i:
                    for k in range(U):
                        u, n = k % 2, 2 * i + k // 2
                        act.wait_ge(turned[u], 2 * n + 2)
                        act.wait_ge(hid[u], 2 * n)
                        nc.scalar.activation(xgT[:, u, :, :], psX[u][:, :, :], ACT.Copy).then_inc(xgT_ok[u], 1)
                        act.wait_ge(hid[u], 2 * n + 2)
                        act.wait_ge(gated[u], n)
                        nc.scalar.activation(sil[:, u, :], psH[u][:, 0, :], ACT.Silu).then_inc(silued[u], 1)

            @block.vector
            def _(dve):
                with dve.Fori(0, E // U) as i:
                    for k in range(U):
                        u, n = k % 2, 2 * i + k // 2
                        dve.wait_ge(silued[u], n + 1)
                        dve.wait_ge(down[k - 2] if k >= 2 else down[k + 2], i + 1 if k >= 2 else i)
                        nc.vector.tensor_tensor(out=hT[:, u, :], in0=psH[u][:, 1, :], in1=sil[:, u, :],
                                                op=ALU.mult).then_inc(gated[u], 1)
                        dve.wait_ge(down[k], i + 1)
                        dve.wait_ge(wcol_ok, U * i + k + 1)
                        nc.vector.tensor_scalar(y[:, k, :], psY[u][:, :], wcol[:, k:k + 1], None, ALU.mult).then_inc(y_ok[u], 1)
        clear_semaphores(nc, mem)


def load_attention_weights(nc, mem, Wq, Wk, Ws, Wv, Wg, Wo, g_norm):
    w = {
        "q": mem.sb("wq", [P, DC, H * DK]), "k": mem.sb("wk", [P, DC, H * DK]), "s": mem.sb("ws", [P, DC, H * M]),
        "v": mem.sb("wv", [P, DC, H * DV]), "g": mem.sb("wg_att", [P, DC, H * DV]),
        "o": mem.sb("wo_att", [DV, H, D]), "norm": mem.sb("g_norm", [P, DV]),
        "here": mem.sem("attention_weights"),
    }
    with nc.Block() as block:
        @block.sync
        def _(sp):
            for name, src in (("q", Wq), ("k", Wk), ("s", Ws), ("v", Wv), ("g", Wg)):
                sp.dma_start(w[name][:, :, :], src.rearrange("(c p) n -> p c n", p=P)).then_inc(w["here"], 16)
            sp.dma_start(w["o"][:, :, :], Wo.rearrange("(h v) d -> v h d", v=DV)).then_inc(w["here"], 16)
            sp.dma_start(w["norm"][:, :], g_norm.partition_broadcast(P)).then_inc(w["here"], 16)
    return w


def attention(nc, cst, w, tag, stream_a, stream_b, x_out):
    HQ = 4
    QPB = H // HQ
    TT = T // P
    NH = HQ // 2
    with ExitStack() as ctx:
        mem = Mem(nc, ctx, tag)
        xab = mem.sb("xab", [P, 2, TT, D])
        xs = mem.sb("xs", [P, TT, D])
        xacc = mem.sb("xacc", [P, TT, D])
        bs = mem.sb("bs", [P, TT, 6])
        mv = mem.sb("mv", [P, TT, 2])
        ve = mem.sb("ve", [P, TT])
        rstd = mem.sb("rstd", [P, TT])
        ln = mem.sb("ln", [P, TT, D])
        lnT = mem.sb("lnT", [P, DC, T])
        norm_half = mem.sb("norm_half", [P, DV])
        qT = mem.sb("qT", [P, NH, T])
        kT = mem.sb("kT", [P, NH, T])
        sc = mem.sb("sc", [P, TT, HQ * M])
        em = mem.sb("em", [P, TT, HQ * M])
        emT = mem.sb("emT", [P, NH, T])
        v = mem.sb("v", [P, 2, TT, HQ * DV])
        gs = mem.sb("gs", [P, 2, TT, HQ * DV])
        th = mem.sb("th", [P, TT, HQ * DV])
        tg = mem.sb("tg", [P, TT, HQ * DV])
        rz = mem.sb("rz", [P, TT, HQ * M])
        at = mem.sb("at", [P, HQ, 3 * P])
        bt = mem.sb("bt", [P, HQ, 3 * P])
        okn = mem.sb("okn", [P, TT * HQ, M])
        mxs = mem.sb("mxs", [P, TT * HQ])
        sub = mem.sb("sub", [P, TT * HQ, M])
        pe_ = mem.sb("pexp", [P, TT * HQ, M])
        sm = mem.sb("sm", [P, TT * HQ])
        rsm = mem.sb("rsm", [P, TT * HQ])
        er = mem.sb("er", [P, TT * HQ, M])
        pz = mem.sb("pz", [P, TT, HQ * M])
        pzT = mem.sb("pzT", [P, NH, T])
        sq = mem.sb("sq", [P, TT * HQ, DV])
        ss = mem.sb("ss", [P, TT * HQ])
        ms = mem.sb("ms", [P, TT * HQ])
        orstd = mem.sb("orstd", [P, TT * HQ])
        o1 = mem.sb("o1", [P, TT * HQ, DV])
        o2 = mem.sb("o2", [P, TT, HQ * DV])
        oT = mem.sb("oT", [P, HQ, T])
        psA = [mem.ps(f"psA{k}", [P, 512]) for k in range(2)]
        psB = [mem.ps(f"psB{k}", [P, 512]) for k in range(2)]
        psC = [mem.ps(f"psC{k}", [P, 512]) for k in range(2)]
        psD = mem.ps("psD", [P, 2, 512])

        names = ("x_here x_out_done xs_ok xacc_ok stats moments shifted rstd_ok ln_ok ln_ps lnT_ok norm_ok "
                 "v_ps v_ok q_ps q_ok k_ps k_ok g_ps th_ok tg_ok gs_ok s_ps sc_ok em_ok z_ps rz_ok et_ps et_ok "
                 "at_ps at_ok ok_ps okn_ok mx_ok sub_ok pe_ok sm_ok rsm_ok er_ok pz_ok pzt_ps pzt_ok bt_ps bt_ok "
                 "ov_ps sq_ok ss_ok ms_ok orstd_ok o1_ok o2_ok ot_ps ot_ok out_ps acc_ok")
        (x_here, x_out_done, xs_ok, xacc_ok, stats, moments, shifted, rstd_ok, ln_ok, ln_ps, lnT_ok, norm_ok,
         v_ps, v_ok, q_ps, q_ok, k_ps, k_ok, g_ps, th_ok, tg_ok, gs_ok, s_ps, sc_ok, em_ok, z_ps, rz_ok, et_ps, et_ok,
         at_ps, at_ok, ok_ps, okn_ok, mx_ok, sub_ok, pe_ok, sm_ok, rsm_ok, er_ok, pz_ok, pzt_ps, pzt_ok, bt_ps, bt_ok,
         ov_ps, sq_ok, ss_ok, ms_ok, orstd_ok, o1_ok, o2_ok, ot_ps, ot_ok, out_ps, acc_ok) = (
            mem.sem(n) for n in names.split())
        av = stream_a[0:NTOK, :].rearrange("(b t p) d -> b p t d", t=TT, p=P)
        bv = stream_b[0:NTOK, :].rearrange("(b t p) d -> b p t d", t=TT, p=P)
        ov = x_out.rearrange("(b t p) d -> b p t d", t=TT, p=P)

        def over_slots(stat):
            return stat[:, :].unsqueeze(2).to_broadcast([P, TT * HQ, M])

        with nc.Block() as block:
            @block.sync
            def _(sp):
                def load(b):
                    sp.dma_start(xab[:, 0, :, :], av[b]).then_inc(x_here, 16)
                    sp.dma_start(xab[:, 1, :, :], bv[b]).then_inc(x_here, 16)

                def store(b):
                    sp.wait_ge(acc_ok, QPB * b + QPB + 1)
                    hold(sp)
                    sp.dma_start(ov[b], xacc[:, :, :]).then_inc(x_out_done, 16)

                load(0)
                with sp.Fori(0, B - 1) as b:
                    sp.wait_ge(xs_ok, b + 1)
                    hold(sp)
                    load(b + 1)
                    store(b)
                store(B - 1)
                sp.wait_ge(x_out_done, 16 * B)

            @block.gpsimd
            def _(pool):
                def add_stream(b):
                    pool.wait_ge(x_here, 32 * b + 32)
                    pool.wait_ge(xacc_ok, b)
                    nc.gpsimd.tensor_tensor(out=xs[:, :, :], in0=xab[:, 0, :, :], in1=xab[:, 1, :, :], op=ALU.add).then_inc(xs_ok, 1)

                def rstd_of_stream(b):
                    pool.wait_ge(moments, TT * b + TT)
                    hold(pool)
                    nc.gpsimd.tensor_scalar(ve[:, :], mv[:, :, 1], EPS, None, ALU.add).then_inc(shifted, 1)
                    pool.wait_ge(shifted, b + 1)
                    nc.gpsimd.tensor_tensor(out=rstd[:, :], in0=ve[:, :], in1=cst["minus_half"][:, 0:TT], op=ALU.pow).then_inc(rstd_ok, 1)

                def gate(m, par):
                    for t in range(TT):
                        pool.wait_ge(tg_ok, TT * m + t + 1)
                        nc.gpsimd.tensor_tensor(out=gs[:, par, t, :].rearrange("p (h v) -> p h v", v=DV),
                                                in0=tg[:, t, :].rearrange("p (h v) -> p h v", v=DV),
                                                in1=norm_half[:, :].unsqueeze(1).to_broadcast([P, HQ, DV]),
                                                op=ALU.mult).then_inc(gs_ok, 1)

                def slot(b, q, last):
                    n = QPB * b + q
                    ahead = not (last and q == QPB - 1)
                    if q == 0:
                        pool.wait_ge(x_out_done, 16 * b)
                        pool.wait_ge(xs_ok, b + 1)
                        hold(pool)
                        nc.gpsimd.tensor_copy(xacc[:, :, :], xs[:, :, :]).then_inc(xacc_ok, 1)
                    if q == 1 and not last:
                        add_stream(b + 1)
                    if q == 2 and not last:
                        rstd_of_stream(b + 1)
                    pool.wait_ge(mx_ok, n + 1)
                    nc.gpsimd.tensor_tensor(out=sub[:, :, :], in0=okn[:, :, :], in1=over_slots(mxs), op=ALU.subtract).then_inc(sub_ok, 1)
                    pool.wait_ge(pe_ok, n + 1)
                    nc.gpsimd.tensor_tensor(out=er[:, :, :], in0=pe_[:, :, :],
                                            in1=rz[:, :, :].rearrange("p t (h m) -> p (t h) m", m=M), op=ALU.mult).then_inc(er_ok, 1)
                    pool.wait_ge(er_ok, n + 1)
                    pool.wait_ge(rsm_ok, n + 1)
                    nc.gpsimd.tensor_tensor(out=pz[:, :, :].rearrange("p t (h m) -> p (t h) m", m=M), in0=er[:, :, :],
                                            in1=over_slots(rsm), op=ALU.mult).then_inc(pz_ok, 1)
                    pool.wait_ge(ss_ok, n + 1)
                    hold(pool)
                    nc.gpsimd.tensor_scalar(ms[:, :], ss[:, :], 1.0 / DV, EPS, ALU.mult, ALU.add).then_inc(ms_ok, 1)
                    pool.wait_ge(ms_ok, n + 1)
                    nc.gpsimd.tensor_tensor(out=orstd[:, :], in0=ms[:, :], in1=cst["minus_half"][:, 0:TT * HQ], op=ALU.pow).then_inc(orstd_ok, 1)
                    pool.wait_ge(orstd_ok, n + 1)
                    pool.wait_ge(o1_ok, n + 1)
                    nc.gpsimd.tensor_tensor(out=o2[:, :, :].rearrange("p t (h v) -> p (t h) v", v=DV), in0=o1[:, :, :],
                                            in1=orstd[:, :].unsqueeze(2).to_broadcast([P, TT * HQ, DV]), op=ALU.mult).then_inc(o2_ok, 1)
                    if ahead:
                        gate(n + 1, (q + 1) % 2)

                pool.wait_ge(w["here"], 16 * 7)
                hold(pool)
                nc.gpsimd.tensor_scalar(norm_half[:, :], w["norm"][:, :], 0.5, None, ALU.mult).then_inc(norm_ok, 1)
                pool.wait_ge(norm_ok, 1)
                add_stream(0)
                rstd_of_stream(0)
                gate(0, 0)
                with pool.Fori(0, B - 1) as b:
                    for q in range(QPB):
                        slot(b, q, False)
                for q in range(QPB):
                    slot(B - 1, q, True)

            @block.scalar
            def _(act):
                def copy(out, in_, done, scale=1.0):
                    nc.scalar.activation(out, in_, ACT.Copy, scale=scale).then_inc(done, 1)

                def turn_stream(b):
                    act.wait_ge(ln_ps, b + 1)
                    copy(lnT[:, :, :].rearrange("p c t -> p (c t)"), psA[1], lnT_ok)

                def value(m, par, t):
                    act.wait_ge(v_ps, TT * m + t + 1)
                    copy(v[:, par, t, :], psA[t], v_ok)

                def query(m):
                    act.wait_ge(q_ps, m + 1)
                    copy(qT[:, :, :].rearrange("p a t -> p (a t)"), psA[0], q_ok, scale=DK ** -0.5)

                def gate_tanh(m):
                    for t in range(TT):
                        act.wait_ge(g_ps, TT * m + t + 1)
                        nc.scalar.activation(th[:, t, :], psA[t], ACT.Tanh, scale=0.5).then_inc(th_ok, 1)

                def exp_s(m):
                    act.wait_ge(sc_ok, m + 1)
                    nc.scalar.activation(em[:, :, :], sc[:, :, :], ACT.Exp).then_inc(em_ok, 1)

                def slot(b, q, last):
                    n = QPB * b + q
                    ahead = not (last and q == QPB - 1)
                    if q == QPB - 1 and not last:
                        turn_stream(b + 1)
                    act.wait_ge(et_ps, n + 1)
                    copy(emT[:, :, :].rearrange("p a t -> p (a t)"), psC[1], et_ok)
                    if ahead:
                        value(n + 1, (q + 1) % 2, 0)
                    act.wait_ge(sub_ok, n + 1)
                    nc.scalar.activation(pe_[:, :, :], sub[:, :, :], ACT.Exp).then_inc(pe_ok, 1)
                    if ahead:
                        value(n + 1, (q + 1) % 2, 1)
                        query(n + 1)
                    act.wait_ge(pzt_ps, n + 1)
                    copy(pzT[:, :, :].rearrange("p a t -> p (a t)"), psC[1], pzt_ok)
                    act.wait_ge(ov_ps, n + 1)
                    nc.scalar.activation(sq[:, :, :].rearrange("p (t h) v -> p t (h v)", t=TT), psD, ACT.Square).then_inc(sq_ok, 1)
                    if ahead:
                        gate_tanh(n + 1)
                        exp_s(n + 1)
                    for a in range(NH):
                        act.wait_ge(ot_ps, NH * n + a + 1)
                        copy(oT[:, 2 * a:2 * a + 2, :].rearrange("p a t -> p (a t)"), psD[:, a, :], ot_ok)

                turn_stream(0)
                value(0, 0, 0)
                value(0, 0, 1)
                query(0)
                gate_tanh(0)
                exp_s(0)
                with act.Fori(0, B - 1) as b:
                    for q in range(QPB):
                        slot(b, q, False)
                for q in range(QPB):
                    slot(B - 1, q, True)

            @block.vector
            def _(dve):
                def moments_of_stream(b):
                    dve.wait_ge(xs_ok, b + 1)
                    for t in range(TT):
                        nc.vector.bn_stats(bs[:, t, :], xs[:, t, :]).then_inc(stats, 1)
                    dve.wait_ge(stats, TT * b + TT)
                    hold(dve)
                    for t in range(TT):
                        nc.vector.bn_aggr(mv[:, t, :], bs[:, t, :]).then_inc(moments, 1)

                def normalise_stream(b):
                    dve.wait_ge(rstd_ok, b + 1)
                    for t in range(TT):
                        nc.vector.tensor_scalar(ln[:, t, :], xs[:, t, :], mv[:, t, 0:1], rstd[:, t:t + 1],
                                                ALU.subtract, ALU.mult).then_inc(ln_ok, 1)

                def key(m):
                    dve.wait_ge(k_ps, m + 1)
                    nc.vector.tensor_copy(kT[:, :, :].rearrange("p a t -> p (a t)"), psA[1]).then_inc(k_ok, 1)

                def gate(m):
                    for t in range(TT):
                        dve.wait_ge(th_ok, TT * m + t + 1)
                        nc.vector.scalar_tensor_tensor(out=tg[:, t, :], in0=th[:, t, :], scalar=1.0, in1=psA[t],
                                                       op0=ALU.add, op1=ALU.mult).then_inc(tg_ok, 1)

                def clip(m):
                    dve.wait_ge(s_ps, m + 1)
                    nc.vector.tensor_scalar(sc[:, :, :].rearrange("p t m -> p (t m)"), psA[0], -32.0, 32.0,
                                            ALU.max, ALU.min).then_inc(sc_ok, 1)

                def invert_z(m):
                    dve.wait_ge(z_ps, m + 1)
                    nc.vector.reciprocal(rz[:, :, :].rearrange("p t m -> p (t m)"), psC[0]).then_inc(rz_ok, 1)

                def masked(dst, n, ps_ready, done):
                    for h in range(HQ):
                        dve.wait_ge(ps_ready, HQ * n + h + 1)
                        nc.vector.tensor_tensor(out=dst[:, h, :], in0=psB[h % 2][:, 0:3 * P],
                                                in1=cst["causal"][:, :, :].rearrange("p a i -> p (a i)"), op=ALU.mult).then_inc(done, 1)

                def slot(b, q, last):
                    n = QPB * b + q
                    ahead = not (last and q == QPB - 1)
                    masked(at, n, at_ps, at_ok)
                    dve.wait_ge(ok_ps, n + 1)
                    dve.wait_ge(rz_ok, n + 1)
                    nc.vector.tensor_tensor(out=okn[:, :, :].rearrange("p a m -> p (a m)"), in0=psC[0],
                                            in1=rz[:, :, :].rearrange("p t m -> p (t m)"), op=ALU.mult).then_inc(okn_ok, 1)
                    dve.wait_ge(okn_ok, n + 1)
                    nc.vector.reduce_max(mxs[:, :], okn[:, :, :], axis=AX.X).then_inc(mx_ok, 1)
                    dve.wait_ge(pe_ok, n + 1)
                    nc.vector.reduce_sum(sm[:, :], pe_[:, :, :], axis=AX.X).then_inc(sm_ok, 1)
                    dve.wait_ge(sm_ok, n + 1)
                    nc.vector.reciprocal(rsm[:, :], sm[:, :]).then_inc(rsm_ok, 1)
                    if ahead:
                        key(n + 1)
                    masked(bt, n, bt_ps, bt_ok)
                    dve.wait_ge(sq_ok, n + 1)
                    dve.wait_ge(gs_ok, TT * n + TT)
                    nc.vector.tensor_tensor(out=o1[:, :, :].rearrange("p (t h) v -> p t (h v)", t=TT), in0=psD,
                                            in1=gs[:, q % 2, :, :], op=ALU.mult).then_inc(o1_ok, 1)
                    nc.vector.reduce_sum(ss[:, :], sq[:, :, :], axis=AX.X).then_inc(ss_ok, 1)
                    if ahead:
                        gate(n + 1)
                        clip(n + 1)
                        invert_z(n + 1)
                    if q == 1 and not last:
                        moments_of_stream(b + 1)
                    if q == 2 and not last:
                        normalise_stream(b + 1)
                    dve.wait_ge(out_ps, n + 1)
                    dve.wait_ge(xacc_ok, b + 1)
                    dve.wait_ge(acc_ok, n + 1)
                    nc.vector.tensor_tensor(out=xacc[:, :, :].rearrange("p t d -> p (t d)"), in0=psA[1],
                                            in1=xacc[:, :, :].rearrange("p t d -> p (t d)"), op=ALU.add).then_inc(acc_ok, 1)

                nc.vector.memset(mxs[:, :], 0.0).then_inc(acc_ok, 1)
                moments_of_stream(0)
                normalise_stream(0)
                key(0)
                gate(0)
                clip(0)
                invert_z(0)
                with dve.Fori(0, B - 1) as b:
                    for q in range(QPB):
                        slot(b, q, False)
                for q in range(QPB):
                    slot(B - 1, q, True)

            @block.tensor
            def _(pe):
                ident = cst["ident"][:, :]
                tri, ones = cst["causal"][:, 0, :], cst["causal"][:, 1, :]

                def turn_stream(b, n):
                    pe.wait_ge(ln_ok, TT * b + TT)
                    pe.wait_ge(tg_ok, TT * n)
                    pe.wait_ge(acc_ok, n)
                    for t in range(TT):
                        for c in range(DC):
                            mm = nc.tensor.transpose(psA[1][:, c * T + t * P:c * T + (t + 1) * P], ln[:, t, c * P:(c + 1) * P], ident)
                    mm.then_inc(ln_ps, 1)

                def wide(name, t, m, q, ready):
                    for c in range(DC):
                        mm = nc.tensor.matmul(psA[t], lnT[:, c, t * P:(t + 1) * P], w[name][:, c, q * HQ * DV:(q + 1) * HQ * DV],
                                              start=(c == 0), stop=(c == DC - 1))
                    mm.then_inc(ready, 1)

                def narrow(name, dst, q, ready):
                    for a in range(NH):
                        col = (q * NH + a) * 2 * DK
                        for c in range(DC):
                            mm = nc.tensor.matmul(dst[:, a * T:(a + 1) * T], w[name][:, c, col:col + 2 * DK], lnT[:, c, :],
                                                  start=(c == 0), stop=(c == DC - 1))
                    mm.then_inc(ready, 1)

                def value_query(b, m, q):
                    pe.wait_ge(lnT_ok, b + 1)
                    pe.wait_ge(sc_ok, m)
                    wide("v", 0, m, q, v_ps)
                    pe.wait_ge(tg_ok, TT * m)
                    pe.wait_ge(acc_ok, m)
                    wide("v", 1, m, q, v_ps)
                    pe.wait_ge(v_ok, TT * m + 1)
                    narrow("q", psA[0], q, q_ps)

                def key(m, q):
                    pe.wait_ge(v_ok, TT * m + 2)
                    narrow("k", psA[1], q, k_ps)

                def gate_slots(m, q):
                    pe.wait_ge(q_ok, m + 1)
                    wide("g", 0, m, q, g_ps)
                    pe.wait_ge(k_ok, m + 1)
                    wide("g", 1, m, q, g_ps)
                    pe.wait_ge(tg_ok, TT * m + 1)
                    for t in range(TT):
                        for c in range(DC):
                            mm = nc.tensor.matmul(psA[0][:, t * HQ * M:(t + 1) * HQ * M], lnT[:, c, t * P:(t + 1) * P],
                                                  w["s"][:, c, q * HQ * M:(q + 1) * HQ * M], start=(c == 0), stop=(c == DC - 1))
                    mm.then_inc(s_ps, 1)

                def z_sums(m):
                    pe.wait_ge(em_ok, m + 1)
                    pe.wait_ge(okn_ok, m)
                    nc.tensor.matmul(psC[0][:, 0:HQ * M], tri, em[:, 0, :], start=True, stop=True)
                    nc.tensor.matmul(psC[0][:, HQ * M:2 * HQ * M], ones, em[:, 0, :], start=True, stop=False)
                    nc.tensor.matmul(psC[0][:, HQ * M:2 * HQ * M], tri, em[:, 1, :], start=False, stop=True).then_inc(z_ps, 1)

                def causal_scores(lhs, rhs, n, ready, read):
                    for h in range(HQ):
                        a, r = h // 2, (h % 2) * DK
                        read(h)
                        nc.tensor.matmul(psB[h % 2][:, 0:2 * P], lhs[r:r + DK, a, 0:P], rhs[r:r + DK, a, 0:T], start=True, stop=True)
                        nc.tensor.matmul(psB[h % 2][:, 2 * P:3 * P], lhs[r:r + DK, a, P:T], rhs[r:r + DK, a, P:T],
                                         start=True, stop=True).then_inc(ready, 1)

                def over_j(dst, lhs, rhs, width, h):
                    nc.tensor.matmul(dst(0, h), lhs[:, h, 0:P], rhs(0, h), start=True, stop=True)
                    nc.tensor.matmul(dst(1, h), lhs[:, h, P:2 * P], rhs(0, h), start=True, stop=False)
                    return nc.tensor.matmul(dst(1, h), lhs[:, h, 2 * P:3 * P], rhs(1, h), start=False, stop=True)

                def slot(b, q, last):
                    n = QPB * b + q
                    ahead = not (last and q == QPB - 1)
                    bn, qn = (b, q + 1) if q < QPB - 1 else (b + 1, 0)
                    if q == QPB - 1 and not last:
                        turn_stream(b + 1, n + 1)
                    pe.wait_ge(q_ok, n + 1)
                    pe.wait_ge(k_ok, n + 1)

                    def b_free_a(h):
                        if h < 2:
                            pe.wait_ge(bt_ok, HQ * n)
                        else:
                            pe.wait_ge(at_ok, HQ * n + h - 1)
                    causal_scores(kT, qT, n, at_ps, b_free_a)
                    pe.wait_ge(pzt_ok, n)
                    for t in range(TT):
                        for a in range(NH):
                            mm = nc.tensor.transpose(psC[1][:, a * T + t * P:a * T + (t + 1) * P], em[:, t, a * P:(a + 1) * P], ident)
                    mm.then_inc(et_ps, 1)
                    pe.wait_ge(rz_ok, n + 1)
                    for h in range(HQ):
                        pe.wait_ge(at_ok, HQ * n + h + 1)
                        mm = over_j(lambda t, h: psC[0][:, (t * HQ + h) * M:(t * HQ + h + 1) * M], at,
                                    lambda t, h: em[:, t, h * M:(h + 1) * M], M, h)
                    mm.then_inc(ok_ps, 1)
                    if ahead:
                        value_query(bn, n + 1, qn)
                    pe.wait_ge(pz_ok, n + 1)
                    pe.wait_ge(et_ok, n + 1)
                    for t in range(TT):
                        for a in range(NH):
                            mm = nc.tensor.transpose(psC[1][:, a * T + t * P:a * T + (t + 1) * P], pz[:, t, a * P:(a + 1) * P], ident)
                    mm.then_inc(pzt_ps, 1)
                    if ahead:
                        key(n + 1, qn)
                    pe.wait_ge(pzt_ok, n + 1)

                    def b_free_b(h):
                        pe.wait_ge(at_ok if h < 2 else bt_ok, HQ * n + (4 if h < 2 else h - 1))
                    causal_scores(emT, pzT, n, bt_ps, b_free_b)
                    pe.wait_ge(v_ok, TT * n + TT)
                    pe.wait_ge(ot_ok, NH * n)
                    for h in range(HQ):
                        pe.wait_ge(bt_ok, HQ * n + h + 1)
                        mm = over_j(lambda t, h: psD[:, t, h * DV:(h + 1) * DV], bt,
                                    lambda t, h: v[:, q % 2, t, h * DV:(h + 1) * DV], DV, h)
                    mm.then_inc(ov_ps, 1)
                    if ahead:
                        gate_slots(n + 1, qn)
                    pe.wait_ge(o2_ok, n + 1)
                    for h in range(HQ):
                        for t in range(TT):
                            mm = nc.tensor.transpose(psD[:, h // 2, (h % 2) * T + t * P:(h % 2) * T + (t + 1) * P],
                                                     o2[:, t, h * DV:(h + 1) * DV], ident)
                        if h % 2:
                            mm.then_inc(ot_ps, 1)
                    if ahead:
                        z_sums(n + 1)
                    pe.wait_ge(tg_ok, TT * (n + 2) if ahead else TT * (n + 1))
                    pe.wait_ge(ot_ok, NH * n + NH)
                    for t in range(TT):
                        for h in range(HQ):
                            mm = nc.tensor.matmul(psA[1][:, t * D:(t + 1) * D], oT[:, h, t * P:(t + 1) * P],
                                                  w["o"][:, q * HQ + h, :], start=(h == 0), stop=(h == HQ - 1))
                    mm.then_inc(out_ps, 1)

                pe.wait_ge(w["here"], 16 * 7)
                turn_stream(0, 0)
                value_query(0, 0, 0)
                key(0, 0)
                gate_slots(0, 0)
                z_sums(0)
                with pe.Fori(0, B - 1) as b:
                    for q in range(QPB):
                        slot(b, q, False)
                for q in range(QPB):
                    slot(B - 1, q, True)
        clear_semaphores(nc, mem)


def lut_columns(n):
    return ((0, 2 * FT * D), (2 * FT * D, 2 * FT * D + DC * INTER))[n]


def turn_matrices(nc, tag, cst, groups):
    NB = 4
    with ExitStack() as ctx:
        mem = Mem(nc, ctx, tag)
        ps = [mem.ps(f"ps{k}", [P, 512]) for k in range(NB)]
        turned, copied_a, copied_v = mem.sem("turned"), mem.sem("copied_a"), mem.sem("copied_v")
        with nc.Block() as block:
            @block.tensor
            def _(pe):
                for k, (dst, srcs) in enumerate(groups):
                    if k >= NB:
                        pe.wait_ge(copied_v if k % 2 else copied_a, (k - NB) // 2 + 1)
                    at = 0
                    for src in srcs:
                        rows, cols = src.shape
                        mm = nc.tensor.transpose(ps[k % NB][0:cols, at:at + rows], src, cst["ident"][0:rows, 0:rows])
                        at += rows
                    mm.then_inc(turned, 1)

            @block.scalar
            def _(act):
                for k, (dst, srcs) in enumerate(groups):
                    if k % 2 == 0:
                        act.wait_ge(turned, k + 1)
                        nc.scalar.activation(dst, ps[k % NB][0:dst.shape[0], 0:dst.shape[1]], ACT.Copy).then_inc(copied_a, 1)

            @block.vector
            def _(dve):
                for k, (dst, srcs) in enumerate(groups):
                    if k % 2 == 1:
                        dve.wait_ge(turned, k + 1)
                        nc.vector.tensor_copy(dst, ps[k % NB][0:dst.shape[0], 0:dst.shape[1]]).then_inc(copied_v, 1)
        clear_semaphores(nc, mem)


def ffn_groups(lut_w, wgT, wuT, wdT):
    groups = []
    for k, dst in ((0, wgT), (1, wuT)):
        w = lut_w[:, k * FT * D:(k + 1) * FT * D].rearrange("p (f d) -> p f d", d=D)
        for c in range(DC):
            for f0 in range(0, FT, 4):
                srcs = [w[0:(P if f < FT - 1 else FLAST), f, c * P:(c + 1) * P] for f in range(f0, min(f0 + 4, FT))]
                end = min((f0 + 4) * P, INTER)
                groups.append((dst[:, c, f0 * P:end], srcs))
    w = lut_w[:, 2 * FT * D:2 * FT * D + DC * INTER].rearrange("p (c o) -> p c o", c=DC)
    for f in range(FT):
        n = P if f < FT - 1 else FLAST
        groups.append((wdT[0:n, f, :], [w[:, c, f * P:f * P + n] for c in range(DC)]))
    return groups


def hgrn_groups(raw, turned):
    return [(turned[:, k, c, :], [raw[:, k, r, c * P:(c + 1) * P] for r in range(DC)])
            for k in range(4) for c in range(DC)]


def lut_ffn(nc, cst, tag, sources, x_out, wgT, wuT, wdT):
    G = 4
    NU = NTILE // G
    with ExitStack() as ctx:
        mem = Mem(nc, ctx, tag)
        two = len(sources) == 2
        xt = mem.sb("xt", [P, 2, G, D])
        xb = mem.sb("xb", [P, G, D])
        bs = mem.sb("bs", [P, G, 6])
        mv = mem.sb("mv", [P, G, 2])
        ve = mem.sb("ve", [P, G])
        rstd = mem.sb("rstd", [P, G])
        ln = mem.sb("ln", [P, G, D])
        lnT = mem.sb("lnT", [P, DC, G * P])
        sil = mem.sb("sil", [P, 2, G * P])
        hT = mem.sb("hT", [P, FT, G * P])
        y = mem.sb("y", [P, G, D])
        psT = [mem.ps(f"psT{c}", [P, G * P]) for c in range(DC)]
        psG = [mem.ps(f"psG{k}", [P, G * P]) for k in range(2)]
        psU = [mem.ps(f"psU{k}", [P, G * P]) for k in range(2)]
        psY = [mem.ps(f"psY{k}", [P, 2 * D]) for k in range(2)]
        names = "x_here added stats moments shifted rstd_ok ln_ok ln_ps lnT_ok gate_ps up_ps sil_ok h_ok down_ps y_ok y_out"
        (x_here, added, stats, moments, shifted, rstd_ok, ln_ok, ln_ps, lnT_ok, gate_ps, up_ps, sil_ok, h_ok, down_ps,
         y_ok, y_out) = (mem.sem(n) for n in names.split())
        NS = len(sources)
        sv = [s[0:NTOK, :].rearrange("(m g p) d -> m p g d", g=G, p=P) for s in sources]
        yv = x_out.rearrange("(m g p) d -> m p g d", g=G, p=P)

        def units(engine, body):
            with engine.Fori(0, NU // 2 - 1) as i:
                for u in range(2):
                    body(2 * i + u, u, True)
            for u in range(2):
                body(NU - 2 + u, u, u == 0)

        with nc.Block() as block:
            @block.sync
            def _(sp):
                def load(m, u):
                    if two:
                        sp.dma_start(xb[:, :, :], sv[1][m]).then_inc(x_here, 16)
                    sp.dma_start(xt[:, u, :, :], sv[0][m]).then_inc(x_here, 16)

                def unit(m, u, ahead):
                    if ahead:
                        sp.wait_ge(y_ok, 2 * m)
                        hold(sp)
                        sp.wait_ge(moments, G * m + G)
                        hold(sp)
                        load(m + 1, 1 - u)
                    sp.wait_ge(y_ok, 2 * m + 2)
                    hold(sp)
                    sp.dma_start(yv[m], y[:, :, :]).then_inc(y_out, 16)
                load(0, 0)
                units(sp, unit)
                sp.wait_ge(y_out, 16 * NU)

            @block.gpsimd
            def _(pool):
                def norm(m, u):
                    if two:
                        pool.wait_ge(x_here, 32 * m + 32)
                        nc.gpsimd.tensor_tensor(out=xt[:, u, :, :], in0=xt[:, u, :, :], in1=xb[:, :, :], op=ALU.add).then_inc(added, 1)
                    pool.wait_ge(moments, G * m + G)
                    hold(pool)
                    nc.gpsimd.tensor_scalar(ve[:, :], mv[:, :, 1], EPS, None, ALU.add).then_inc(shifted, 1)
                    pool.wait_ge(shifted, m + 1)
                    nc.gpsimd.tensor_tensor(out=rstd[:, :], in0=ve[:, :], in1=cst["minus_half"][:, 0:G], op=ALU.pow).then_inc(rstd_ok, 1)

                def unit(m, u, ahead):
                    if ahead:
                        norm(m + 1, 1 - u)
                norm(0, 0)
                units(pool, unit)

            @block.scalar
            def _(act):
                def turn(m):
                    act.wait_ge(ln_ps, m + 1)
                    for c in range(DC):
                        nc.scalar.activation(lnT[:, c, :], psT[c], ACT.Copy).then_inc(lnT_ok, 1)

                def unit(m, u, ahead):
                    for f in range(FT):
                        n = P if f < FT - 1 else FLAST
                        act.wait_ge(gate_ps, FT * m + f + 1)
                        nc.scalar.activation(sil[0:n, f % 2, :], psG[f % 2][0:n, :], ACT.Silu).then_inc(sil_ok, 1)
                    if ahead:
                        turn(m + 1)
                turn(0)
                units(act, unit)

            @block.vector
            def _(dve):
                def moments_of(m, u):
                    if two:
                        dve.wait_ge(added, m + 1)
                    else:
                        dve.wait_ge(x_here, 16 * m + 16)
                    for g in range(G):
                        nc.vector.bn_stats(bs[:, g, :], xt[:, u, g, :]).then_inc(stats, 1)
                    dve.wait_ge(stats, G * m + G)
                    hold(dve)
                    for g in range(G):
                        nc.vector.bn_aggr(mv[:, g, :], bs[:, g, :]).then_inc(moments, 1)

                def normalise(m, u):
                    dve.wait_ge(rstd_ok, m + 1)
                    for g in range(G):
                        nc.vector.tensor_scalar(ln[:, g, :], xt[:, u, g, :], mv[:, g, 0:1], rstd[:, g:g + 1],
                                                ALU.subtract, ALU.mult).then_inc(ln_ok, 1)

                def unit(m, u, ahead):
                    for f in range(FT):
                        n = P if f < FT - 1 else FLAST
                        dve.wait_ge(up_ps, FT * m + f + 1)
                        dve.wait_ge(sil_ok, FT * m + f + 1)
                        nc.vector.tensor_tensor(out=hT[0:n, f, :], in0=psU[f % 2][0:n, :], in1=sil[0:n, f % 2, :],
                                                op=ALU.mult).then_inc(h_ok, 1)
                        if f == 1 and ahead:
                            moments_of(m + 1, 1 - u)
                        if f == 3 and ahead:
                            normalise(m + 1, 1 - u)
                    dve.wait_ge(y_out, 16 * m)
                    for k in range(2):
                        dve.wait_ge(down_ps, 2 * m + k + 1)
                        nc.vector.scalar_tensor_tensor(out=y[:, 2 * k:2 * k + 2, :].rearrange("p g d -> p (g d)"), in0=psY[k], scalar=0.5,
                                                       in1=xt[:, u, 2 * k:2 * k + 2, :].rearrange("p g d -> p (g d)"),
                                                       op0=ALU.mult, op1=ALU.add).then_inc(y_ok, 1)
                moments_of(0, 0)
                normalise(0, 0)
                units(dve, unit)

            @block.tensor
            def _(pe):
                def turn(m):
                    pe.wait_ge(ln_ok, G * m + G)
                    pe.wait_ge(lnT_ok, DC * m)
                    for c in range(DC):
                        for g in range(G):
                            mm = nc.tensor.transpose(psT[c][:, g * P:(g + 1) * P], ln[:, g, c * P:(c + 1) * P], cst["ident"][:, :])
                    mm.then_inc(ln_ps, 1)

                def unit(m, u, ahead):
                    pe.wait_ge(lnT_ok, DC * m + DC)
                    for f in range(FT):
                        n = P if f < FT - 1 else FLAST
                        pe.wait_ge(h_ok, FT * m + max(f - 1, 0))
                        for w, ps, ready in ((wgT, psG, gate_ps), (wuT, psU, up_ps)):
                            for c in range(DC):
                                mm = nc.tensor.matmul(ps[f % 2][0:n, :], w[:, c, f * P:f * P + n], lnT[:, c, :],
                                                      start=(c == 0), stop=(c == DC - 1))
                            mm.then_inc(ready, 1)
                    if ahead:
                        turn(m + 1)
                    pe.wait_ge(h_ok, FT * m + FT)
                    for k in range(2):
                        pe.wait_ge(y_ok, 2 * m)
                        for g in (2 * k, 2 * k + 1):
                            for f in range(FT):
                                n = P if f < FT - 1 else FLAST
                                mm = nc.tensor.matmul(psY[k][:, (g % 2) * D:(g % 2 + 1) * D], hT[0:n, f, g * P:(g + 1) * P],
                                                      wdT[0:n, f, :], start=(f == 0), stop=(f == FT - 1))
                        mm.then_inc(down_ps, 1)
                turn(0)
                units(pe, unit)
        clear_semaphores(nc, mem)


def hgrn(nc, cst, tag, x_in, x_out, wT, norm_w):
    R = 4
    TT = T // P
    with ExitStack() as ctx:
        mem = Mem(nc, ctx, tag)
        xt = mem.sb("xt", [P, R, TT, D])
        nw = mem.sb("nw", [P, DC])
        nwh = mem.sb("nwh", [P, DC])
        bs = mem.sb("bs", [P, TT, 6])
        mv = mem.sb("mv", [P, TT, 2])
        ve = mem.sb("ve", [P, TT])
        rstd = mem.sb("rstd", [P, TT])
        ln = mem.sb("ln", [P, TT, D])
        lnT = mem.sb("lnT", [P, DC, T])
        ti, tf, tg, ai, ag, gate, rest, val, o, osq, pT = (
            mem.sb(n, [P, DC, T]) for n in "ti tf tg ai ag gate rest val o osq pT".split())
        ms = mem.sb("ms", [P, TT])
        orstd = mem.sb("orstd", [P, TT])
        y = mem.sb("y", [P, 2, TT, D])
        psI = mem.ps("psI", [P, DC * T])
        psF = mem.ps("psF", [P, DC * T])
        psG = mem.ps("psG", [P, DC * T])
        psI2 = mem.ps("psI2", [P, DC * T])
        psG2 = mem.ps("psG2", [P, DC * T])
        psT = mem.ps("psT", [P, DC * T])
        psS = mem.ps("psS", [P, TT])
        psY = mem.ps("psY", [P, TT * D])
        I, Gt = [psI, psI2], [psG, psG2]
        names = ("nw_here nw_ok stats moments shifted rstd_ok ln_ok ln_ps lnT_ok i_ps f_ps g_ps ti_ok tf_ok tg_ok "
                 "ai_ok ag_ok gate_ok rest_ok val_ok o_ok osq_ok ss_ps ms_ok orstd_ok pT_ok y_ps y_ok y_out")
        (nw_here, nw_ok, stats, moments, shifted, rstd_ok, ln_ok, ln_ps, lnT_ok, i_ps, f_ps, g_ps, ti_ok, tf_ok,
         tg_ok, ai_ok, ag_ok, gate_ok, rest_ok, val_ok, o_ok, osq_ok, ss_ps, ms_ok, orstd_ok, pT_ok, y_ps, y_ok, y_out) = (
            mem.sem(n) for n in names.split())
        x_here = mem.sem2("x_of_parity")
        xv = x_in.rearrange("(b t p) d -> b p t d", t=TT, p=P)
        yv = x_out.rearrange("(b t p) d -> b p t d", t=TT, p=P)

        def flat(a):
            return a.rearrange("p c t -> p (c t)")

        def slots(engine, body):
            with engine.Fori(0, B // R - 1) as i:
                for k in range(R):
                    body(R * i + k, k, True, True)
            for k in range(R):
                body(B - R + k, k, k < R - 1, k < R - 2)

        with nc.Block() as block:
            @block.sync
            def _(sp):
                def load(b, k):
                    sp.dma_start(xt[:, k, :, :], xv[b]).then_inc(x_here[k % 2], 16)

                def slot(b, k, ahead, ahead2):
                    if ahead2:
                        sp.wait_ge(y_ok, 2 * b)
                        hold(sp)
                        sp.wait_ge(moments, TT * b + TT)
                        hold(sp)
                        load(b + 2, (k + 2) % R)
                    sp.wait_ge(y_ok, 2 * b + 2)
                    hold(sp)
                    sp.dma_start(yv[b], y[:, k % 2, :, :]).then_inc(y_out, 16)
                load(0, 0)
                load(1, 1)
                with nc.allow_non_contiguous_dma(reason="256 words, once"):
                    sp.dma_start(nw[:, :], norm_w.rearrange("(c p) -> p c", p=P)).then_inc(nw_here, 16)
                slots(sp, slot)
                sp.wait_ge(y_out, 16 * B)

            @block.gpsimd
            def _(pool):
                def norm(b):
                    pool.wait_ge(moments, TT * b + TT)
                    hold(pool)
                    nc.gpsimd.tensor_scalar(ve[:, :], mv[:, :, 1], EPS, None, ALU.add).then_inc(shifted, 1)
                    pool.wait_ge(shifted, b + 1)
                    nc.gpsimd.tensor_tensor(out=rstd[:, :], in0=ve[:, :], in1=cst["minus_half"][:, 0:TT], op=ALU.pow).then_inc(rstd_ok, 1)

                def slot(b, k, ahead, ahead2):
                    pool.wait_ge(tf_ok, b + 1)
                    pool.wait_ge(o_ok, DC * b)
                    hold(pool)
                    nc.gpsimd.tensor_scalar(gate[:, :, :], tf[:, :, :], 0.5, 0.5, ALU.mult, ALU.add).then_inc(gate_ok, 1)
                    nc.gpsimd.tensor_scalar(rest[:, :, :], tf[:, :, :], -0.25, 0.25, ALU.mult, ALU.add).then_inc(rest_ok, 1)
                    pool.wait_ge(rest_ok, b + 1)
                    pool.wait_ge(ai_ok, b + 1)
                    nc.gpsimd.tensor_tensor(out=val[:, :, :], in0=ai[:, :, :], in1=rest[:, :, :], op=ALU.mult).then_inc(val_ok, 1)
                    if ahead2:
                        norm(b + 2)
                    pool.wait_ge(ms_ok, b + 1)
                    nc.gpsimd.tensor_tensor(out=orstd[:, :], in0=ms[:, :], in1=cst["minus_half"][:, 0:TT], op=ALU.pow).then_inc(orstd_ok, 1)
                pool.wait_ge(nw_here, 16)
                hold(pool)
                nc.gpsimd.tensor_scalar(nwh[:, :], nw[:, :], 0.5, None, ALU.mult).then_inc(nw_ok, 1)
                norm(0)
                norm(1)
                slots(pool, slot)

            @block.scalar
            def _(act):
                def turn(b):
                    act.wait_ge(ln_ps, b + 1)
                    nc.scalar.activation(flat(lnT[:, :, :]), psT, ACT.Copy).then_inc(lnT_ok, 1)

                def tanhs(b, par):
                    act.wait_ge(rest_ok, b)
                    act.wait_ge(ag_ok, b)
                    for ps, dst, ready, done in ((psF, tf, f_ps, tf_ok), (I[par], ti, i_ps, ti_ok), (Gt[par], tg, g_ps, tg_ok)):
                        act.wait_ge(ready, b + 1)
                        nc.scalar.activation(flat(dst[:, :, :]), ps, ACT.Tanh, scale=0.5).then_inc(done, 1)

                def slot(b, k, ahead, ahead2):
                    act.wait_ge(o_ok, DC * b + DC)
                    nc.scalar.activation(osq[:, :, :], o[:, :, :], ACT.Square).then_inc(osq_ok, 1)
                    if ahead:
                        tanhs(b + 1, (k + 1) % 2)
                    if ahead2:
                        turn(b + 2)
                turn(0)
                tanhs(0, 0)
                turn(1)
                slots(act, slot)

            @block.vector
            def _(dve):
                def moments_of(b, k):
                    dve.wait_ge(x_here[k % 2], 8 * (b - k % 2) + 16)
                    for t in range(TT):
                        nc.vector.bn_stats(bs[:, t, :], xt[:, k, t, :]).then_inc(stats, 1)
                    dve.wait_ge(stats, TT * b + TT)
                    hold(dve)
                    for t in range(TT):
                        nc.vector.bn_aggr(mv[:, t, :], bs[:, t, :]).then_inc(moments, 1)

                def normalise(b, k):
                    dve.wait_ge(rstd_ok, b + 1)
                    dve.wait_ge(ln_ps, b)
                    for t in range(TT):
                        nc.vector.tensor_scalar(ln[:, t, :], xt[:, k, t, :], mv[:, t, 0:1], rstd[:, t:t + 1],
                                                ALU.subtract, ALU.mult).then_inc(ln_ok, 1)

                def slot(b, k, ahead, ahead2):
                    dve.wait_ge(ti_ok, b + 1)
                    dve.wait_ge(val_ok, b)
                    nc.vector.scalar_tensor_tensor(out=flat(ai[:, :, :]), in0=flat(ti[:, :, :]), scalar=1.0, in1=I[k % 2],
                                                   op0=ALU.add, op1=ALU.mult).then_inc(ai_ok, 1)
                    dve.wait_ge(tg_ok, b + 1)
                    dve.wait_ge(pT_ok, DC * b)
                    nc.vector.scalar_tensor_tensor(out=flat(ag[:, :, :]), in0=flat(tg[:, :, :]), scalar=1.0, in1=Gt[k % 2],
                                                   op0=ALU.add, op1=ALU.mult).then_inc(ag_ok, 1)
                    dve.wait_ge(gate_ok, b + 1)
                    dve.wait_ge(val_ok, b + 1)
                    dve.wait_ge(osq_ok, b)
                    for c in range(DC):
                        nc.vector.tensor_tensor_scan(o[:, c, :], gate[:, c, :], val[:, c, :], 0.0, ALU.mult, ALU.add).then_inc(o_ok, 1)
                    dve.wait_ge(o_ok, DC * b + DC)
                    dve.wait_ge(y_ps, b)
                    for c in range(DC):
                        nc.vector.scalar_tensor_tensor(out=pT[:, c, :], in0=ag[:, c, :], scalar=nwh[:, c:c + 1], in1=o[:, c, :],
                                                       op0=ALU.mult, op1=ALU.mult).then_inc(pT_ok, 1)
                    if ahead2:
                        moments_of(b + 2, (k + 2) % R)
                    dve.wait_ge(ss_ps, b + 1)
                    nc.vector.tensor_scalar(ms[:, :], psS, 1.0 / D, EPS, ALU.mult, ALU.add).then_inc(ms_ok, 1)
                    if ahead2:
                        normalise(b + 2, (k + 2) % R)
                    dve.wait_ge(orstd_ok, b + 1)
                    dve.wait_ge(y_ps, b + 1)
                    dve.wait_ge(y_out, 16 * b)
                    for t in range(TT):
                        nc.vector.scalar_tensor_tensor(out=y[:, k % 2, t, :], in0=psY[:, t * D:(t + 1) * D], scalar=orstd[:, t:t + 1],
                                                       in1=xt[:, k, t, :], op0=ALU.mult, op1=ALU.add).then_inc(y_ok, 1)
                for b in range(2):
                    moments_of(b, b)
                    normalise(b, b)
                dve.wait_ge(nw_ok, 1)
                slots(dve, slot)

            @block.tensor
            def _(pe):
                def turn(b):
                    pe.wait_ge(ln_ok, TT * b + TT)
                    pe.wait_ge(lnT_ok, b)
                    for c in range(DC):
                        for t in range(TT):
                            mm = nc.tensor.transpose(psT[:, c * T + t * P:c * T + (t + 1) * P], ln[:, t, c * P:(c + 1) * P], cst["ident"][:, :])
                    mm.then_inc(ln_ps, 1)

                def project(b, par):
                    pe.wait_ge(lnT_ok, b + 1)
                    pe.wait_ge(tf_ok, b)
                    for k, ps, ready in ((1, psF, f_ps), (0, I[par], i_ps), (2, Gt[par], g_ps)):
                        if k == 0:
                            pe.wait_ge(ai_ok, b if par else b)
                        for f in range(DC):
                            for c in range(DC):
                                mm = nc.tensor.matmul(ps[:, f * T:(f + 1) * T], wT[:, k, c, f * P:(f + 1) * P], lnT[:, c, :],
                                                      start=(c == 0), stop=(c == DC - 1))
                        mm.then_inc(ready, 1)

                def slot(b, k, ahead, ahead2):
                    if ahead:
                        project(b + 1, (k + 1) % 2)
                    pe.wait_ge(osq_ok, b + 1)
                    pe.wait_ge(ms_ok, b)
                    for t in range(TT):
                        for c in range(DC):
                            mm = nc.tensor.matmul(psS[:, t:t + 1], osq[:, c, t * P:(t + 1) * P], cst["causal"][:, 1, 0:1],
                                                  start=(c == 0), stop=(c == DC - 1))
                    mm.then_inc(ss_ps, 1)
                    pe.wait_ge(pT_ok, DC * b + DC)
                    pe.wait_ge(y_ok, 2 * b)
                    for t in range(TT):
                        for c in range(DC):
                            mm = nc.tensor.matmul(psY[:, t * D:(t + 1) * D], pT[:, c, t * P:(t + 1) * P], wT[:, 3, c, :],
                                                  start=(c == 0), stop=(c == DC - 1))
                    mm.then_inc(y_ps, 1)
                    if ahead2:
                        turn(b + 2)
                turn(0)
                project(0, 0)
                turn(1)
                slots(pe, slot)
        clear_semaphores(nc, mem)


def macaron(nc, x, Wq, Wk, Wv, Wg, Ws, Wo, g_norm, gate_w, w_gate, w_up, w_down,
            Wi1, Wf1, Wg1, Wo1, gnorm1, lut, gate_idx, up_idx, down_idx, out):
    rows = nc.dram_tensor("rows", [NTOK + P, ROW], F32, kind="Internal").ap()
    stream_a = nc.dram_tensor("stream_a", [NTOK + P, D], F32, kind="Internal").ap()
    stream_b = nc.dram_tensor("stream_b", [NTOK + P, D], F32, kind="Internal").ap()
    x_att = nc.dram_tensor("x_att", [NTOK, D], F32, kind="Internal").ap()
    x_ffn = nc.dram_tensor("x_ffn", [NTOK, D], F32, kind="Internal").ap()
    x_hgrn = nc.dram_tensor("x_hgrn", [NTOK, D], F32, kind="Internal").ap()
    NL = 2 * FT * D + DC * INTER
    with ExitStack() as ctx:
        mem = Mem(nc, ctx)
        slot_tok = mem.sb("slot_tok", [P, E], U32)
        lut_w = mem.sb("lut_w", [P, NL])
        pool_dma = [mem.sem(f"got{k}") for k in range(4)], mem.sem2("added")
        lut_row = mem.sb("lut_row", [P, NLUT])
        cst = constants(nc, mem)
        idx = (gate_idx, up_idx, down_idx)
        with ExitStack() as inner:
            wmem = Mem(nc, inner)
            w = load_attention_weights(nc, wmem, Wq, Wk, Ws, Wv, Wg, Wo, g_norm)
            moe_router(nc, cst, "r1_", x, gate_w, rows, stream_a, stream_b, slot_tok, (lut, idx, lut_row, lut_w, 0))
            moe_experts(nc, cst, "e1_", rows, w_gate, w_up, w_down, slot_tok, stream_a, stream_b, pool_dma, 0)
            attention(nc, cst, w, "a_", stream_a, stream_b, x_att)
            clear_semaphores(nc, wmem)
        moe_router(nc, cst, "r2_", x_att, gate_w, rows, stream_a, stream_b, slot_tok, (lut, idx, lut_row, lut_w, 1))
        moe_experts(nc, cst, "e2_", rows, w_gate, w_up, w_down, slot_tok, stream_a, stream_b, pool_dma, 1)
        wgT = mem.sb("wgT", [P, DC, INTER])
        wuT = mem.sb("wuT", [P, DC, INTER])
        wdT = mem.sb("wdT", [P, FT, D])
        h_raw = mem.sb("h_raw", [P, 4, DC, D])
        h_T = mem.sb("h_T", [P, 4, DC, D])
        h_here = mem.sem("h_here")
        with nc.Block() as block:
            @block.sync
            def _(sp):
                for k, src in enumerate((Wi1, Wf1, Wg1, Wo1)):
                    sp.dma_start(h_raw[:, k, :, :], src.rearrange("(r p) n -> p r n", p=P)).then_inc(h_here, 16)
                sp.wait_ge(h_here, 64)
        turn_matrices(nc, "t_", cst, ffn_groups(lut_w, wgT, wuT, wdT) + hgrn_groups(h_raw, h_T))
        lut_ffn(nc, cst, "f1_", [stream_a, stream_b], x_ffn, wgT, wuT, wdT)
        hgrn(nc, cst, "h_", x_ffn, x_hgrn, h_T, gnorm1)
        lut_ffn(nc, cst, "f2_", [x_hgrn], out, wgT, wuT, wdT)


_INS = ['L0_attn_hidden_states', 'L0_attn_Wq', 'L0_attn_Wk', 'L0_attn_Wv', 'L0_attn_Wg', 'L0_attn_Ws', 'L0_attn_Wo',
        'L0_attn_g_norm_weight', 'L0_ffn_gate_w', 'L0_ffn_w_gate', 'L0_ffn_w_up', 'L0_ffn_w_down',
        'L1_attn_Wi', 'L1_attn_Wf', 'L1_attn_Wg', 'L1_attn_Wo', 'L1_attn_gnorm_w',
        'L1_ffn_lut', 'L1_ffn_gate_idx', 'L1_ffn_up_idx', 'L1_ffn_down_idx']


def kernel(**inputs):
    import numpy as _np
    import concourse.bacc as _bacc
    from concourse import mybir as _mybir
    from concourse.bass_utils import run_bass_kernel_spmd as _run

    nc = _bacc.Bacc("TRN2", target_bir_lowering=False, num_devices=1)
    arrays, args = {}, []
    for name in _INS:
        a = _np.ascontiguousarray(inputs[name])
        if name == 'L0_attn_hidden_states':
            a = a.reshape(NTOK, D)
        arrays[f"in_{name}"] = a
        args.append(nc.dram_tensor(f"in_{name}", a.shape, _mybir.dt.from_np(a.dtype), kind="ExternalInput").ap())
    out = nc.dram_tensor("out_stream", (NTOK, D), _mybir.dt.float32, kind="ExternalOutput").ap()
    macaron(nc, *args, out)
    r = _run(nc, [arrays], core_ids=[0])
    return r.results[0]["out_stream"].reshape(B, T, D)
```

```python
from contextlib import ExitStack

import concourse.bass as bass
from concourse import mybir

F32 = mybir.dt.float32
F32R = mybir.dt.float32r
U32 = mybir.dt.uint32
I32 = mybir.dt.int32
ALU = mybir.AluOpType
ACT = mybir.ActivationFunctionType
AX = mybir.AxisListType

P = 128
D = 256
DC = D // P
B, T = 16, 256
NTOK = B * T
NTILE = NTOK // P
E, F, CAP = 64, 128, 128
H, DK, DV, M = 16, 64, 128, 64
INTER = 688
NLUT = 16
FT = -(-INTER // P)
FLAST = INTER - (FT - 1) * P
WIDE = DC * H * DV
LCOL = INTER * D // (P * B)
EPS = 1e-5
ROW = D + E


class Mem:

    def __init__(self, nc, ctx, tag=""):
        self.nc, self.ctx, self.tag = nc, ctx, tag
        self.sems = []

    def sb(self, name, shape, dt=F32):
        return self.ctx.enter_context(self.nc.sbuf_tensor(self.tag + name, shape, dt))

    def ps(self, name, shape):
        size = 1
        for n in shape[1:]:
            size *= n
        whole = self.ctx.enter_context(self.nc.psum_tensor(self.tag + name, [P, -(-size // 512) * 512], F32))
        part = whole[0:shape[0], 0:size]
        return part.rearrange("p (a b) -> p a b", b=shape[2]) if len(shape) == 3 else part

    def sem(self, name):
        self.sems.append(self.ctx.enter_context(self.nc.semaphore(self.tag + name)))
        return self.sems[-1]

    def sem2(self, name):
        return [self.sem(name + "0"), self.sem(name + "1")]


def clear_semaphores(nc, mem):
    with nc.Block() as block:
        @block.gpsimd
        def _(pool):
            for s in mem.sems:
                pool.sem_clear(s)


def hold(engine):
    engine.nop(nofuse=True)


def flat_rows(matrix):
    return matrix.rearrange("a b -> (a b)").rearrange("(p c) -> p c", p=P)


def constants(nc, mem):
    c = {
        "ident": mem.sb("ident", [P, P]),
        "causal": mem.sb("causal", [P, 3, P]),
        "minus_half": mem.sb("minus_half", [P, 8]),
    }
    s_set, s_cut = mem.sem("c_set"), mem.sem("c_cut")
    with nc.Block() as block:
        @block.gpsimd
        def _(pool):
            nc.gpsimd.memset(c["ident"][:, :], 0.0).then_inc(s_set, 1)
            nc.gpsimd.memset(c["causal"][:, :, :], 1.0).then_inc(s_set, 1)
            nc.gpsimd.memset(c["minus_half"][:, :], -0.5).then_inc(s_set, 1)
            pool.wait_ge(s_set, 3)
            nc.gpsimd.affine_select(out=c["ident"][:, :], in_=c["ident"][:, :], compare_op=ALU.not_equal,
                                    fill=1.0, base=0, pattern=[[-1, P]], channel_multiplier=1).then_inc(s_cut, 1)
            for blk in (0, 2):
                nc.gpsimd.affine_select(out=c["causal"][:, blk, :], in_=c["causal"][:, blk, :],
                                        compare_op=ALU.is_ge, fill=0.0, base=0, pattern=[[1, P]],
                                        channel_multiplier=-1).then_inc(s_cut, 1)
            pool.wait_ge(s_cut, 3)
    return c


def moe_router(nc, cst, tag, x_src, gate_w, rows, stream_a, stream_b, slot_tok):
    HALF = NTILE // 2
    with ExitStack() as ctx:
        mem = Mem(nc, ctx, tag)
        gw_in = mem.sb("gw_in", [E, D])
        gwT = mem.sb("gwT", [P, DC, E])
        zeros = mem.sb("zeros", [P, (NTOK // P + 1) * D])
        xt = mem.sb("xt", [P, 2, 2, D])
        bs = mem.sb("bs", [P, 2, 2, 6])
        mv = mem.sb("mv", [P, 2, 2, 2])
        ve = mem.sb("ve", [P, 2, 2])
        rstd = mem.sb("rstd", [P, 2, 2])
        row = mem.sb("row", [P, 2, 2, ROW])
        lnT = mem.sb("lnT", [P, 2, DC, 2 * P])
        lg = mem.sb("lg", [P, 2, 2, E])
        mx = mem.sb("mx", [P, 2, 2, 8])
        nm = mem.sb("nm", [P, 2, 2])
        left = mem.sb("left", [P, 2, 2, E])
        chosen = mem.sb("chosen", [P, 2, 2, E])
        ex = mem.sb("ex", [P, 2, 2, E])
        den = mem.sb("den", [P, 2, 2])
        rden = mem.sb("rden", [P, 2, 2])
        desc_i = mem.sb("desc_i", [P, HALF * P], I32)
        desc = mem.sb("desc", [P, HALF * P])
        key = mem.sb("key", [P, HALF * P])
        cand = mem.sb("cand", [P, CAP])
        both = mem.sb("both", [E, 2, CAP])
        best = mem.sb("best", [E, CAP])
        slot_i = mem.sb("slot_i", [P, 1], I32)
        slot_n = mem.sb("slot_n", [P, 1])
        pad = mem.sb("pad", [P, E])
        tok = mem.sb("tok", [P, E])
        psT = [mem.ps(f"psT{u}", [P, DC, 2 * P]) for u in range(2)]
        psL = [mem.ps(f"psL{u}", [P, 2, E]) for u in range(2)]
        psM = [mem.ps(f"psM{u}", [P, P]) for u in range(2)]
        psG = mem.ps("psG", [P, DC, E])

        gw_here, gw_turned, gw_ready = mem.sem("gw_here"), mem.sem("gw_turned"), mem.sem("gw_ready")
        zero_set, zero_out, desc_set = mem.sem("zero_set"), mem.sem("zero_out"), mem.sem("desc_set")
        x_here, x_kept, row_out = mem.sem2("x_here"), mem.sem2("x_kept"), mem.sem2("row_out")
        stats, moments, shifted, rstd_ok = (mem.sem2(n) for n in ("stats", "moments", "shifted", "rstd_ok"))
        normed, turned, lnT_ok, logits, lg_ok = (mem.sem2(n) for n in ("normed", "turned", "lnT_ok", "logits", "lg_ok"))
        top, cut, nm_ok, chosen_ok, exps, rden_ok, weights = (
            mem.sem2(n) for n in ("top", "cut", "nm_ok", "chosen_ok", "exps", "rden_ok", "weights"))
        maskT, keyed = mem.sem2("maskT"), mem.sem2("keyed")
        found, struck, moved, found2, struck2 = (mem.sem(n) for n in ("found", "struck", "moved", "found2", "struck2"))
        bestT, padded, tokened, tabled = (mem.sem(n) for n in ("bestT", "padded", "tokened", "tabled"))

        xv = x_src.rearrange("(h j p) d -> j p h d", h=2, p=P)
        av = stream_a[0:NTOK, :].rearrange("(h j p) d -> j p h d", h=2, p=P)
        rv = rows[0:NTOK, :].rearrange("(h j p) d -> j p h d", h=2, p=P)

        with nc.Block() as block:
            @block.sync
            def _(sp):
                sp.dma_start(gw_in[:, :], gate_w).then_inc(gw_here, 16)
                def turn(i):
                    for u in range(2):
                        sp.wait_ge(normed[u], 2 * i)
                        hold(sp)
                        sp.wait_ge(x_kept[u], 16 * i)
                        hold(sp)
                        sp.dma_start(xt[:, u, :, :], xv[2 * i + u]).then_inc(x_here[u], 16)
                turn(0)
                with sp.Fori(1, HALF // 2) as i:
                    turn(i)
                sp.wait_ge(found, CAP // 8)
                for h in range(2):
                    sp.dma_start(both[:, h, :], cand[h * E:(h + 1) * E, :]).then_inc(moved, 16)

            @block.scalar
            def _(act):
                act.wait_ge(zero_set, 1)
                act.dma_start(stream_b.rearrange("(p r) d -> p (r d)", p=P), zeros[:, :]).then_inc(zero_out, 16)
                act.dma_start(stream_a[NTOK:NTOK + P, :], zeros[:, 0:D]).then_inc(zero_out, 16)
                act.dma_start(rows[NTOK:NTOK + P, :], zeros[:, 0:ROW]).then_inc(zero_out, 16)
                act.wait_ge(gw_turned, DC)
                nc.scalar.activation(gwT[:, :, :], psG[:, :, :], ACT.Copy).then_inc(gw_ready, 1)
                def turn(i):
                    for u in range(2):
                        act.wait_ge(x_here[u], 16 * i + 16)
                        act.dma_start(av[2 * i + u], xt[:, u, :, :]).then_inc(x_kept[u], 16)
                    for u in range(2):
                        act.wait_ge(turned[u], 4 * i + 4)
                        act.wait_ge(logits[u], 2 * i)
                        nc.scalar.activation(lnT[:, u, :, :], psT[u][:, :, :], ACT.Copy).then_inc(lnT_ok[u], 1)
                    for u in range(2):
                        act.wait_ge(nm_ok[u], i + 1)
                        act.wait_ge(weights[u], 2 * i)
                        for h in range(2):
                            nc.scalar.activation(ex[:, u, h, :], lg[:, u, h, :], ACT.Exp, bias=nm[:, u, h:h + 1],
                                                 accum_out=den[:, u, h:h + 1]).then_inc(exps[u], 1)
                    for u in range(2):
                        act.wait_ge(weights[u], 2 * i + 2)
                        act.dma_start(rv[2 * i + u], row[:, u, :, :]).then_inc(row_out[u], 16)
                turn(0)
                with act.Fori(1, HALF // 2) as i:
                    turn(i)
                for u in range(2):
                    act.wait_ge(x_kept[u], 16 * (HALF // 2))
                    act.wait_ge(row_out[u], 16 * (HALF // 2))
                act.wait_ge(zero_out, 48)

            @block.gpsimd
            def _(pool):
                nc.gpsimd.memset(zeros[:, :], 0.0).then_inc(zero_set, 1)
                nc.gpsimd.iota(slot_i[:, :], pattern=[[0, 1]], base=0, channel_multiplier=1).then_inc(desc_set, 1)
                for h in range(2):
                    pool.wait_ge(desc_set, 1 + h)
                    nc.gpsimd.iota(desc_i[h * E:(h + 1) * E, :], pattern=[[-1, HALF * P]],
                                   base=NTOK - h * HALF * P, channel_multiplier=0).then_inc(desc_set, 1)
                pool.wait_ge(desc_set, 3)
                hold(pool)
                nc.gpsimd.tensor_copy(desc[:, :], desc_i[:, :]).then_inc(desc_set, 1)
                nc.gpsimd.tensor_copy(slot_n[:, :], slot_i[:, :]).then_inc(desc_set, 1)
                def turn(i):
                    for u in range(2):
                        pool.wait_ge(moments[u], 2 * i + 2)
                        hold(pool)
                        nc.gpsimd.tensor_scalar(ve[:, u, :], mv[:, u, :, 1], EPS, None, ALU.add).then_inc(shifted[u], 1)
                        pool.wait_ge(shifted[u], i + 1)
                        pool.wait_ge(normed[u], 2 * i)
                        nc.gpsimd.tensor_tensor(out=rstd[:, u, :], in0=ve[:, u, :], in1=cst["minus_half"][:, 0:2],
                                                op=ALU.pow).then_inc(rstd_ok[u], 1)
                turn(0)
                with pool.Fori(1, HALF // 2) as i:
                    turn(i)

            @block.vector
            def _(dve):
                dve.wait_ge(desc_set, 5)
                def turn(i):
                    for u in range(2):
                        dve.wait_ge(x_here[u], 16 * i + 16)
                        for h in range(2):
                            nc.vector.bn_stats(bs[:, u, h, :], xt[:, u, h, :]).then_inc(stats[u], 1)
                    for u in range(2):
                        dve.wait_ge(stats[u], 2 * i + 2)
                        dve.wait_ge(rstd_ok[u], i)
                        hold(dve)
                        for h in range(2):
                            nc.vector.bn_aggr(mv[:, u, h, :], bs[:, u, h, :]).then_inc(moments[u], 1)
                    for u in range(2):
                        dve.wait_ge(rstd_ok[u], i + 1)
                        dve.wait_ge(row_out[u], 16 * i)
                        for h in range(2):
                            nc.vector.tensor_scalar(row[:, u, h, 0:D], xt[:, u, h, :], mv[:, u, h, 0:1],
                                                    rstd[:, u, h:h + 1], ALU.subtract, ALU.mult).then_inc(normed[u], 1)
                    for u in range(2):
                        dve.wait_ge(logits[u], 2 * i + 2)
                        dve.wait_ge(exps[u], 2 * i)
                        nc.vector.tensor_copy(lg[:, u, :, :], psL[u][:, :, :]).then_inc(lg_ok[u], 1)
                    for u in range(2):
                        dve.wait_ge(lg_ok[u], i + 1)
                        hold(dve)
                        for h in range(2):
                            nc.vector.max(out=mx[:, u, h, :], in_=lg[:, u, h, :]).then_inc(top[u], 1)
                    for u in range(2):
                        dve.wait_ge(top[u], 2 * i + 2)
                        nc.vector.tensor_scalar(nm[:, u, :], mx[:, u, :, 0], -1.0, None, ALU.mult).then_inc(nm_ok[u], 1)
                        for h in range(2):
                            nc.vector.match_replace(out=left[:, u, h, :], in_to_replace=mx[:, u, h, :],
                                                    in_values=lg[:, u, h, :], imm_value=-3.0e38).then_inc(cut[u], 1)
                    for u in range(2):
                        dve.wait_ge(cut[u], 2 * i + 2)
                        dve.wait_ge(maskT[u], i)
                        nc.vector.tensor_tensor(out=chosen[:, u, :, :], in0=left[:, u, :, :], in1=lg[:, u, :, :],
                                                op=ALU.not_equal).then_inc(chosen_ok[u], 1)
                    for u in range(2):
                        dve.wait_ge(exps[u], 2 * i + 2)
                        nc.vector.reciprocal(rden[:, u, :], den[:, u, :]).then_inc(rden_ok[u], 1)
                        dve.wait_ge(rden_ok[u], i + 1)
                        for h in range(2):
                            nc.vector.tensor_scalar(row[:, u, h, D:ROW], ex[:, u, h, :], rden[:, u, h:h + 1], 0.5,
                                                    ALU.mult, ALU.mult).then_inc(weights[u], 1)
                    for u in range(2):
                        dve.wait_ge(maskT[u], i + 1)
                        at = bass.ds((2 * i + u) * P, P)
                        nc.vector.tensor_tensor(out=key[:, at], in0=psM[u][:, :], in1=desc[:, at],
                                                op=ALU.mult).then_inc(keyed[u], 1)
                turn(0)
                with dve.Fori(1, HALF // 2) as i:
                    turn(i)
                for u in range(2):
                    dve.wait_ge(keyed[u], HALF // 2)
                for r in range(CAP // 8):
                    dve.wait_ge(struck, r)
                    nc.vector.max(out=cand[:, 8 * r:8 * r + 8], in_=key[:, :]).then_inc(found, 1)
                    dve.wait_ge(found, r + 1)
                    nc.vector.match_replace(out=key[:, :], in_to_replace=cand[:, 8 * r:8 * r + 8],
                                            in_values=key[:, :], imm_value=0.0).then_inc(struck, 1)
                dve.wait_ge(moved, 32)
                for r in range(CAP // 8):
                    dve.wait_ge(struck2, r)
                    nc.vector.max(out=best[:, 8 * r:8 * r + 8], in_=both[:, :, :].rearrange("e h c -> e (h c)")).then_inc(found2, 1)
                    dve.wait_ge(found2, r + 1)
                    nc.vector.match_replace(out=both[:, :, :].rearrange("e h c -> e (h c)"),
                                            in_to_replace=best[:, 8 * r:8 * r + 8],
                                            in_values=both[:, :, :].rearrange("e h c -> e (h c)"), imm_value=0.0).then_inc(struck2, 1)
                dve.wait_ge(bestT, 1)
                nc.vector.tensor_scalar(pad[:, :], psG[:, 0, :], 0.0, slot_n[:, 0:1], ALU.is_equal, ALU.mult).then_inc(padded, 1)
                dve.wait_ge(padded, 1)
                nc.vector.tensor_tensor(out=tok[:, :], in0=pad[:, :], in1=psG[:, 0, :], op=ALU.subtract).then_inc(tokened, 1)
                dve.wait_ge(tokened, 1)
                nc.vector.tensor_scalar(slot_tok[:, :], tok[:, :], float(NTOK), None, ALU.add).then_inc(tabled, 1)
                dve.wait_ge(tabled, 1)

            @block.tensor
            def _(pe):
                pe.wait_ge(gw_here, 16)
                for c in range(DC):
                    nc.tensor.transpose(psG[:, c, :], gw_in[:, c * P:(c + 1) * P], cst["ident"][0:E, 0:E]).then_inc(gw_turned, 1)
                pe.wait_ge(gw_ready, 1)
                def turn(i):
                    for u in range(2):
                        pe.wait_ge(normed[u], 2 * i + 2)
                        pe.wait_ge(lnT_ok[u], i)
                        for h in range(2):
                            for c in range(DC):
                                nc.tensor.transpose(psT[u][:, c, h * P:(h + 1) * P], row[:, u, h, c * P:(c + 1) * P],
                                                    cst["ident"][:, :]).then_inc(turned[u], 1)
                    for u in range(2):
                        pe.wait_ge(lnT_ok[u], i + 1)
                        pe.wait_ge(lg_ok[u], i)
                        for h in range(2):
                            for c in range(DC):
                                mm = nc.tensor.matmul(psL[u][:, h, :], lnT[:, u, c, h * P:(h + 1) * P], gwT[:, c, :],
                                                      start=(c == 0), stop=(c == DC - 1))
                            mm.then_inc(logits[u], 1)
                    for u in range(2):
                        pe.wait_ge(chosen_ok[u], i + 1)
                        pe.wait_ge(keyed[u], i)
                        nc.tensor.transpose(psM[u][:, :], chosen[:, u, :, :].rearrange("p h e -> p (h e)"),
                                            cst["ident"][:, :]).then_inc(maskT[u], 1)
                turn(0)
                with pe.Fori(1, HALF // 2) as i:
                    turn(i)
                pe.wait_ge(found2, CAP // 8)
                nc.tensor.transpose(psG[:, 0, :], best[:, :], cst["ident"][0:E, 0:E]).then_inc(bestT, 1)
        clear_semaphores(nc, mem)


def moe_experts(nc, cst, tag, rows, w_gate, w_up, w_down, slot_tok, stream_a, stream_b, pool_dma, run, wide=None):
    U = 4
    with ExitStack() as ctx:
        mem = Mem(nc, ctx, tag)
        wg = mem.sb("wg", [P, U, DC, F])
        wu = mem.sb("wu", [P, U, DC, F])
        wd = mem.sb("wd", [P, U, D])
        idx = mem.sb("idx", [P, U], U32)
        xg = mem.sb("xg", [P, U, ROW])
        wcol = mem.sb("wcol", [P, U])
        xgT = mem.sb("xgT", [P, 2, DC, CAP])
        sil = mem.sb("sil", [P, 2, CAP])
        hT = mem.sb("hT", [P, 2, CAP])
        y = mem.sb("y", [P, U, D])
        psX = [mem.ps(f"psX{u}", [P, DC, CAP]) for u in range(2)]
        psH = [mem.ps(f"psH{u}", [P, 2, CAP]) for u in range(2)]
        psY = [mem.ps(f"psY{u}", [P, D]) for u in range(2)]
        w_here = [mem.sem(f"w_here{k}") for k in range(U)]
        got, added = pool_dma
        got0, added0 = 16 * run * (E // U), 16 * run * (E // 2)
        idx_ok, wcol_ok = mem.sem("idx_ok"), mem.sem("wcol_ok")
        down = [mem.sem(f"down{k}") for k in range(U)]
        turned, xgT_ok, hid, silued, gated, y_ok = (
            mem.sem2(n) for n in ("turned", "xgT_ok", "hid", "silued", "gated", "y_ok"))
        streams = [stream_a, stream_b]
        if wide:
            wide_src, wide_hi, wide_lo = wide
            wide_raw = mem.sb("wide_raw", [P, 3, WIDE])
            wide_here, wide_high, wide_low = mem.sem("wide_here"), mem.sem("wide_high"), mem.sem("wide_low")

        def share(buf, i):
            return buf[:, :, bass.ds(i * (WIDE // (E // U)), WIDE // (E // U))]
        wgv = w_gate.rearrange("e (c p) f -> e p c f", p=P)
        wuv = w_up.rearrange("e (c p) f -> e p c f", p=P)

        with nc.Block() as block:
            @block.sync
            def _(sp):
                def turn(i):
                    for k in range(U):
                        sp.wait_ge(down[k], i)
                        hold(sp)
                        e = U * i + k
                        sp.dma_start(wg[:, k, :, :], wgv[e]).then_inc(w_here[k], 16)
                        sp.dma_start(wu[:, k, :, :], wuv[e]).then_inc(w_here[k], 16)
                        sp.dma_start(wd[:, k, :], w_down[e]).then_inc(w_here[k], 16)
                turn(0)
                with sp.Fori(1, E // U) as i:
                    turn(i)

            @block.gpsimd
            def _(pool):
                def fetch(i, k):
                    e = U * i + k
                    nc.gpsimd.tensor_copy(idx[:, k:k + 1], slot_tok[:, bass.ds(e, 1)]).then_inc(idx_ok, 1)
                    pool.wait_ge(idx_ok, e + 1)
                    hold(pool)
                    pool.indirect_dma_start(out=xg[:, k, :], out_offset=None, in_=rows,
                                            in_offset=bass.IndirectOffsetOnAxis(ap=idx[:, k:k + 1], axis=0)).then_inc(got[k], 16)

                def scatter(i, k):
                    u = k % 2
                    pool.wait_ge(y_ok[u], 2 * i + k // 2 + 1)
                    pool.wait_ge(added[u], added0 + 16 * (2 * i + k // 2))
                    hold(pool)
                    pool.indirect_dma_start(out=streams[u], out_offset=bass.IndirectOffsetOnAxis(ap=idx[:, k:k + 1], axis=0),
                                            in_=y[:, k, :], in_offset=None, compute_op=ALU.add).then_inc(added[u], 16)

                def weight(i, k):
                    pool.wait_ge(got[k], got0 + 16 * i + 16)
                    hold(pool)
                    nc.gpsimd.tensor_copy(wcol[:, k:k + 1], xg[:, k, bass.ds(D + U * i + k, 1)]).then_inc(wcol_ok, 1)

                for k in range(2):
                    fetch(0, k)
                def turn(i):
                    for k in range(U):
                        weight(i, k)
                        n, kk = (i, k + 2) if k < 2 else (i + 1, k - 2)
                        u = kk % 2
                        pool.wait_ge(added[u], added0 + (16 * (2 * (n - 1) + kk // 2 + 1) if k >= 2 else 16 * (2 * n)))
                        fetch(n, kk)
                        scatter(i, k)
                turn(0)
                with pool.Fori(1, E // U - 1) as i:
                    turn(i)
                i = E // U - 1
                for k in range(U):
                    weight(i, k)
                    if k < 2:
                        pool.wait_ge(added[k % 2], added0 + 16 * (2 * i))
                        fetch(i, k + 2)
                    scatter(i, k)
                for u in range(2):
                    pool.wait_ge(added[u], added0 + 16 * (E // 2))

            @block.tensor
            def _(pe):
                def turn(i):
                    for k in range(U):
                        u, n = k % 2, 2 * i + k // 2
                        pe.wait_ge(got[k], got0 + 16 * i + 16)
                        pe.wait_ge(xgT_ok[u], n)
                        for c in range(DC):
                            nc.tensor.transpose(psX[u][:, c, :], xg[:, k, c * P:(c + 1) * P], cst["ident"][:, :]).then_inc(turned[u], 1)
                        pe.wait_ge(w_here[k], 48 * i + 48)
                        pe.wait_ge(xgT_ok[u], n + 1)
                        pe.wait_ge(gated[u], n)
                        for g, w in enumerate((wg, wu)):
                            for c in range(DC):
                                mm = nc.tensor.matmul(psH[u][:, g, :], w[:, k, c, :], xgT[:, u, c, :],
                                                      start=(c == 0), stop=(c == DC - 1))
                            mm.then_inc(hid[u], 1)
                        pe.wait_ge(gated[u], n + 1)
                        pe.wait_ge(y_ok[u], n)
                        nc.tensor.matmul(psY[u][:, :], hT[:, u, :], wd[:, k, :], start=True, stop=True).then_inc(down[k], 1)
                turn(0)
                with pe.Fori(1, E // U) as i:
                    turn(i)

            @block.scalar
            def _(act):
                def high_part(i):
                    act.wait_ge(wide_here, 48)
                    nc.scalar.activation(share(wide_hi, i), share(wide_raw, i), ACT.Copy).then_inc(wide_high, 1)

                if wide:
                    for k, src in enumerate(wide_src):
                        act.dma_start(wide_raw[:, k, :].rearrange("p (c n) -> p c n", n=src.shape[2]), src).then_inc(wide_here, 16)

                def turn(i):
                    for k in range(U):
                        u, n = k % 2, 2 * i + k // 2
                        act.wait_ge(turned[u], 2 * n + 2)
                        act.wait_ge(hid[u], 2 * n)
                        nc.scalar.activation(xgT[:, u, :, :], psX[u][:, :, :], ACT.Copy).then_inc(xgT_ok[u], 1)
                        act.wait_ge(hid[u], 2 * n + 2)
                        act.wait_ge(gated[u], n)
                        nc.scalar.activation(sil[:, u, :], psH[u][:, 0, :], ACT.Silu).then_inc(silued[u], 1)
                turn(0)
                with act.Fori(1, E // U) as i:
                    turn(i)
                    if wide:
                        high_part(i - 1)
                if wide:
                    high_part(E // U - 1)

            @block.vector
            def _(dve):
                def turn(i):
                    for k in range(U):
                        u, n = k % 2, 2 * i + k // 2
                        dve.wait_ge(silued[u], n + 1)
                        dve.wait_ge(down[k - 2] if k >= 2 else down[k + 2], i + 1 if k >= 2 else i)
                        nc.vector.tensor_tensor(out=hT[:, u, :], in0=psH[u][:, 1, :], in1=sil[:, u, :],
                                                op=ALU.mult).then_inc(gated[u], 1)
                        dve.wait_ge(down[k], i + 1)
                        dve.wait_ge(wcol_ok, U * i + k + 1)
                        nc.vector.tensor_scalar(y[:, k, :], psY[u][:, :], wcol[:, k:k + 1], None, ALU.mult).then_inc(y_ok[u], 1)

                def low_part(i):
                    dve.wait_ge(wide_high, i + 1)
                    nc.vector.tensor_tensor(out=share(wide_lo, i), in0=share(wide_raw, i), in1=share(wide_hi, i),
                                            op=ALU.subtract).then_inc(wide_low, 1)
                turn(0)
                with dve.Fori(1, E // U) as i:
                    turn(i)
                    if wide:
                        low_part(i - 1)
                if wide:
                    low_part(E // U - 1)
        clear_semaphores(nc, mem)


def attention_weights(nc, mem, Wq, Wk, Ws, g_norm, lut):
    w = {
        "q": mem.sb("wq", [P, DC, H * DK]), "k": mem.sb("wk", [P, DC, H * DK]), "s": mem.sb("ws", [P, DC, H * M]),
        "norm": mem.sb("g_norm", [P, DV]), "lut": mem.sb("lut_row", [P, NLUT]),
        "here": mem.sem("attention_weights"),
    }
    with nc.Block() as block:
        @block.sync
        def _(sp):
            for name, src in (("q", Wq), ("k", Wk), ("s", Ws)):
                sp.dma_start(w[name][:, :, :], src.rearrange("(c p) n -> p c n", p=P)).then_inc(w["here"], 16)
            sp.dma_start(w["norm"][:, :], g_norm.partition_broadcast(P)).then_inc(w["here"], 16)
            sp.dma_start(w["lut"][:, :], lut.partition_broadcast(P)).then_inc(w["here"], 16)
    return w


def attention(nc, cst, w, tag, stream_a, stream_b, x_out, indices, looked_up):
    HQ = 4
    QPB = H // HQ
    TT = T // P
    NH = HQ // 2
    with ExitStack() as ctx:
        mem = Mem(nc, ctx, tag)
        xab = mem.sb("xab", [P, 2, TT, D])
        xs = mem.sb("xs", [P, TT, D])
        xacc = mem.sb("xacc", [P, TT, D])
        bs = mem.sb("bs", [P, TT, 6])
        mv = mem.sb("mv", [P, TT, 2])
        ve = mem.sb("ve", [P, TT])
        rstd = mem.sb("rstd", [P, TT])
        ln = mem.sb("ln", [P, TT, D])
        lnT = mem.sb("lnT", [P, DC, T])
        lnTp = mem.sb("lnTp", [P, 2, DC, T], F32R)
        norm_half = mem.sb("norm_half", [P, DV])
        qT = mem.sb("qT", [P, NH, T])
        kT = mem.sb("kT", [P, NH, T])
        em = mem.sb("em", [P, TT, HQ * M])
        emT = mem.sb("emT", [P, NH, T])
        v = mem.sb("v", [P, 2, TT, HQ * DV])
        gs = mem.sb("gs", [P, TT, HQ * DV])
        tg = mem.sb("tg", [P, TT, HQ * DV])
        rz = mem.sb("rz", [P, TT, HQ * M])
        at = mem.sb("at", [P, HQ, 3 * P])
        bt = at
        okn = mem.sb("okn", [P, TT * HQ, M])
        mxs = mem.sb("mxs", [P, TT * HQ])
        sm = mem.sb("sm", [P, TT * HQ])
        rsm = mem.sb("rsm", [P, TT * HQ])
        pz = mem.sb("pz", [P, TT, HQ * M])
        pzT = mem.sb("pzT", [P, NH, T])
        sq = mem.sb("sq", [P, TT * HQ, DV])
        ss = mem.sb("ss", [P, TT * HQ])
        ms = mem.sb("ms", [P, TT * HQ])
        orstd = mem.sb("orstd", [P, TT * HQ])
        o1 = mem.sb("o1", [P, TT * HQ, DV])
        o2 = sq.rearrange("p (t h) v -> p t (h v)", t=TT)
        oT = mem.sb("oT", [P, 2, HQ, T], F32R)
        index = mem.sb("index", [P, 3, LCOL], I32)
        pick = mem.sb("pick", [P, 3, LCOL])
        found = mem.sb("found", [P, 2, 3, LCOL])
        psA = [mem.ps(f"psA{k}", [P, 512]) for k in range(2)]
        psB = [mem.ps(f"psB{k}", [P, 512]) for k in range(2)]
        psC = [mem.ps(f"psC{k}", [P, 512]) for k in range(2)]
        psD = mem.ps("psD", [P, 2, 512])

        names = ("x_here x_out_done xs_ok xacc_ok stats moments shifted rstd_ok ln_ok ln_ps lnT_ok norm_ok "
                 "v_ps v_ok q_ps q_ok k_ps k_ok g_ps th_ok tg_ok gs_ok s_ps sc_ok em_ok z_ps rz_ok et_ps et_ok "
                 "at_ps at_ok ok_ps okn_ok mx_ok sub_ok pe_ok sm_ok rsm_ok er_ok pz_ok pzt_ps pzt_ok bt_ps bt_ok "
                 "ov_ps sq_ok ss_ok ms_ok orstd_ok o1_ok o2_ok ot_ps ot_ok out_ps acc_ok "
                 "index_here picked looked looked_out lnTh_ok lnTl_ok otl_ok")
        (x_here, x_out_done, xs_ok, xacc_ok, stats, moments, shifted, rstd_ok, ln_ok, ln_ps, lnT_ok, norm_ok,
         v_ps, v_ok, q_ps, q_ok, k_ps, k_ok, g_ps, th_ok, tg_ok, gs_ok, s_ps, sc_ok, em_ok, z_ps, rz_ok, et_ps, et_ok,
         at_ps, at_ok, ok_ps, okn_ok, mx_ok, sub_ok, pe_ok, sm_ok, rsm_ok, er_ok, pz_ok, pzt_ps, pzt_ok, bt_ps, bt_ok,
         ov_ps, sq_ok, ss_ok, ms_ok, orstd_ok, o1_ok, o2_ok, ot_ps, ot_ok, out_ps, acc_ok,
         index_here, picked, looked, looked_out, lnTh_ok, lnTl_ok, otl_ok) = (
            mem.sem(n) for n in names.split())
        av = stream_a[0:NTOK, :].rearrange("(b t p) d -> b p t d", t=TT, p=P)
        bv = stream_b[0:NTOK, :].rearrange("(b t p) d -> b p t d", t=TT, p=P)
        ov = x_out.rearrange("(b t p) d -> b p t d", t=TT, p=P)

        def over_slots(stat):
            return stat[:, :].unsqueeze(2).to_broadcast([P, TT * HQ, M])

        with nc.Block() as block:
            @block.sync
            def _(sp):
                def load(b):
                    sp.dma_start(xab[:, 0, :, :], av[b]).then_inc(x_here, 16)
                    sp.dma_start(xab[:, 1, :, :], bv[b]).then_inc(x_here, 16)

                def load_index(b):
                    for k in range(3):
                        sp.dma_start(index[:, k, :], flat_rows(indices[k])[:, bass.ds(b * LCOL, LCOL)]).then_inc(index_here, 16)

                def store_looked_up(b):
                    sp.wait_ge(looked, NLUT * b + NLUT)
                    hold(sp)
                    for k in range(3):
                        sp.dma_start(flat_rows(looked_up[k])[:, bass.ds(b * LCOL, LCOL)], found[:, (NLUT - 1) % 2, k, :]).then_inc(looked_out, 16)

                def store(b):
                    sp.wait_ge(acc_ok, QPB * b + QPB + 1)
                    hold(sp)
                    sp.dma_start(ov[b], xacc[:, :, :]).then_inc(x_out_done, 16)

                load(0)
                load_index(0)
                def turn(b):
                    sp.wait_ge(xs_ok, b + 1)
                    hold(sp)
                    load(b + 1)
                    store_looked_up(b)
                    load_index(b + 1)
                    store(b)
                turn(0)
                with sp.Fori(1, B - 1) as b:
                    turn(b)
                store_looked_up(B - 1)
                store(B - 1)
                sp.wait_ge(x_out_done, 16 * B)
                sp.wait_ge(looked_out, 48 * B)

            @block.gpsimd
            def _(pool):
                def add_stream(b):
                    pool.wait_ge(x_here, 32 * b + 32)
                    pool.wait_ge(xacc_ok, b)
                    nc.gpsimd.tensor_tensor(out=xs[:, :, :], in0=xab[:, 0, :, :], in1=xab[:, 1, :, :], op=ALU.add).then_inc(xs_ok, 1)

                def rstd_of_stream(b):
                    pool.wait_ge(moments, TT * b + TT)
                    hold(pool)
                    nc.gpsimd.tensor_scalar(ve[:, :], mv[:, :, 1], EPS, None, ALU.add).then_inc(shifted, 1)
                    pool.wait_ge(shifted, b + 1)
                    nc.gpsimd.tensor_tensor(out=rstd[:, :], in0=ve[:, :], in1=cst["minus_half"][:, 0:TT], op=ALU.pow).then_inc(rstd_ok, 1)

                def gate(m):
                    for t in range(TT):
                        pool.wait_ge(tg_ok, TT * m + t + 1)
                        nc.gpsimd.tensor_tensor(out=gs[:, t, :].rearrange("p (h v) -> p h v", v=DV),
                                                in0=tg[:, t, :].rearrange("p (h v) -> p h v", v=DV),
                                                in1=norm_half[:, :].unsqueeze(1).to_broadcast([P, HQ, DV]),
                                                op=ALU.mult).then_inc(gs_ok, 1)

                def look_up(b, codes):
                    for c in codes:
                        pool.wait_ge(looked, NLUT * b + c)
                        if c == 0:
                            pool.wait_ge(index_here, 48 * b + 48)
                        if c == 1:
                            pool.wait_ge(looked_out, 48 * b)
                        hold(pool)
                        nc.gpsimd.tensor_scalar(found[:, 0, :, :] if c == 0 else pick[:, :, :], index[:, :, :], float(c),
                                                w["lut"][:, c:c + 1], ALU.is_equal, ALU.mult).then_inc(looked if c == 0 else picked, 1)
                        if c > 0:
                            pool.wait_ge(picked, (NLUT - 1) * b + c)
                            nc.gpsimd.tensor_tensor(out=found[:, c % 2, :, :], in0=found[:, 1 - c % 2, :, :], in1=pick[:, :, :],
                                                    op=ALU.add).then_inc(looked, 1)

                def slot(b, q, last):
                    n = QPB * b + q
                    ahead = not (last and q == QPB - 1)
                    look_up(b, range(4 * q, 4 * q + 1))
                    if q == 1 and not last:
                        add_stream(b + 1)
                    if q == 2 and not last:
                        rstd_of_stream(b + 1)
                    pool.wait_ge(mx_ok, n + 1)
                    nc.gpsimd.tensor_tensor(out=okn[:, :, :], in0=okn[:, :, :], in1=over_slots(mxs), op=ALU.subtract).then_inc(sub_ok, 1)
                    pool.wait_ge(pe_ok, n + 1)
                    nc.gpsimd.tensor_tensor(out=pz[:, :, :].rearrange("p t (h m) -> p (t h) m", m=M), in0=okn[:, :, :],
                                            in1=rz[:, :, :].rearrange("p t (h m) -> p (t h) m", m=M), op=ALU.mult).then_inc(er_ok, 1)
                    pool.wait_ge(er_ok, n + 1)
                    pool.wait_ge(rsm_ok, n + 1)
                    nc.gpsimd.tensor_tensor(out=pz[:, :, :].rearrange("p t (h m) -> p (t h) m", m=M),
                                            in0=pz[:, :, :].rearrange("p t (h m) -> p (t h) m", m=M),
                                            in1=over_slots(rsm), op=ALU.mult).then_inc(pz_ok, 1)
                    look_up(b, range(4 * q + 1, 4 * q + 4))
                    pool.wait_ge(ss_ok, n + 1)
                    hold(pool)
                    nc.gpsimd.tensor_scalar(ms[:, :], ss[:, :], 1.0 / DV, EPS, ALU.mult, ALU.add).then_inc(ms_ok, 1)
                    pool.wait_ge(ms_ok, n + 1)
                    nc.gpsimd.tensor_tensor(out=orstd[:, :], in0=ms[:, :], in1=cst["minus_half"][:, 0:TT * HQ], op=ALU.pow).then_inc(orstd_ok, 1)
                    pool.wait_ge(orstd_ok, n + 1)
                    pool.wait_ge(o1_ok, n + 1)
                    nc.gpsimd.tensor_tensor(out=o2[:, :, :].rearrange("p t (h v) -> p (t h) v", v=DV), in0=o1[:, :, :],
                                            in1=orstd[:, :].unsqueeze(2).to_broadcast([P, TT * HQ, DV]), op=ALU.mult).then_inc(o2_ok, 1)
                    if ahead:
                        gate(n + 1)
                    if q == 0:
                        pool.wait_ge(x_out_done, 16 * b)
                        pool.wait_ge(xs_ok, b + 1)
                        hold(pool)
                        nc.gpsimd.tensor_copy(xacc[:, :, :], xs[:, :, :]).then_inc(xacc_ok, 1)

                pool.wait_ge(w["here"], 16 * 5)
                hold(pool)
                nc.gpsimd.tensor_scalar(norm_half[:, :], w["norm"][:, :], 0.5, None, ALU.mult).then_inc(norm_ok, 1)
                pool.wait_ge(norm_ok, 1)
                add_stream(0)
                rstd_of_stream(0)
                gate(0)
                for q in range(QPB):
                    slot(0, q, False)
                with pool.Fori(1, B - 1) as b:
                    for q in range(QPB):
                        slot(b, q, False)
                for q in range(QPB):
                    slot(B - 1, q, True)

            @block.scalar
            def _(act):
                def copy(out, in_, done, scale=1.0):
                    nc.scalar.activation(out, in_, ACT.Copy, scale=scale).then_inc(done, 1)

                def turn_stream(b):
                    act.wait_ge(ln_ps, b + 1)
                    copy(lnT[:, :, :].rearrange("p c t -> p (c t)"), psC[1], lnT_ok)
                    copy(lnTp[:, 0, :, :].rearrange("p c t -> p (c t)"), psC[1], lnTh_ok)

                def value(m, par, t):
                    act.wait_ge(v_ps, TT * m + t + 1)
                    copy(v[:, par, t, :], psA[t], v_ok)

                def query(m):
                    act.wait_ge(q_ps, m + 1)
                    copy(qT[:, :, :].rearrange("p a t -> p (a t)"), psA[0], q_ok, scale=DK ** -0.5)

                def gate_tanh(m):
                    for t in range(TT):
                        act.wait_ge(g_ps, TT * m + t + 1)
                        act.wait_ge(gs_ok, TT * m)
                        nc.scalar.activation(tg[:, t, :], psA[t], ACT.Tanh, scale=0.5).then_inc(th_ok, 1)

                def exp_s(m):
                    act.wait_ge(sc_ok, m + 1)
                    nc.scalar.activation(em[:, :, :], em[:, :, :], ACT.Exp).then_inc(em_ok, 1)

                def slot(b, q, last):
                    n = QPB * b + q
                    ahead = not (last and q == QPB - 1)
                    if q == QPB - 1 and not last:
                        turn_stream(b + 1)
                    act.wait_ge(et_ps, n + 1)
                    copy(emT[:, :, :].rearrange("p a t -> p (a t)"), psC[1], et_ok)
                    if ahead:
                        value(n + 1, (q + 1) % 2, 0)
                    act.wait_ge(sub_ok, n + 1)
                    nc.scalar.activation(okn[:, :, :], okn[:, :, :], ACT.Exp).then_inc(pe_ok, 1)
                    if ahead:
                        value(n + 1, (q + 1) % 2, 1)
                        query(n + 1)
                    act.wait_ge(pzt_ps, n + 1)
                    copy(pzT[:, :, :].rearrange("p a t -> p (a t)"), psC[1], pzt_ok)
                    act.wait_ge(ov_ps, n + 1)
                    nc.scalar.activation(sq[:, :, :].rearrange("p (t h) v -> p t (h v)", t=TT), psD, ACT.Square).then_inc(sq_ok, 1)
                    if ahead:
                        gate_tanh(n + 1)
                        exp_s(n + 1)
                    for a in range(NH):
                        act.wait_ge(ot_ps, NH * n + a + 1)
                        copy(oT[:, 0, 2 * a:2 * a + 2, :].rearrange("p a t -> p (a t)"), psD[:, a, :], ot_ok)

                turn_stream(0)
                value(0, 0, 0)
                value(0, 0, 1)
                query(0)
                gate_tanh(0)
                exp_s(0)
                for q in range(QPB):
                    slot(0, q, False)
                with act.Fori(1, B - 1) as b:
                    for q in range(QPB):
                        slot(b, q, False)
                for q in range(QPB):
                    slot(B - 1, q, True)

            @block.vector
            def _(dve):
                def moments_of_stream(b):
                    dve.wait_ge(xs_ok, b + 1)
                    for t in range(TT):
                        nc.vector.bn_stats(bs[:, t, :], xs[:, t, :]).then_inc(stats, 1)
                    dve.wait_ge(stats, TT * b + TT)
                    hold(dve)
                    for t in range(TT):
                        nc.vector.bn_aggr(mv[:, t, :], bs[:, t, :]).then_inc(moments, 1)

                def normalise_stream(b):
                    dve.wait_ge(rstd_ok, b + 1)
                    for t in range(TT):
                        nc.vector.tensor_scalar(ln[:, t, :], xs[:, t, :], mv[:, t, 0:1], rstd[:, t:t + 1],
                                                ALU.subtract, ALU.mult).then_inc(ln_ok, 1)

                def low_part_of_stream(b):
                    dve.wait_ge(lnTh_ok, b + 1)
                    dve.wait_ge(lnT_ok, b + 1)
                    nc.vector.tensor_tensor(out=lnTp[:, 1, :, :], in0=lnT[:, :, :], in1=lnTp[:, 0, :, :], op=ALU.subtract).then_inc(lnTl_ok, 1)

                def low_part_of_output(n):
                    for a in range(NH):
                        dve.wait_ge(ot_ok, NH * n + a + 1)
                        nc.vector.tensor_tensor(out=oT[:, 1, 2 * a:2 * a + 2, :].rearrange("p a t -> p (a t)"), in0=psD[:, a, :],
                                                in1=oT[:, 0, 2 * a:2 * a + 2, :].rearrange("p a t -> p (a t)"),
                                                op=ALU.subtract).then_inc(otl_ok, 1)

                def add_output(b, n):
                    dve.wait_ge(out_ps, n + 1)
                    dve.wait_ge(xacc_ok, b + 1)
                    dve.wait_ge(acc_ok, n + 1)
                    nc.vector.tensor_tensor(out=xacc[:, :, :].rearrange("p t d -> p (t d)"), in0=psA[1],
                                            in1=xacc[:, :, :].rearrange("p t d -> p (t d)"), op=ALU.add).then_inc(acc_ok, 1)

                def key(m):
                    dve.wait_ge(k_ps, m + 1)
                    nc.vector.tensor_copy(kT[:, :, :].rearrange("p a t -> p (a t)"), psA[1]).then_inc(k_ok, 1)

                def gate(m):
                    for t in range(TT):
                        dve.wait_ge(th_ok, TT * m + t + 1)
                        nc.vector.scalar_tensor_tensor(out=tg[:, t, :], in0=tg[:, t, :], scalar=1.0, in1=psA[t],
                                                       op0=ALU.add, op1=ALU.mult).then_inc(tg_ok, 1)

                def clip(m):
                    dve.wait_ge(s_ps, m + 1)
                    nc.vector.tensor_scalar(em[:, :, :].rearrange("p t m -> p (t m)"), psA[0], -32.0, 32.0,
                                            ALU.max, ALU.min).then_inc(sc_ok, 1)

                def invert_z(m):
                    dve.wait_ge(z_ps, m + 1)
                    nc.vector.reciprocal(rz[:, :, :].rearrange("p t m -> p (t m)"), psC[0]).then_inc(rz_ok, 1)

                def masked(dst, n, ps_ready, done):
                    for h in range(HQ):
                        dve.wait_ge(ps_ready, HQ * n + h + 1)
                        nc.vector.tensor_tensor(out=dst[:, h, :], in0=psB[h % 2][:, 0:3 * P],
                                                in1=cst["causal"][:, :, :].rearrange("p a i -> p (a i)"), op=ALU.mult).then_inc(done, 1)

                def scores(m):
                    masked(at, m, at_ps, at_ok)
                    invert_z(m)

                def slot(b, q, last, first=False):
                    n = QPB * b + q
                    ahead = not (last and q == QPB - 1)
                    if q == QPB - 1 and not last:
                        low_part_of_stream(b + 1)
                    dve.wait_ge(ok_ps, n + 1)
                    dve.wait_ge(rz_ok, n + 1)
                    nc.vector.tensor_tensor(out=okn[:, :, :].rearrange("p a m -> p (a m)"), in0=psA[1],
                                            in1=rz[:, :, :].rearrange("p t m -> p (t m)"), op=ALU.mult).then_inc(okn_ok, 1)
                    dve.wait_ge(okn_ok, n + 1)
                    nc.vector.reduce_max(mxs[:, :], okn[:, :, :], axis=AX.X).then_inc(mx_ok, 1)
                    if not first:
                        low_part_of_output(n - 1)
                    dve.wait_ge(pe_ok, n + 1)
                    nc.vector.reduce_sum(sm[:, :], okn[:, :, :], axis=AX.X).then_inc(sm_ok, 1)
                    dve.wait_ge(sm_ok, n + 1)
                    nc.vector.reciprocal(rsm[:, :], sm[:, :]).then_inc(rsm_ok, 1)
                    if q == 1 and not last:
                        moments_of_stream(b + 1)
                    if q == 2 and not last:
                        normalise_stream(b + 1)
                    if not first:
                        add_output(b - 1 if q == 0 else b, n - 1)
                    if ahead:
                        key(n + 1)
                    masked(bt, n, bt_ps, bt_ok)
                    dve.wait_ge(sq_ok, n + 1)
                    dve.wait_ge(gs_ok, TT * n + TT)
                    nc.vector.tensor_tensor(out=o1[:, :, :].rearrange("p (t h) v -> p t (h v)", t=TT), in0=psD,
                                            in1=gs[:, :, :], op=ALU.mult).then_inc(o1_ok, 1)
                    nc.vector.reduce_sum(ss[:, :], sq[:, :, :], axis=AX.X).then_inc(ss_ok, 1)
                    if ahead:
                        gate(n + 1)
                        clip(n + 1)
                        scores(n + 1)

                nc.vector.memset(mxs[:, :], 0.0).then_inc(acc_ok, 1)
                moments_of_stream(0)
                normalise_stream(0)
                low_part_of_stream(0)
                key(0)
                gate(0)
                clip(0)
                scores(0)
                for q in range(QPB):
                    slot(0, q, False, q == 0)
                with dve.Fori(1, B - 1) as b:
                    for q in range(QPB):
                        slot(b, q, False)
                for q in range(QPB):
                    slot(B - 1, q, True)
                low_part_of_output(QPB * B - 1)
                add_output(B - 1, QPB * B - 1)

            @block.tensor
            def _(pe):
                ident = cst["ident"][:, :]
                tri, ones = cst["causal"][:, 0, :], cst["causal"][:, 1, :]

                def turn_stream(b):
                    pe.wait_ge(ln_ok, TT * b + TT)
                    for t in range(TT):
                        for c in range(DC):
                            mm = nc.tensor.transpose(psC[1][:, c * T + t * P:c * T + (t + 1) * P], ln[:, t, c * P:(c + 1) * P], ident)
                    mm.then_inc(ln_ps, 1)

                def wide(name, t, m, q, ready):
                    for c in range(DC):
                        mm = split_matmul(nc, psA[t], [lnTp[:, part, c, t * P:(t + 1) * P] for part in range(2)],
                                          [w[name][part][:, c, q * HQ * DV:(q + 1) * HQ * DV] for part in range(2)],
                                          c == 0, c == DC - 1)
                    mm.then_inc(ready, 1)

                def narrow(name, dst, q, ready):
                    for a in range(NH):
                        col = (q * NH + a) * 2 * DK
                        for c in range(DC):
                            mm = nc.tensor.matmul(dst[:, a * T:(a + 1) * T], w[name][:, c, col:col + 2 * DK], lnT[:, c, :],
                                                  start=(c == 0), stop=(c == DC - 1))
                    mm.then_inc(ready, 1)

                def value_query(b, m, q):
                    pe.wait_ge(lnTl_ok, b + 1)
                    pe.wait_ge(sc_ok, m)
                    wide("v", 0, m, q, v_ps)
                    pe.wait_ge(okn_ok, m)
                    wide("v", 1, m, q, v_ps)
                    pe.wait_ge(v_ok, TT * m + 1)
                    narrow("q", psA[0], q, q_ps)

                def key(m, q):
                    pe.wait_ge(v_ok, TT * m + 2)
                    pe.wait_ge(acc_ok, m)
                    narrow("k", psA[1], q, k_ps)

                def gate_slots(m, q):
                    pe.wait_ge(q_ok, m + 1)
                    wide("g", 0, m, q, g_ps)
                    pe.wait_ge(k_ok, m + 1)
                    wide("g", 1, m, q, g_ps)
                    pe.wait_ge(tg_ok, TT * m + 1)
                    for t in range(TT):
                        for c in range(DC):
                            mm = nc.tensor.matmul(psA[0][:, t * HQ * M:(t + 1) * HQ * M], lnT[:, c, t * P:(t + 1) * P],
                                                  w["s"][:, c, q * HQ * M:(q + 1) * HQ * M], start=(c == 0), stop=(c == DC - 1))
                    mm.then_inc(s_ps, 1)

                def z_sums(m):
                    pe.wait_ge(em_ok, m + 1)
                    pe.wait_ge(rz_ok, m)
                    nc.tensor.matmul(psC[0][:, 0:HQ * M], tri, em[:, 0, :], start=True, stop=True)
                    nc.tensor.matmul(psC[0][:, HQ * M:2 * HQ * M], ones, em[:, 0, :], start=True, stop=False)
                    nc.tensor.matmul(psC[0][:, HQ * M:2 * HQ * M], tri, em[:, 1, :], start=False, stop=True).then_inc(z_ps, 1)

                def causal_scores(lhs, rhs, n, ready, read):
                    for h in range(HQ):
                        a, r = h // 2, (h % 2) * DK
                        read(h)
                        nc.tensor.matmul(psB[h % 2][:, 0:2 * P], lhs[r:r + DK, a, 0:P], rhs[r:r + DK, a, 0:T], start=True, stop=True)
                        nc.tensor.matmul(psB[h % 2][:, 2 * P:3 * P], lhs[r:r + DK, a, P:T], rhs[r:r + DK, a, P:T],
                                         start=True, stop=True).then_inc(ready, 1)

                def over_j(dst, lhs, rhs, width, h):
                    nc.tensor.matmul(dst(0, h), lhs[:, h, 0:P], rhs(0, h), start=True, stop=True)
                    nc.tensor.matmul(dst(1, h), lhs[:, h, P:2 * P], rhs(0, h), start=True, stop=False)
                    return nc.tensor.matmul(dst(1, h), lhs[:, h, 2 * P:3 * P], rhs(1, h), start=False, stop=True)

                def output(n, q):
                    pe.wait_ge(otl_ok, NH * n + NH)
                    for t in range(TT):
                        for h in range(HQ):
                            mm = split_matmul(nc, psA[1][:, t * D:(t + 1) * D], [oT[:, part, h, t * P:(t + 1) * P] for part in range(2)],
                                              [w["o"][part][:, q * HQ + h, :] for part in range(2)], h == 0, h == HQ - 1)
                    mm.then_inc(out_ps, 1)

                def scores(m):
                    pe.wait_ge(q_ok, m + 1)
                    pe.wait_ge(k_ok, m + 1)

                    def b_free_a(h):
                        if h < 2:
                            pe.wait_ge(bt_ok, HQ * m)
                        else:
                            pe.wait_ge(at_ok, HQ * m + h - 1)
                    causal_scores(kT, qT, m, at_ps, b_free_a)

                def slot(b, q, last, first=False):
                    n = QPB * b + q
                    ahead = not (last and q == QPB - 1)
                    bn, qn = (b, q + 1) if q < QPB - 1 else (b + 1, 0)
                    pe.wait_ge(pzt_ok, n)
                    if q == QPB - 1 and not last:
                        turn_stream(b + 1)
                    pe.wait_ge(tg_ok, TT * n + TT)
                    for h in range(HQ):
                        pe.wait_ge(at_ok, HQ * n + h + 1)
                        mm = over_j(lambda t, h: psA[1][:, (t * HQ + h) * M:(t * HQ + h + 1) * M], at,
                                    lambda t, h: em[:, t, h * M:(h + 1) * M], M, h)
                    mm.then_inc(ok_ps, 1)
                    if q == QPB - 1 and not last:
                        pe.wait_ge(lnTh_ok, b + 2)
                    for t in range(TT):
                        for a in range(NH):
                            mm = nc.tensor.transpose(psC[1][:, a * T + t * P:a * T + (t + 1) * P], em[:, t, a * P:(a + 1) * P], ident)
                    mm.then_inc(et_ps, 1)
                    if ahead:
                        value_query(bn, n + 1, qn)
                    if not first:
                        if ahead:
                            pe.wait_ge(v_ok, TT * n + 2 * TT)
                        else:
                            pe.wait_ge(okn_ok, n + 1)
                        output(n - 1, (q - 1) % QPB)
                    pe.wait_ge(pz_ok, n + 1)
                    pe.wait_ge(et_ok, n + 1)
                    for t in range(TT):
                        for a in range(NH):
                            mm = nc.tensor.transpose(psC[1][:, a * T + t * P:a * T + (t + 1) * P], pz[:, t, a * P:(a + 1) * P], ident)
                    mm.then_inc(pzt_ps, 1)
                    if ahead:
                        key(n + 1, qn)
                    pe.wait_ge(pzt_ok, n + 1)

                    def b_free_b(h):
                        pe.wait_ge(at_ok if h < 2 else bt_ok, HQ * n + (4 if h < 2 else h - 1))
                    causal_scores(emT, pzT, n, bt_ps, b_free_b)
                    pe.wait_ge(v_ok, TT * n + TT)
                    pe.wait_ge(otl_ok, NH * n)
                    for h in range(HQ):
                        pe.wait_ge(bt_ok, HQ * n + h + 1)
                        mm = over_j(lambda t, h: psD[:, t, h * DV:(h + 1) * DV], bt,
                                    lambda t, h: v[:, q % 2, t, h * DV:(h + 1) * DV], DV, h)
                    mm.then_inc(ov_ps, 1)
                    if ahead:
                        gate_slots(n + 1, qn)
                        scores(n + 1)
                        z_sums(n + 1)
                    pe.wait_ge(o2_ok, n + 1)
                    for h in range(HQ):
                        for t in range(TT):
                            mm = nc.tensor.transpose(psD[:, h // 2, (h % 2) * T + t * P:(h % 2) * T + (t + 1) * P],
                                                     o2[:, t, h * DV:(h + 1) * DV], ident)
                        if h % 2:
                            mm.then_inc(ot_ps, 1)

                pe.wait_ge(w["here"], 16 * 5)
                turn_stream(0)
                value_query(0, 0, 0)
                key(0, 0)
                gate_slots(0, 0)
                scores(0)
                z_sums(0)
                for q in range(QPB):
                    slot(0, q, False, q == 0)
                with pe.Fori(1, B - 1) as b:
                    for q in range(QPB):
                        slot(b, q, False)
                for q in range(QPB):
                    slot(B - 1, q, True)
                pe.wait_ge(acc_ok, QPB * B)
                output(QPB * B - 1, QPB - 1)
        clear_semaphores(nc, mem)


def turn_matrices(nc, tag, cst, groups):
    NB = 4
    with ExitStack() as ctx:
        mem = Mem(nc, ctx, tag)
        ps = [mem.ps(f"ps{k}", [P, 512]) for k in range(NB)]
        turned, high_ok, left_ps = mem.sem("turned"), mem.sem("high_ok"), mem.sem("left_ps")
        with nc.Block() as block:
            @block.tensor
            def _(pe):
                for k, (high, low, srcs) in enumerate(groups):
                    if k >= NB:
                        pe.wait_ge(left_ps, k - NB + 1)
                    at = 0
                    for src in srcs:
                        rows, cols = src.shape
                        mm = nc.tensor.transpose(ps[k % NB][0:cols, at:at + rows], src, cst["ident"][0:rows, 0:rows])
                        at += rows
                    mm.then_inc(turned, 1)

            @block.scalar
            def _(act):
                for k, (high, low, srcs) in enumerate(groups):
                    if low is not None:
                        act.wait_ge(turned, k + 1)
                        nc.scalar.activation(high, ps[k % NB][0:high.shape[0], 0:high.shape[1]], ACT.Copy).then_inc(high_ok, 1)

            @block.vector
            def _(dve):
                split = 0
                for k, (high, low, srcs) in enumerate(groups):
                    whole = ps[k % NB][0:high.shape[0], 0:high.shape[1]]
                    if low is None:
                        dve.wait_ge(turned, k + 1)
                        nc.vector.tensor_copy(high, whole).then_inc(left_ps, 1)
                    else:
                        split += 1
                        dve.wait_ge(high_ok, split)
                        nc.vector.tensor_tensor(out=low, in0=whole, in1=high, op=ALU.subtract).then_inc(left_ps, 1)
        clear_semaphores(nc, mem)


def ffn_groups(w_gu, w_dn, wgT, wuT, wdT):
    groups = []
    for w, dst in ((w_gu[0], wgT), (w_gu[1], wuT)):
        for c in range(DC):
            for f0 in range(0, FT, 4):
                srcs = [w[0:(P if f < FT - 1 else FLAST), f, c * P:(c + 1) * P] for f in range(f0, min(f0 + 4, FT))]
                end = min((f0 + 4) * P, INTER)
                groups.append((dst[:, 0, c, f0 * P:end], dst[:, 1, c, f0 * P:end], srcs))
    for f in range(FT):
        n = P if f < FT - 1 else FLAST
        groups.append((wdT[0:n, 0, f, :], wdT[0:n, 1, f, :], [w_dn[:, c, f * P:f * P + n] for c in range(DC)]))
    return groups


def hgrn_groups(raw, turned):
    return [(turned[:, k, c, :], None, [raw[:, k, r, c * P:(c + 1) * P] for r in range(DC)])
            for k in range(4) for c in range(DC)]


def split_matmul(nc, out, lhs, rhs, first, last):
    nc.tensor.matmul(out, lhs[0], rhs[0], start=first, stop=False)
    nc.tensor.matmul(out, lhs[0], rhs[1], start=False, stop=False)
    return nc.tensor.matmul(out, lhs[1], rhs[0], start=False, stop=last)


def lut_ffn(nc, cst, tag, sources, x_out, wgT, wuT, wdT):
    G = 4
    NU = NTILE // G
    with ExitStack() as ctx:
        mem = Mem(nc, ctx, tag)
        two = len(sources) == 2
        xt = mem.sb("xt", [P, 2, G, D])
        xb = mem.sb("xb", [P, G, D])
        res = mem.sb("res", [P, 2, G, D])
        bs = mem.sb("bs", [P, G, 6])
        mv = mem.sb("mv", [P, G, 2])
        ve = mem.sb("ve", [P, G])
        rstd = mem.sb("rstd", [P, G])
        ln = mem.sb("ln", [P, G, D])
        lnT = mem.sb("lnT", [P, 2, 2, DC, G * P], F32R)
        sil = mem.sb("sil", [P, 2, G * P])
        hs = mem.sb("hs", [P, 2, G * P])
        hT = mem.sb("hT", [P, 2, 2, FT, G * P], F32R)
        y = mem.sb("y", [P, G, D])
        psT = [mem.ps(f"psT{c}", [P, G * P]) for c in range(DC)]
        psG = [mem.ps(f"psG{k}", [P, G * P]) for k in range(2)]
        psU = [mem.ps(f"psU{k}", [P, G * P]) for k in range(2)]
        psY = [mem.ps(f"psY{k}", [P, 2 * D]) for k in range(2)]
        names = ("x_here added res_ok stats moments shifted rstd_ok ln_ok ln_ps lnT_hi lnT_lo gate_ps up_ps sil_ok h_ok "
                 "h_hi h_lo down_ps y_ok y_out")
        (x_here, added, res_ok, stats, moments, shifted, rstd_ok, ln_ok, ln_ps, lnT_hi, lnT_lo, gate_ps, up_ps, sil_ok,
         h_ok, h_hi, h_lo, down_ps, y_ok, y_out) = (mem.sem(n) for n in names.split())
        sv = [s[0:NTOK, :].rearrange("(m g p) d -> m p g d", g=G, p=P) for s in sources]
        yv = x_out.rearrange("(m g p) d -> m p g d", g=G, p=P)

        def rows_of(f):
            return P if f < FT - 1 else FLAST

        def units(engine, body):
            body(0, 0, True, False)
            body(1, 1, True, True)
            with engine.Fori(1, NU // 2 - 1) as i:
                for u in range(2):
                    body(2 * i + u, u, True, True)
            body(NU - 2, 0, True, True)
            body(NU - 1, 1, False, True)

        with nc.Block() as block:
            @block.sync
            def _(sp):
                def load(m, u):
                    if two:
                        sp.dma_start(xb[:, :, :], sv[1][m]).then_inc(x_here, 16)
                    sp.dma_start(xt[:, u, :, :], sv[0][m]).then_inc(x_here, 16)

                def store(m):
                    sp.wait_ge(y_ok, 2 * m + 2)
                    hold(sp)
                    sp.dma_start(yv[m], y[:, :, :]).then_inc(y_out, 16)

                def unit(m, u, ahead, behind):
                    if ahead:
                        sp.wait_ge(moments, G * m + G)
                        hold(sp)
                        sp.wait_ge(res_ok, m + 1)
                        hold(sp)
                        sp.wait_ge(ln_ok, G * m)
                        hold(sp)
                        load(m + 1, 1 - u)
                    if behind:
                        store(m - 1)
                load(0, 0)
                units(sp, unit)
                store(NU - 1)
                sp.wait_ge(y_out, 16 * NU)

            @block.gpsimd
            def _(pool):
                def norm(m, u, used):
                    if two:
                        pool.wait_ge(x_here, 32 * m + 32)
                        nc.gpsimd.tensor_tensor(out=xt[:, u, :, :], in0=xt[:, u, :, :], in1=xb[:, :, :], op=ALU.add).then_inc(added, 1)
                    pool.wait_ge(moments, G * m + G)
                    hold(pool)
                    nc.gpsimd.tensor_scalar(ve[:, :], mv[:, :, 1], EPS, None, ALU.add).then_inc(shifted, 1)
                    pool.wait_ge(shifted, m + 1)
                    nc.gpsimd.tensor_tensor(out=rstd[:, :], in0=ve[:, :], in1=cst["minus_half"][:, 0:G], op=ALU.pow).then_inc(rstd_ok, 1)
                    if used:
                        pool.wait_ge(y_ok, 2 * m - 2)
                        hold(pool)
                    nc.gpsimd.tensor_copy(res[:, u, :, :], xt[:, u, :, :]).then_inc(res_ok, 1)

                def unit(m, u, ahead, behind):
                    if ahead:
                        norm(m + 1, 1 - u, behind)
                norm(0, 0, False)
                units(pool, unit)

            @block.scalar
            def _(act):
                def turn(m, u):
                    act.wait_ge(ln_ps, m + 1)
                    for c in range(DC):
                        nc.scalar.activation(lnT[:, u, 0, c, :], psT[c], ACT.Copy).then_inc(lnT_hi, 1)

                def high(m, u, f):
                    act.wait_ge(h_ok, FT * m + f + 1)
                    nc.scalar.activation(hT[0:rows_of(f), u, 0, f, :], hs[0:rows_of(f), f % 2, :], ACT.Copy).then_inc(h_hi, 1)

                def unit(m, u, ahead, behind):
                    for f in range(FT):
                        act.wait_ge(gate_ps, FT * m + f + 1)
                        nc.scalar.activation(sil[0:rows_of(f), f % 2, :], psG[f % 2][0:rows_of(f), :], ACT.Silu).then_inc(sil_ok, 1)
                        if f == 0 and behind:
                            act.wait_ge(down_ps, 2 * m - 2)
                        if f > 0:
                            high(m, u, f - 1)
                        if f == 4 and ahead:
                            turn(m + 1, 1 - u)
                    high(m, u, FT - 1)
                turn(0, 0)
                units(act, unit)

            @block.vector
            def _(dve):
                def moments_of(m, u):
                    if two:
                        dve.wait_ge(added, m + 1)
                    else:
                        dve.wait_ge(x_here, 16 * m + 16)
                    for g in range(G):
                        nc.vector.bn_stats(bs[:, g, :], xt[:, u, g, :]).then_inc(stats, 1)
                    dve.wait_ge(stats, G * m + G)
                    hold(dve)
                    for g in range(G):
                        nc.vector.bn_aggr(mv[:, g, :], bs[:, g, :]).then_inc(moments, 1)

                def normalise(m, u):
                    dve.wait_ge(rstd_ok, m + 1)
                    dve.wait_ge(ln_ps, m)
                    for g in range(G):
                        nc.vector.tensor_scalar(ln[:, g, :], xt[:, u, g, :], mv[:, g, 0:1], rstd[:, g:g + 1],
                                                ALU.subtract, ALU.mult).then_inc(ln_ok, 1)

                def turn(m, u):
                    for c in range(DC):
                        dve.wait_ge(lnT_hi, DC * m + c + 1)
                        nc.vector.tensor_tensor(out=lnT[:, u, 1, c, :], in0=psT[c], in1=lnT[:, u, 0, c, :], op=ALU.subtract).then_inc(lnT_lo, 1)

                def low(m, u, f):
                    dve.wait_ge(h_hi, FT * m + f + 1)
                    n = rows_of(f)
                    nc.vector.tensor_tensor(out=hT[0:n, u, 1, f, :], in0=hs[0:n, f % 2, :], in1=hT[0:n, u, 0, f, :],
                                            op=ALU.subtract).then_inc(h_lo, 1)

                def output(m, u):
                    dve.wait_ge(y_out, 16 * m)
                    dve.wait_ge(res_ok, m + 1)
                    for k in range(2):
                        dve.wait_ge(down_ps, 2 * m + k + 1)
                        nc.vector.scalar_tensor_tensor(out=y[:, 2 * k:2 * k + 2, :].rearrange("p g d -> p (g d)"), in0=psY[k], scalar=0.5,
                                                       in1=res[:, u, 2 * k:2 * k + 2, :].rearrange("p g d -> p (g d)"),
                                                       op0=ALU.mult, op1=ALU.add).then_inc(y_ok, 1)

                def unit(m, u, ahead, behind):
                    for f in range(FT):
                        n = rows_of(f)
                        dve.wait_ge(up_ps, FT * m + f + 1)
                        dve.wait_ge(sil_ok, FT * m + f + 1)
                        if behind or f > 1:
                            dve.wait_ge(h_lo, FT * m + f - 1)
                        nc.vector.tensor_tensor(out=hs[0:n, f % 2, :], in0=psU[f % 2][0:n, :], in1=sil[0:n, f % 2, :],
                                                op=ALU.mult).then_inc(h_ok, 1)
                        if f > 0:
                            low(m, u, f - 1)
                        if f == 0 and ahead:
                            moments_of(m + 1, 1 - u)
                        if f == 2 and ahead:
                            normalise(m + 1, 1 - u)
                        if f == 3 and behind:
                            output(m - 1, 1 - u)
                        if f == 4 and ahead:
                            turn(m + 1, 1 - u)
                    low(m, u, FT - 1)
                moments_of(0, 0)
                normalise(0, 0)
                turn(0, 0)
                units(dve, unit)
                output(NU - 1, 1)

            @block.tensor
            def _(pe):
                def turn(m):
                    pe.wait_ge(ln_ok, G * m + G)
                    pe.wait_ge(lnT_lo, DC * m)
                    for c in range(DC):
                        for g in range(G):
                            mm = nc.tensor.transpose(psT[c][:, g * P:(g + 1) * P], ln[:, g, c * P:(c + 1) * P], cst["ident"][:, :])
                    mm.then_inc(ln_ps, 1)

                def down(m, u):
                    pe.wait_ge(h_lo, FT * m + FT)
                    pe.wait_ge(y_ok, 2 * m)
                    for k in range(2):
                        for g in (2 * k, 2 * k + 1):
                            for f in range(FT):
                                n = rows_of(f)
                                mm = split_matmul(nc, psY[k][:, (g % 2) * D:(g % 2 + 1) * D],
                                                  [hT[0:n, u, part, f, g * P:(g + 1) * P] for part in range(2)],
                                                  [wdT[0:n, part, f, :] for part in range(2)], f == 0, f == FT - 1)
                        mm.then_inc(down_ps, 1)

                def unit(m, u, ahead, behind):
                    pe.wait_ge(lnT_lo, DC * m + DC)
                    for f in range(FT):
                        n = rows_of(f)
                        if behind or f > 1:
                            pe.wait_ge(h_ok, FT * m + f - 1)
                        for w, ps, ready in ((wgT, psG, gate_ps), (wuT, psU, up_ps)):
                            for c in range(DC):
                                mm = split_matmul(nc, ps[f % 2][0:n, :], [w[:, part, c, f * P:f * P + n] for part in range(2)],
                                                  [lnT[:, u, part, c, :] for part in range(2)], c == 0, c == DC - 1)
                            mm.then_inc(ready, 1)
                        if f == 1 and behind:
                            down(m - 1, 1 - u)
                        if f == 3 and ahead:
                            turn(m + 1)
                turn(0)
                units(pe, unit)
                down(NU - 1, 1)
        clear_semaphores(nc, mem)


def hgrn(nc, cst, tag, x_in, x_out, wT, norm_w):
    R = 4
    TT = T // P
    with ExitStack() as ctx:
        mem = Mem(nc, ctx, tag)
        xt = mem.sb("xt", [P, R, TT, D])
        nw = mem.sb("nw", [P, DC])
        nwh = mem.sb("nwh", [P, DC])
        bs = mem.sb("bs", [P, TT, 6])
        mv = mem.sb("mv", [P, TT, 2])
        ve = mem.sb("ve", [P, TT])
        rstd = mem.sb("rstd", [P, TT])
        ln = mem.sb("ln", [P, TT, D])
        lnT = mem.sb("lnT", [P, DC, T])
        ti, tf, tg, ai, ag, gate, rest, val, o, osq, pT = (
            mem.sb(n, [P, DC, T]) for n in "ti tf tg ai ag gate rest val o osq pT".split())
        ms = mem.sb("ms", [P, TT])
        orstd = mem.sb("orstd", [P, TT])
        y = mem.sb("y", [P, 2, TT, D])
        psI = mem.ps("psI", [P, DC * T])
        psF = mem.ps("psF", [P, DC * T])
        psG = mem.ps("psG", [P, DC * T])
        psI2 = mem.ps("psI2", [P, DC * T])
        psG2 = mem.ps("psG2", [P, DC * T])
        psT = mem.ps("psT", [P, DC * T])
        psS = mem.ps("psS", [P, TT])
        psY = mem.ps("psY", [P, TT * D])
        I, Gt = [psI, psI2], [psG, psG2]
        names = ("nw_here nw_ok stats moments shifted rstd_ok ln_ok ln_ps lnT_ok i_ps f_ps g_ps ti_ok tf_ok tg_ok "
                 "ai_ok ag_ok gate_ok rest_ok val_ok o_ok osq_ok ss_ps ms_ok orstd_ok pT_ok y_ps y_ok y_out")
        (nw_here, nw_ok, stats, moments, shifted, rstd_ok, ln_ok, ln_ps, lnT_ok, i_ps, f_ps, g_ps, ti_ok, tf_ok,
         tg_ok, ai_ok, ag_ok, gate_ok, rest_ok, val_ok, o_ok, osq_ok, ss_ps, ms_ok, orstd_ok, pT_ok, y_ps, y_ok, y_out) = (
            mem.sem(n) for n in names.split())
        x_here = mem.sem2("x_of_parity")
        xv = x_in.rearrange("(b t p) d -> b p t d", t=TT, p=P)
        yv = x_out.rearrange("(b t p) d -> b p t d", t=TT, p=P)

        def flat(a):
            return a.rearrange("p c t -> p (c t)")

        def slots(engine, body):
            for k in range(R):
                body(k, k, True, True)
            with engine.Fori(1, B // R - 1) as i:
                for k in range(R):
                    body(R * i + k, k, True, True)
            for k in range(R):
                body(B - R + k, k, k < R - 1, k < R - 2)

        with nc.Block() as block:
            @block.sync
            def _(sp):
                def load(b, k):
                    sp.dma_start(xt[:, k, :, :], xv[b]).then_inc(x_here[k % 2], 16)

                def slot(b, k, ahead, ahead2):
                    if ahead2:
                        sp.wait_ge(y_ok, 2 * b)
                        hold(sp)
                        sp.wait_ge(moments, TT * b + TT)
                        hold(sp)
                        load(b + 2, (k + 2) % R)
                    sp.wait_ge(y_ok, 2 * b + 2)
                    hold(sp)
                    sp.dma_start(yv[b], y[:, k % 2, :, :]).then_inc(y_out, 16)
                load(0, 0)
                load(1, 1)
                with nc.allow_non_contiguous_dma(reason="256 words, once"):
                    sp.dma_start(nw[:, :], norm_w.rearrange("(c p) -> p c", p=P)).then_inc(nw_here, 16)
                slots(sp, slot)
                sp.wait_ge(y_out, 16 * B)

            @block.gpsimd
            def _(pool):
                def norm(b):
                    pool.wait_ge(moments, TT * b + TT)
                    hold(pool)
                    nc.gpsimd.tensor_scalar(ve[:, :], mv[:, :, 1], EPS, None, ALU.add).then_inc(shifted, 1)
                    pool.wait_ge(shifted, b + 1)
                    nc.gpsimd.tensor_tensor(out=rstd[:, :], in0=ve[:, :], in1=cst["minus_half"][:, 0:TT], op=ALU.pow).then_inc(rstd_ok, 1)

                def slot(b, k, ahead, ahead2):
                    pool.wait_ge(tf_ok, b + 1)
                    pool.wait_ge(o_ok, DC * b)
                    hold(pool)
                    nc.gpsimd.tensor_scalar(gate[:, :, :], tf[:, :, :], 0.5, 0.5, ALU.mult, ALU.add).then_inc(gate_ok, 1)
                    nc.gpsimd.tensor_scalar(rest[:, :, :], tf[:, :, :], -0.25, 0.25, ALU.mult, ALU.add).then_inc(rest_ok, 1)
                    pool.wait_ge(rest_ok, b + 1)
                    pool.wait_ge(ai_ok, b + 1)
                    nc.gpsimd.tensor_tensor(out=val[:, :, :], in0=ai[:, :, :], in1=rest[:, :, :], op=ALU.mult).then_inc(val_ok, 1)
                    if ahead2:
                        norm(b + 2)
                    pool.wait_ge(ms_ok, b + 1)
                    nc.gpsimd.tensor_tensor(out=orstd[:, :], in0=ms[:, :], in1=cst["minus_half"][:, 0:TT], op=ALU.pow).then_inc(orstd_ok, 1)
                pool.wait_ge(nw_here, 16)
                hold(pool)
                nc.gpsimd.tensor_scalar(nwh[:, :], nw[:, :], 0.5, None, ALU.mult).then_inc(nw_ok, 1)
                norm(0)
                norm(1)
                slots(pool, slot)

            @block.scalar
            def _(act):
                def turn(b):
                    act.wait_ge(ln_ps, b + 1)
                    nc.scalar.activation(flat(lnT[:, :, :]), psT, ACT.Copy).then_inc(lnT_ok, 1)

                def tanhs(b, par):
                    act.wait_ge(rest_ok, b)
                    act.wait_ge(ag_ok, b)
                    for ps, dst, ready, done in ((psF, tf, f_ps, tf_ok), (I[par], ti, i_ps, ti_ok), (Gt[par], tg, g_ps, tg_ok)):
                        act.wait_ge(ready, b + 1)
                        nc.scalar.activation(flat(dst[:, :, :]), ps, ACT.Tanh, scale=0.5).then_inc(done, 1)

                def slot(b, k, ahead, ahead2):
                    act.wait_ge(o_ok, DC * b + DC)
                    nc.scalar.activation(osq[:, :, :], o[:, :, :], ACT.Square).then_inc(osq_ok, 1)
                    if ahead:
                        tanhs(b + 1, (k + 1) % 2)
                    if ahead2:
                        turn(b + 2)
                turn(0)
                tanhs(0, 0)
                turn(1)
                slots(act, slot)

            @block.vector
            def _(dve):
                def moments_of(b, k):
                    dve.wait_ge(x_here[k % 2], 8 * (b - k % 2) + 16)
                    for t in range(TT):
                        nc.vector.bn_stats(bs[:, t, :], xt[:, k, t, :]).then_inc(stats, 1)
                    dve.wait_ge(stats, TT * b + TT)
                    hold(dve)
                    for t in range(TT):
                        nc.vector.bn_aggr(mv[:, t, :], bs[:, t, :]).then_inc(moments, 1)

                def normalise(b, k):
                    dve.wait_ge(rstd_ok, b + 1)
                    dve.wait_ge(ln_ps, b)
                    for t in range(TT):
                        nc.vector.tensor_scalar(ln[:, t, :], xt[:, k, t, :], mv[:, t, 0:1], rstd[:, t:t + 1],
                                                ALU.subtract, ALU.mult).then_inc(ln_ok, 1)

                def slot(b, k, ahead, ahead2):
                    dve.wait_ge(ti_ok, b + 1)
                    dve.wait_ge(val_ok, b)
                    nc.vector.scalar_tensor_tensor(out=flat(ai[:, :, :]), in0=flat(ti[:, :, :]), scalar=1.0, in1=I[k % 2],
                                                   op0=ALU.add, op1=ALU.mult).then_inc(ai_ok, 1)
                    dve.wait_ge(tg_ok, b + 1)
                    dve.wait_ge(pT_ok, DC * b)
                    nc.vector.scalar_tensor_tensor(out=flat(ag[:, :, :]), in0=flat(tg[:, :, :]), scalar=1.0, in1=Gt[k % 2],
                                                   op0=ALU.add, op1=ALU.mult).then_inc(ag_ok, 1)
                    dve.wait_ge(gate_ok, b + 1)
                    dve.wait_ge(val_ok, b + 1)
                    dve.wait_ge(osq_ok, b)
                    for c in range(DC):
                        nc.vector.tensor_tensor_scan(o[:, c, :], gate[:, c, :], val[:, c, :], 0.0, ALU.mult, ALU.add).then_inc(o_ok, 1)
                    dve.wait_ge(o_ok, DC * b + DC)
                    dve.wait_ge(y_ps, b)
                    for c in range(DC):
                        nc.vector.scalar_tensor_tensor(out=pT[:, c, :], in0=ag[:, c, :], scalar=nwh[:, c:c + 1], in1=o[:, c, :],
                                                       op0=ALU.mult, op1=ALU.mult).then_inc(pT_ok, 1)
                    if ahead2:
                        moments_of(b + 2, (k + 2) % R)
                    dve.wait_ge(ss_ps, b + 1)
                    nc.vector.tensor_scalar(ms[:, :], psS, 1.0 / D, EPS, ALU.mult, ALU.add).then_inc(ms_ok, 1)
                    if ahead2:
                        normalise(b + 2, (k + 2) % R)
                    dve.wait_ge(orstd_ok, b + 1)
                    dve.wait_ge(y_ps, b + 1)
                    dve.wait_ge(y_out, 16 * b)
                    for t in range(TT):
                        nc.vector.scalar_tensor_tensor(out=y[:, k % 2, t, :], in0=psY[:, t * D:(t + 1) * D], scalar=orstd[:, t:t + 1],
                                                       in1=xt[:, k, t, :], op0=ALU.mult, op1=ALU.add).then_inc(y_ok, 1)
                for b in range(2):
                    moments_of(b, b)
                    normalise(b, b)
                dve.wait_ge(nw_ok, 1)
                slots(dve, slot)

            @block.tensor
            def _(pe):
                def turn(b):
                    pe.wait_ge(ln_ok, TT * b + TT)
                    pe.wait_ge(lnT_ok, b)
                    for c in range(DC):
                        for t in range(TT):
                            mm = nc.tensor.transpose(psT[:, c * T + t * P:c * T + (t + 1) * P], ln[:, t, c * P:(c + 1) * P], cst["ident"][:, :])
                    mm.then_inc(ln_ps, 1)

                def project(b, par):
                    pe.wait_ge(lnT_ok, b + 1)
                    pe.wait_ge(tf_ok, b)
                    for k, ps, ready in ((1, psF, f_ps), (0, I[par], i_ps), (2, Gt[par], g_ps)):
                        if k == 0:
                            pe.wait_ge(ai_ok, b if par else b)
                        for f in range(DC):
                            for c in range(DC):
                                mm = nc.tensor.matmul(ps[:, f * T:(f + 1) * T], wT[:, k, c, f * P:(f + 1) * P], lnT[:, c, :],
                                                      start=(c == 0), stop=(c == DC - 1))
                        mm.then_inc(ready, 1)

                def slot(b, k, ahead, ahead2):
                    if ahead:
                        project(b + 1, (k + 1) % 2)
                    pe.wait_ge(osq_ok, b + 1)
                    pe.wait_ge(ms_ok, b)
                    for t in range(TT):
                        for c in range(DC):
                            mm = nc.tensor.matmul(psS[:, t:t + 1], osq[:, c, t * P:(t + 1) * P], cst["causal"][:, 1, 0:1],
                                                  start=(c == 0), stop=(c == DC - 1))
                    mm.then_inc(ss_ps, 1)
                    pe.wait_ge(pT_ok, DC * b + DC)
                    pe.wait_ge(y_ok, 2 * b)
                    for t in range(TT):
                        for c in range(DC):
                            mm = nc.tensor.matmul(psY[:, t * D:(t + 1) * D], pT[:, c, t * P:(t + 1) * P], wT[:, 3, c, :],
                                                  start=(c == 0), stop=(c == DC - 1))
                    mm.then_inc(y_ps, 1)
                    if ahead2:
                        turn(b + 2)
                turn(0)
                project(0, 0)
                turn(1)
                slots(pe, slot)
        clear_semaphores(nc, mem)


def macaron(nc, x, Wq, Wk, Wv, Wg, Ws, Wo, g_norm, gate_w, w_gate, w_up, w_down,
            Wi1, Wf1, Wg1, Wo1, gnorm1, lut, gate_idx, up_idx, down_idx, out):
    rows = nc.dram_tensor("rows", [NTOK + P, ROW], F32, kind="Internal").ap()
    stream_a = nc.dram_tensor("stream_a", [NTOK + P, D], F32, kind="Internal").ap()
    stream_b = nc.dram_tensor("stream_b", [NTOK + P, D], F32, kind="Internal").ap()
    x_att = nc.dram_tensor("x_att", [NTOK, D], F32, kind="Internal").ap()
    x_ffn = nc.dram_tensor("x_ffn", [NTOK, D], F32, kind="Internal").ap()
    x_hgrn = nc.dram_tensor("x_hgrn", [NTOK, D], F32, kind="Internal").ap()
    looked_up = [nc.dram_tensor(f"looked_up{k}", idx.shape, F32, kind="Internal").ap()
                 for k, idx in enumerate((gate_idx, up_idx, down_idx))]
    with ExitStack() as ctx:
        mem = Mem(nc, ctx)
        slot_tok = mem.sb("slot_tok", [P, E], U32)
        pool_dma = [mem.sem(f"got{k}") for k in range(4)], mem.sem2("added")
        cst = constants(nc, mem)
        with ExitStack() as inner:
            wmem = Mem(nc, inner)
            w = attention_weights(nc, wmem, Wq, Wk, Ws, g_norm, lut)
            moe_router(nc, cst, "r1_", x, gate_w, rows, stream_a, stream_b, slot_tok)
            wide = [wmem.sb(f"wide_{part}", [P, 3, WIDE], F32R) for part in ("high", "low")]
            wide_src = [Wv.rearrange("(c p) n -> p c n", p=P), Wg.rearrange("(c p) n -> p c n", p=P),
                        Wo.rearrange("(h v) d -> v h d", v=DV)]
            moe_experts(nc, cst, "e1_", rows, w_gate, w_up, w_down, slot_tok, stream_a, stream_b, pool_dma, 0,
                        (wide_src, wide[0], wide[1]))
            w["v"], w["g"] = ([part[:, k, :].rearrange("p (c n) -> p c n", c=DC) for part in wide] for k in range(2))
            w["o"] = [part[:, 2, :].rearrange("p (h d) -> p h d", h=H) for part in wide]
            attention(nc, cst, w, "a_", stream_a, stream_b, x_att, (gate_idx, up_idx, down_idx), looked_up)
            clear_semaphores(nc, wmem)
        moe_router(nc, cst, "r2_", x_att, gate_w, rows, stream_a, stream_b, slot_tok)
        moe_experts(nc, cst, "e2_", rows, w_gate, w_up, w_down, slot_tok, stream_a, stream_b, pool_dma, 1)
        w_gu = [mem.sb(f"w_gu{k}", [P, FT, D]) for k in range(2)]
        w_dn = mem.sb("w_down", [P, DC, INTER])
        wgT = mem.sb("wgT", [P, 2, DC, INTER], F32R)
        wuT = mem.sb("wuT", [P, 2, DC, INTER], F32R)
        wdT = mem.sb("wdT", [P, 2, FT, D], F32R)
        h_raw = mem.sb("h_raw", [P, 4, DC, D])
        h_T = mem.sb("h_T", [P, 4, DC, D])
        h_here = mem.sem("h_here")
        with nc.Block() as block:
            @block.sync
            def _(sp):
                for k, src in enumerate((Wi1, Wf1, Wg1, Wo1)):
                    sp.dma_start(h_raw[:, k, :, :], src.rearrange("(r p) n -> p r n", p=P)).then_inc(h_here, 16)
                for k in range(2):
                    sp.dma_start(w_gu[k][:, 0:FT - 1, :], looked_up[k][0:(FT - 1) * P, :].rearrange("(f p) d -> p f d", p=P)).then_inc(h_here, 16)
                    sp.dma_start(w_gu[k][0:FLAST, FT - 1, :], looked_up[k][(FT - 1) * P:INTER, :]).then_inc(h_here, 16)
                sp.dma_start(w_dn[:, :, :], looked_up[2].rearrange("(c p) o -> p c o", p=P)).then_inc(h_here, 16)
                sp.wait_ge(h_here, 16 * 9)
        turn_matrices(nc, "t_", cst, ffn_groups(w_gu, w_dn, wgT, wuT, wdT) + hgrn_groups(h_raw, h_T))
        lut_ffn(nc, cst, "f1_", [stream_a, stream_b], x_ffn, wgT, wuT, wdT)
        hgrn(nc, cst, "h_", x_ffn, x_hgrn, h_T, gnorm1)
        lut_ffn(nc, cst, "f2_", [x_hgrn], out, wgT, wuT, wdT)


_INS = ['L0_attn_hidden_states', 'L0_attn_Wq', 'L0_attn_Wk', 'L0_attn_Wv', 'L0_attn_Wg', 'L0_attn_Ws', 'L0_attn_Wo',
        'L0_attn_g_norm_weight', 'L0_ffn_gate_w', 'L0_ffn_w_gate', 'L0_ffn_w_up', 'L0_ffn_w_down',
        'L1_attn_Wi', 'L1_attn_Wf', 'L1_attn_Wg', 'L1_attn_Wo', 'L1_attn_gnorm_w',
        'L1_ffn_lut', 'L1_ffn_gate_idx', 'L1_ffn_up_idx', 'L1_ffn_down_idx']


def kernel(**inputs):
    import numpy as _np
    import concourse.bacc as _bacc
    from concourse import mybir as _mybir
    from concourse.bass_utils import run_bass_kernel_spmd as _run

    nc = _bacc.Bacc("TRN2", target_bir_lowering=False, num_devices=1)
    arrays, args = {}, []
    for name in _INS:
        a = _np.ascontiguousarray(inputs[name])
        if name == 'L0_attn_hidden_states':
            a = a.reshape(NTOK, D)
        arrays[f"in_{name}"] = a
        args.append(nc.dram_tensor(f"in_{name}", a.shape, _mybir.dt.from_np(a.dtype), kind="ExternalInput").ap())
    out = nc.dram_tensor("out_stream", (NTOK, D), _mybir.dt.float32, kind="ExternalOutput").ap()
    macaron(nc, *args, out)
    r = _run(nc, [arrays], core_ids=[0])
    return r.results[0]["out_stream"].reshape(B, T, D)
```

```python
from contextlib import ExitStack

import concourse.bass as bass
from concourse import mybir

F32 = mybir.dt.float32
F32R = mybir.dt.float32r
U32 = mybir.dt.uint32
I32 = mybir.dt.int32
ALU = mybir.AluOpType
ACT = mybir.ActivationFunctionType
AX = mybir.AxisListType

P = 128
D = 256
DC = D // P
B, T = 16, 256
NTOK = B * T
NTILE = NTOK // P
E, F, CAP = 64, 128, 128
H, DK, DV, M = 16, 64, 128, 64
INTER = 688
NLUT = 16
FT = -(-INTER // P)
FLAST = INTER - (FT - 1) * P
WIDE = DC * H * DV
LCOL = INTER * D // (P * B)
EPS = 1e-5
ROW = D + E


class Mem:

    def __init__(self, nc, ctx, tag=""):
        self.nc, self.ctx, self.tag = nc, ctx, tag
        self.sems = []

    def sb(self, name, shape, dt=F32):
        return self.ctx.enter_context(self.nc.sbuf_tensor(self.tag + name, shape, dt))

    def ps(self, name, shape):
        size = 1
        for n in shape[1:]:
            size *= n
        whole = self.ctx.enter_context(self.nc.psum_tensor(self.tag + name, [P, -(-size // 512) * 512], F32))
        part = whole[0:shape[0], 0:size]
        return part.rearrange("p (a b) -> p a b", b=shape[2]) if len(shape) == 3 else part

    def sem(self, name):
        self.sems.append(self.ctx.enter_context(self.nc.semaphore(self.tag + name)))
        return self.sems[-1]

    def sem2(self, name):
        return [self.sem(name + "0"), self.sem(name + "1")]


def clear_semaphores(nc, mem):
    with nc.Block() as block:
        @block.gpsimd
        def _(pool):
            for s in mem.sems:
                pool.sem_clear(s)


def hold(engine):
    engine.nop(nofuse=True)


def flat_rows(matrix):
    return matrix.rearrange("a b -> (a b)").rearrange("(p c) -> p c", p=P)


def constants(nc, mem):
    c = {
        "ident": mem.sb("ident", [P, P]),
        "causal": mem.sb("causal", [P, 3, P]),
        "minus_half": mem.sb("minus_half", [P, 8]),
    }
    s_set, s_cut = mem.sem("c_set"), mem.sem("c_cut")
    with nc.Block() as block:
        @block.gpsimd
        def _(pool):
            nc.gpsimd.memset(c["ident"][:, :], 0.0).then_inc(s_set, 1)
            nc.gpsimd.memset(c["causal"][:, :, :], 1.0).then_inc(s_set, 1)
            nc.gpsimd.memset(c["minus_half"][:, :], -0.5).then_inc(s_set, 1)
            pool.wait_ge(s_set, 3)
            nc.gpsimd.affine_select(out=c["ident"][:, :], in_=c["ident"][:, :], compare_op=ALU.not_equal,
                                    fill=1.0, base=0, pattern=[[-1, P]], channel_multiplier=1).then_inc(s_cut, 1)
            for blk in (0, 2):
                nc.gpsimd.affine_select(out=c["causal"][:, blk, :], in_=c["causal"][:, blk, :],
                                        compare_op=ALU.is_ge, fill=0.0, base=0, pattern=[[1, P]],
                                        channel_multiplier=-1).then_inc(s_cut, 1)
            pool.wait_ge(s_cut, 3)
    return c


def moe_router(nc, cst, tag, x_src, gate_w, rows, stream_a, stream_b, slot_tok):
    HALF = NTILE // 2
    NZ = 11
    NI = HALF // 4
    with ExitStack() as ctx:
        mem = Mem(nc, ctx, tag)
        gw_in = mem.sb("gw_in", [E, D])
        gwT = mem.sb("gwT", [P, DC, E])
        zeros = mem.sb("zeros", [P, (NTOK // P + 1) * D // NZ])
        xt = mem.sb("xt", [P, 2, 2, 2, D])
        bs = mem.sb("bs", [P, 2, 2, 6])
        mv = mem.sb("mv", [P, 2, 2, 2])
        ve = mem.sb("ve", [P, 2, 2])
        rstd = mem.sb("rstd", [P, 2, 2])
        row = mem.sb("row", [P, 2, 2, 2, ROW])
        lnT = mem.sb("lnT", [P, 2, DC, 2 * P])
        lg = mem.sb("lg", [P, 2, 2, E])
        mx = mem.sb("mx", [P, 2, 2, 8])
        nm = mem.sb("nm", [P, 2, 2])
        left = mem.sb("left", [P, 2, 2, E])
        chosen = mem.sb("chosen", [P, 2, 2, E])
        ex = mem.sb("ex", [P, 2, 2, E])
        den = mem.sb("den", [P, 2, 2])
        rden = mem.sb("rden", [P, 2, 2])
        desc = mem.sb("desc", [P, HALF * P], I32)
        key = mem.sb("key", [P, HALF * P])
        cand = mem.sb("cand", [P, CAP])
        both = mem.sb("both", [E, 2, CAP])
        best = mem.sb("best", [E, CAP])
        slot_i = mem.sb("slot_i", [P, 1], I32)
        slot_n = mem.sb("slot_n", [P, 1])
        pad = mem.sb("pad", [P, E])
        tok = mem.sb("tok", [P, E])
        psT = [mem.ps(f"psT{u}", [P, DC, 2 * P]) for u in range(2)]
        psL = [mem.ps(f"psL{u}", [P, 2, E]) for u in range(2)]
        psM = [mem.ps(f"psM{u}", [P, P]) for u in range(2)]
        psG = mem.ps("psG", [P, DC, E])

        gw_here, gw_turned, gw_ready = mem.sem("gw_here"), mem.sem("gw_turned"), mem.sem("gw_ready")
        zero_set, zero_out, desc_set = mem.sem("zero_set"), mem.sem("zero_out"), mem.sem("desc_set")
        x_here, x_kept, row_out = ([mem.sem2(f"{n}{p}_") for p in range(2)] for n in ("x_here", "x_kept", "row_out"))
        stats, moments, shifted, rstd_ok = (mem.sem2(n) for n in ("stats", "moments", "shifted", "rstd_ok"))
        normed, turned, lnT_ok, logits, lg_ok = (mem.sem2(n) for n in ("normed", "turned", "lnT_ok", "logits", "lg_ok"))
        top, cut, nm_ok, chosen_ok, exps, rden_ok, weights = (
            mem.sem2(n) for n in ("top", "cut", "nm_ok", "chosen_ok", "exps", "rden_ok", "weights"))
        maskT, keyed = mem.sem2("maskT"), mem.sem2("keyed")
        found, struck, moved, found2, struck2 = (mem.sem(n) for n in ("found", "struck", "moved", "found2", "struck2"))
        bestT, padded, tokened, tabled = (mem.sem(n) for n in ("bestT", "padded", "tokened", "tabled"))

        xv = x_src.rearrange("(h j p) d -> j p h d", h=2, p=P)
        av = stream_a[0:NTOK, :].rearrange("(h j p) d -> j p h d", h=2, p=P)
        rv = rows[0:NTOK, :].rearrange("(h j p) d -> j p h d", h=2, p=P)

        def pairs(engine, body):
            for p in range(2):
                body(0, p, True)
            with engine.Fori(1, NI - 1) as i:
                for p in range(2):
                    body(i, p, True)
            for p in range(2):
                body(NI - 1, p, p == 0)

        with nc.Block() as block:
            @block.sync
            def _(sp):
                sp.dma_start(gw_in[:, :], gate_w).then_inc(gw_here, 16)
                def load(i, p, ahead):
                    j = 2 * i + p
                    for u in range(2):
                        if not (isinstance(i, int) and i == 0):
                            sp.wait_ge(normed[u], 2 * j - 2)
                            hold(sp)
                            sp.wait_ge(x_kept[p][u], 16 * i)
                            hold(sp)
                        sp.dma_start(xt[:, p, u, :, :], xv[2 * j + u]).then_inc(x_here[p][u], 16)
                pairs(sp, load)
                sp.wait_ge(found, CAP // 8)
                for h in range(2):
                    sp.dma_start(both[:, h, :], cand[h * E:(h + 1) * E, :]).then_inc(moved, 16)

            @block.scalar
            def _(act):
                act.wait_ge(gw_turned, DC)
                nc.scalar.activation(gwT[:, :, :], psG[:, :, :], ACT.Copy).then_inc(gw_ready, 1)
                def pair(i, p, ahead):
                    j = 2 * i + p
                    for u in range(2):
                        act.wait_ge(x_here[p][u], 16 * i + 16)
                        act.dma_start(av[2 * j + u], xt[:, p, u, :, :]).then_inc(x_kept[p][u], 16)
                    for u in range(2):
                        act.wait_ge(turned[u], 4 * j + 4)
                        act.wait_ge(logits[u], 2 * j)
                        nc.scalar.activation(lnT[:, u, :, :], psT[u][:, :, :], ACT.Copy).then_inc(lnT_ok[u], 1)
                    for u in range(2):
                        act.wait_ge(nm_ok[u], j + 1)
                        act.wait_ge(weights[u], 2 * j)
                        for h in range(2):
                            nc.scalar.activation(ex[:, u, h, :], lg[:, u, h, :], ACT.Exp, bias=nm[:, u, h:h + 1],
                                                 accum_out=den[:, u, h:h + 1]).then_inc(exps[u], 1)
                    for u in range(2):
                        act.wait_ge(weights[u], 2 * j + 2)
                        act.dma_start(rv[2 * j + u], row[:, p, u, :, :]).then_inc(row_out[p][u], 16)
                pairs(act, pair)
                for p in range(2):
                    for u in range(2):
                        act.wait_ge(x_kept[p][u], 16 * NI)
                        act.wait_ge(row_out[p][u], 16 * NI)
                act.wait_ge(zero_set, 1)
                for k in range(NZ):
                    act.dma_start(stream_b.rearrange("(p k r) d -> p k (r d)", p=P, k=NZ)[:, k, :], zeros[:, :]).then_inc(zero_out, 16)
                act.dma_start(stream_a[NTOK:NTOK + P, :], zeros[:, 0:D]).then_inc(zero_out, 16)
                act.dma_start(rows[NTOK:NTOK + P, :], zeros[:, 0:ROW]).then_inc(zero_out, 16)
                act.wait_ge(zero_out, 16 * NZ + 32)

            @block.gpsimd
            def _(pool):
                nc.gpsimd.memset(zeros[:, :], 0.0).then_inc(zero_set, 1)
                nc.gpsimd.iota(slot_i[:, :], pattern=[[0, 1]], base=0, channel_multiplier=1).then_inc(desc_set, 1)
                for h in range(2):
                    pool.wait_ge(desc_set, 1 + h)
                    nc.gpsimd.iota(desc[h * E:(h + 1) * E, :], pattern=[[-1, HALF * P]],
                                   base=NTOK - h * HALF * P, channel_multiplier=0).then_inc(desc_set, 1)
                pool.wait_ge(desc_set, 3)
                hold(pool)
                nc.gpsimd.tensor_copy(slot_n[:, :], slot_i[:, :]).then_inc(desc_set, 1)
                def pair(i, p, ahead):
                    j = 2 * i + p
                    for u in range(2):
                        pool.wait_ge(moments[u], 2 * j + 2)
                        hold(pool)
                        nc.gpsimd.tensor_scalar(ve[:, u, :], mv[:, u, :, 1], EPS, None, ALU.add).then_inc(shifted[u], 1)
                        pool.wait_ge(shifted[u], j + 1)
                        pool.wait_ge(normed[u], 2 * j)
                        nc.gpsimd.tensor_tensor(out=rstd[:, u, :], in0=ve[:, u, :], in1=cst["minus_half"][:, 0:2],
                                                op=ALU.pow).then_inc(rstd_ok[u], 1)
                pairs(pool, pair)

            @block.vector
            def _(dve):
                def normalise(i, p):
                    j = 2 * i + p
                    for u in range(2):
                        dve.wait_ge(x_here[p][u], 16 * i + 16)
                        for h in range(2):
                            nc.vector.bn_stats(bs[:, u, h, :], xt[:, p, u, h, :]).then_inc(stats[u], 1)
                    for u in range(2):
                        dve.wait_ge(stats[u], 2 * j + 2)
                        dve.wait_ge(rstd_ok[u], j)
                        hold(dve)
                        for h in range(2):
                            nc.vector.bn_aggr(mv[:, u, h, :], bs[:, u, h, :]).then_inc(moments[u], 1)
                    for u in range(2):
                        dve.wait_ge(rstd_ok[u], j + 1)
                        dve.wait_ge(row_out[p][u], 16 * i)
                        for h in range(2):
                            nc.vector.tensor_scalar(row[:, p, u, h, 0:D], xt[:, p, u, h, :], mv[:, u, h, 0:1],
                                                    rstd[:, u, h:h + 1], ALU.subtract, ALU.mult).then_inc(normed[u], 1)

                def pair(i, p, ahead):
                    j = 2 * i + p
                    if ahead:
                        normalise(i + p, 1 - p)
                    for u in range(2):
                        dve.wait_ge(logits[u], 2 * j + 2)
                        dve.wait_ge(exps[u], 2 * j)
                        nc.vector.tensor_copy(lg[:, u, :, :], psL[u][:, :, :]).then_inc(lg_ok[u], 1)
                    for u in range(2):
                        dve.wait_ge(lg_ok[u], j + 1)
                        hold(dve)
                        for h in range(2):
                            nc.vector.max(out=mx[:, u, h, :], in_=lg[:, u, h, :]).then_inc(top[u], 1)
                    for u in range(2):
                        dve.wait_ge(top[u], 2 * j + 2)
                        nc.vector.tensor_scalar(nm[:, u, :], mx[:, u, :, 0], -1.0, None, ALU.mult).then_inc(nm_ok[u], 1)
                        for h in range(2):
                            nc.vector.match_replace(out=left[:, u, h, :], in_to_replace=mx[:, u, h, :],
                                                    in_values=lg[:, u, h, :], imm_value=-3.0e38).then_inc(cut[u], 1)
                    for u in range(2):
                        dve.wait_ge(cut[u], 2 * j + 2)
                        dve.wait_ge(maskT[u], j)
                        nc.vector.tensor_tensor(out=chosen[:, u, :, :], in0=left[:, u, :, :], in1=lg[:, u, :, :],
                                                op=ALU.not_equal).then_inc(chosen_ok[u], 1)
                    for u in range(2):
                        dve.wait_ge(exps[u], 2 * j + 2)
                        nc.vector.reciprocal(rden[:, u, :], den[:, u, :]).then_inc(rden_ok[u], 1)
                        dve.wait_ge(rden_ok[u], j + 1)
                        for h in range(2):
                            nc.vector.tensor_scalar(row[:, p, u, h, D:ROW], ex[:, u, h, :], rden[:, u, h:h + 1], 0.5,
                                                    ALU.mult, ALU.mult).then_inc(weights[u], 1)
                    if isinstance(i, int) and i + p == 0:
                        dve.wait_ge(desc_set, 4)
                    for u in range(2):
                        dve.wait_ge(maskT[u], j + 1)
                        at = bass.ds((2 * j + u) * P, P)
                        nc.vector.tensor_tensor(out=key[:, at], in0=psM[u][:, :], in1=desc[:, at],
                                                op=ALU.mult).then_inc(keyed[u], 1)
                normalise(0, 0)
                pairs(dve, pair)
                for u in range(2):
                    dve.wait_ge(keyed[u], HALF // 2)
                for r in range(CAP // 8):
                    dve.wait_ge(struck, r)
                    nc.vector.max(out=cand[:, 8 * r:8 * r + 8], in_=key[:, :]).then_inc(found, 1)
                    dve.wait_ge(found, r + 1)
                    nc.vector.match_replace(out=key[:, :], in_to_replace=cand[:, 8 * r:8 * r + 8],
                                            in_values=key[:, :], imm_value=0.0).then_inc(struck, 1)
                dve.wait_ge(moved, 32)
                for r in range(CAP // 8):
                    dve.wait_ge(struck2, r)
                    nc.vector.max(out=best[:, 8 * r:8 * r + 8], in_=both[:, :, :].rearrange("e h c -> e (h c)")).then_inc(found2, 1)
                    dve.wait_ge(found2, r + 1)
                    nc.vector.match_replace(out=both[:, :, :].rearrange("e h c -> e (h c)"),
                                            in_to_replace=best[:, 8 * r:8 * r + 8],
                                            in_values=both[:, :, :].rearrange("e h c -> e (h c)"), imm_value=0.0).then_inc(struck2, 1)
                dve.wait_ge(bestT, 1)
                nc.vector.tensor_scalar(pad[:, :], psG[:, 0, :], 0.0, slot_n[:, 0:1], ALU.is_equal, ALU.mult).then_inc(padded, 1)
                dve.wait_ge(padded, 1)
                nc.vector.tensor_tensor(out=tok[:, :], in0=pad[:, :], in1=psG[:, 0, :], op=ALU.subtract).then_inc(tokened, 1)
                dve.wait_ge(tokened, 1)
                nc.vector.tensor_scalar(slot_tok[:, :], tok[:, :], float(NTOK), None, ALU.add).then_inc(tabled, 1)
                dve.wait_ge(tabled, 1)

            @block.tensor
            def _(pe):
                pe.wait_ge(gw_here, 16)
                for c in range(DC):
                    nc.tensor.transpose(psG[:, c, :], gw_in[:, c * P:(c + 1) * P], cst["ident"][0:E, 0:E]).then_inc(gw_turned, 1)
                pe.wait_ge(gw_ready, 1)
                def pair(i, p, ahead):
                    j = 2 * i + p
                    for u in range(2):
                        pe.wait_ge(normed[u], 2 * j + 2)
                        pe.wait_ge(lnT_ok[u], j)
                        for h in range(2):
                            for c in range(DC):
                                nc.tensor.transpose(psT[u][:, c, h * P:(h + 1) * P], row[:, p, u, h, c * P:(c + 1) * P],
                                                    cst["ident"][:, :]).then_inc(turned[u], 1)
                    for u in range(2):
                        pe.wait_ge(lnT_ok[u], j + 1)
                        pe.wait_ge(lg_ok[u], j)
                        for h in range(2):
                            for c in range(DC):
                                mm = nc.tensor.matmul(psL[u][:, h, :], lnT[:, u, c, h * P:(h + 1) * P], gwT[:, c, :],
                                                      start=(c == 0), stop=(c == DC - 1))
                            mm.then_inc(logits[u], 1)
                    for u in range(2):
                        pe.wait_ge(chosen_ok[u], j + 1)
                        pe.wait_ge(keyed[u], j)
                        nc.tensor.transpose(psM[u][:, :], chosen[:, u, :, :].rearrange("p h e -> p (h e)"),
                                            cst["ident"][:, :]).then_inc(maskT[u], 1)
                pairs(pe, pair)
                pe.wait_ge(found2, CAP // 8)
                nc.tensor.transpose(psG[:, 0, :], best[:, :], cst["ident"][0:E, 0:E]).then_inc(bestT, 1)
        clear_semaphores(nc, mem)


def moe_experts(nc, cst, tag, rows, w_gate, w_up, w_down, slot_tok, stream_a, stream_b, pool_dma, run, wide=None):
    U = 8
    V = 4
    AHEAD = 4
    SHARES = 2 * (E // U)
    with ExitStack() as ctx:
        mem = Mem(nc, ctx, tag)
        wg = mem.sb("wg", [P, V, DC, F])
        wu = mem.sb("wu", [P, V, DC, F])
        wd = mem.sb("wd", [P, V, D])
        idx = mem.sb("idx", [P, U], U32)
        xg = mem.sb("xg", [P, U, ROW])
        wcol = mem.sb("wcol", [P, U])
        xgT = mem.sb("xgT", [P, 2, DC, CAP])
        sil = mem.sb("sil", [P, 2, CAP])
        hT = mem.sb("hT", [P, 2, CAP])
        y = mem.sb("y", [P, V, D])
        psX = [mem.ps(f"psX{u}", [P, DC, CAP]) for u in range(2)]
        psH = [mem.ps(f"psH{u}", [P, 2, CAP]) for u in range(2)]
        psY = [mem.ps(f"psY{u}", [P, D]) for u in range(2)]
        w_here = [mem.sem(f"w_here{k}") for k in range(V)]
        got, added = pool_dma
        got0, added0 = 16 * run * (E // U), 16 * run * (E // 2)
        idx_ok, wcol_ok = mem.sem("idx_ok"), mem.sem("wcol_ok")
        down = [mem.sem(f"down{k}") for k in range(V)]
        turned, xgT_ok, hid, silued, gated, y_ok = (
            mem.sem2(n) for n in ("turned", "xgT_ok", "hid", "silued", "gated", "y_ok"))
        streams = [stream_a, stream_b]
        if wide:
            wide_src, wide_hi, wide_lo = wide
            wide_raw = mem.sb("wide_raw", [P, 3, WIDE])
            wide_here, wide_high, wide_low = mem.sem("wide_here"), mem.sem("wide_high"), mem.sem("wide_low")

        def share(buf, i):
            return buf[:, :, bass.ds(i * (WIDE // SHARES), WIDE // SHARES)]

        def same_parity(i, k):
            return (U // 2) * i + k // 2

        def same_slot(i, k):
            return (U // V) * i + k // V
        wgv = w_gate.rearrange("e (c p) f -> e p c f", p=P)
        wuv = w_up.rearrange("e (c p) f -> e p c f", p=P)

        with nc.Block() as block:
            @block.sync
            def _(sp):
                def turn(i):
                    for k in range(U):
                        sp.wait_ge(down[k % V], same_slot(i, k))
                        hold(sp)
                        e = U * i + k
                        sp.dma_start(wg[:, k % V, :, :], wgv[e]).then_inc(w_here[k % V], 16)
                        sp.dma_start(wu[:, k % V, :, :], wuv[e]).then_inc(w_here[k % V], 16)
                        sp.dma_start(wd[:, k % V, :], w_down[e]).then_inc(w_here[k % V], 16)
                turn(0)
                with sp.Fori(1, E // U) as i:
                    turn(i)

            @block.gpsimd
            def _(pool):
                def fetch(i, k):
                    e = U * i + k
                    nc.gpsimd.tensor_copy(idx[:, k:k + 1], slot_tok[:, bass.ds(e, 1)]).then_inc(idx_ok, 1)
                    pool.wait_ge(idx_ok, e + 1)
                    hold(pool)
                    pool.indirect_dma_start(out=xg[:, k, :], out_offset=None, in_=rows,
                                            in_offset=bass.IndirectOffsetOnAxis(ap=idx[:, k:k + 1], axis=0)).then_inc(got[k], 16)

                def scatter(i, k):
                    u = k % 2
                    pool.wait_ge(y_ok[u], same_parity(i, k) + 1)
                    pool.wait_ge(added[u], added0 + 16 * same_parity(i, k))
                    hold(pool)
                    pool.indirect_dma_start(out=streams[u], out_offset=bass.IndirectOffsetOnAxis(ap=idx[:, k:k + 1], axis=0),
                                            in_=y[:, k % V, :], in_offset=None, compute_op=ALU.add).then_inc(added[u], 16)

                def weight(i, k):
                    pool.wait_ge(got[k], got0 + 16 * i + 16)
                    hold(pool)
                    nc.gpsimd.tensor_copy(wcol[:, k:k + 1], xg[:, k, bass.ds(D + U * i + k, 1)]).then_inc(wcol_ok, 1)

                def turn(i, first, last):
                    for k in range(U):
                        if k + AHEAD < U:
                            if not first:
                                pool.wait_ge(added[k % 2], added0 + 16 * same_parity(i - 1, k + AHEAD) + 16)
                            fetch(i, k + AHEAD)
                        elif not last:
                            pool.wait_ge(added[k % 2], added0 + 16 * same_parity(i, k + AHEAD - U) + 16)
                            fetch(i + 1, k + AHEAD - U)
                        if k + 1 < U:
                            weight(i, k + 1)
                        elif not last:
                            weight(i + 1, 0)
                        scatter(i, k)

                for k in range(AHEAD):
                    fetch(0, k)
                weight(0, 0)
                turn(0, True, False)
                with pool.Fori(1, E // U - 1) as i:
                    turn(i, False, False)
                turn(E // U - 1, False, True)
                for u in range(2):
                    pool.wait_ge(added[u], added0 + 16 * (E // 2))

            @block.tensor
            def _(pe):
                def rows_turned(i, k):
                    u, n = k % 2, same_parity(i, k)
                    pe.wait_ge(got[k], got0 + 16 * i + 16)
                    pe.wait_ge(xgT_ok[u], n)
                    for c in range(DC):
                        nc.tensor.transpose(psX[u][:, c, :], xg[:, k, c * P:(c + 1) * P], cst["ident"][:, :]).then_inc(turned[u], 1)

                def hidden(i, k):
                    u, n = k % 2, same_parity(i, k)
                    pe.wait_ge(w_here[k % V], 48 * same_slot(i, k) + 48)
                    pe.wait_ge(xgT_ok[u], n + 1)
                    pe.wait_ge(gated[u], n)
                    for g, w in enumerate((wg, wu)):
                        for c in range(DC):
                            mm = nc.tensor.matmul(psH[u][:, g, :], w[:, k % V, c, :], xgT[:, u, c, :],
                                                  start=(c == 0), stop=(c == DC - 1))
                        mm.then_inc(hid[u], 1)

                def result(i, k):
                    u, n = k % 2, same_parity(i, k)
                    pe.wait_ge(gated[u], n + 1)
                    pe.wait_ge(y_ok[u], n)
                    nc.tensor.matmul(psY[u][:, :], hT[:, u, :], wd[:, k % V, :], start=True, stop=True).then_inc(down[k % V], 1)

                def turn(i, first, last):
                    for k in range(U):
                        if k + 1 < U:
                            rows_turned(i, k + 1)
                        elif not last:
                            rows_turned(i + 1, 0)
                        hidden(i, k)
                        if k > 0:
                            result(i, k - 1)
                        elif not first:
                            result(i - 1, U - 1)
                rows_turned(0, 0)
                turn(0, True, False)
                with pe.Fori(1, E // U - 1) as i:
                    turn(i, False, False)
                turn(E // U - 1, False, True)
                result(E // U - 1, U - 1)

            @block.scalar
            def _(act):
                def high_part(j):
                    act.wait_ge(wide_here, 48)
                    nc.scalar.activation(share(wide_hi, j), share(wide_raw, j), ACT.Copy).then_inc(wide_high, 1)

                def load_wide(k):
                    src = wide_src[k]
                    act.dma_start(wide_raw[:, k, :].rearrange("p (c n) -> p c n", n=src.shape[2]), src).then_inc(wide_here, 16)

                def rows_out(i, k):
                    u, n = k % 2, same_parity(i, k)
                    act.wait_ge(turned[u], 2 * n + 2)
                    act.wait_ge(hid[u], 2 * n)
                    nc.scalar.activation(xgT[:, u, :, :], psX[u][:, :, :], ACT.Copy).then_inc(xgT_ok[u], 1)

                def turn(i, last, split):
                    for k in range(U):
                        u, n = k % 2, same_parity(i, k)
                        if k + 1 < U:
                            rows_out(i, k + 1)
                        elif not last:
                            rows_out(i + 1, 0)
                        act.wait_ge(hid[u], 2 * n + 2)
                        act.wait_ge(gated[u], n)
                        nc.scalar.activation(sil[:, u, :], psH[u][:, 0, :], ACT.Silu).then_inc(silued[u], 1)
                        if wide and isinstance(i, int) and i == 0 and k in (0, 3, 6):
                            load_wide(k // 3)
                        if split and k % V == V - 1:
                            high_part(2 * i - 2 + k // V)
                rows_out(0, 0)
                turn(0, False, False)
                with act.Fori(1, E // U - 1) as i:
                    turn(i, False, bool(wide))
                turn(E // U - 1, True, bool(wide))
                if wide:
                    for j in (SHARES - 2, SHARES - 1):
                        high_part(j)

            @block.vector
            def _(dve):
                def low_part(j):
                    dve.wait_ge(wide_high, j + 1)
                    nc.vector.tensor_tensor(out=share(wide_lo, j), in0=share(wide_raw, j), in1=share(wide_hi, j),
                                            op=ALU.subtract).then_inc(wide_low, 1)

                def weighted(i, k, first):
                    u, n = k % 2, same_parity(i, k)
                    dve.wait_ge(down[k % V], same_slot(i, k) + 1)
                    dve.wait_ge(wcol_ok, U * i + k + 1)
                    if not (first and k < V):
                        dve.wait_ge(added[u], added0 + 16 * (n - V // 2 + 1))
                    hold(dve)
                    nc.vector.tensor_scalar(y[:, k % V, :], psY[u][:, :], wcol[:, k:k + 1], None, ALU.mult).then_inc(y_ok[u], 1)

                def turn(i, first, split):
                    for k in range(U):
                        u, n = k % 2, same_parity(i, k)
                        dve.wait_ge(silued[u], n + 1)
                        dve.wait_ge(down[(k - 2) % V], same_slot(i, k - 2) + 1)
                        nc.vector.tensor_tensor(out=hT[:, u, :], in0=psH[u][:, 1, :], in1=sil[:, u, :],
                                                op=ALU.mult).then_inc(gated[u], 1)
                        if k > 0:
                            weighted(i, k - 1, first)
                        elif not first:
                            weighted(i - 1, U - 1, False)
                        if split and k % V == V - 1:
                            low_part(2 * i - 2 + k // V)
                turn(0, True, False)
                with dve.Fori(1, E // U) as i:
                    turn(i, False, bool(wide))
                weighted(E // U - 1, U - 1, False)
                if wide:
                    for j in (SHARES - 2, SHARES - 1):
                        low_part(j)
        clear_semaphores(nc, mem)


def attention_weights(nc, mem, Wq, Wk, Ws, g_norm, lut):
    w = {
        "q": mem.sb("wq", [P, DC, H * DK]), "k": mem.sb("wk", [P, DC, H * DK]), "s": mem.sb("ws", [P, DC, H * M]),
        "norm": mem.sb("g_norm", [P, DV]), "lut": mem.sb("lut_row", [P, NLUT]),
        "here": mem.sem("attention_weights"),
    }
    with nc.Block() as block:
        @block.sync
        def _(sp):
            for name, src in (("q", Wq), ("k", Wk), ("s", Ws)):
                sp.dma_start(w[name][:, :, :], src.rearrange("(c p) n -> p c n", p=P)).then_inc(w["here"], 16)
            sp.dma_start(w["norm"][:, :], g_norm.partition_broadcast(P)).then_inc(w["here"], 16)
            sp.dma_start(w["lut"][:, :], lut.partition_broadcast(P)).then_inc(w["here"], 16)
    return w


def attention(nc, cst, w, tag, stream_a, stream_b, x_out, indices, looked_up):
    HQ = 4
    QPB = H // HQ
    TT = T // P
    NH = HQ // 2
    with ExitStack() as ctx:
        mem = Mem(nc, ctx, tag)
        xab = mem.sb("xab", [P, 2, TT, D])
        xs = mem.sb("xs", [P, TT, D])
        xacc = mem.sb("xacc", [P, TT, D])
        bs = mem.sb("bs", [P, TT, 6])
        mv = mem.sb("mv", [P, TT, 2])
        ve = mem.sb("ve", [P, TT])
        rstd = mem.sb("rstd", [P, TT])
        ln = mem.sb("ln", [P, TT, D])
        lnT = mem.sb("lnT", [P, DC, T])
        lnTp = mem.sb("lnTp", [P, 2, DC, T], F32R)
        norm_half = mem.sb("norm_half", [P, DV])
        qT = mem.sb("qT", [P, NH, T])
        kT = mem.sb("kT", [P, NH, T])
        em = mem.sb("em", [P, TT, HQ * M])
        emT = mem.sb("emT", [P, NH, T])
        v = mem.sb("v", [P, 2, TT, HQ * DV])
        gs = mem.sb("gs", [P, TT, HQ * DV])
        tg = mem.sb("tg", [P, TT, HQ * DV])
        rz = mem.sb("rz", [P, TT, HQ * M])
        at = mem.sb("at", [P, HQ, 3 * P])
        bt = at
        okn = mem.sb("okn", [P, TT * HQ, M])
        mxs = mem.sb("mxs", [P, TT * HQ])
        sm = mem.sb("sm", [P, TT * HQ])
        rsm = mem.sb("rsm", [P, TT * HQ])
        pz = mem.sb("pz", [P, TT, HQ * M])
        pzT = mem.sb("pzT", [P, NH, T])
        sq = mem.sb("sq", [P, TT * HQ, DV])
        ss = mem.sb("ss", [P, TT * HQ])
        ms = mem.sb("ms", [P, TT * HQ])
        orstd = mem.sb("orstd", [P, TT * HQ])
        o1 = mem.sb("o1", [P, TT * HQ, DV])
        o2 = sq.rearrange("p (t h) v -> p t (h v)", t=TT)
        oT = mem.sb("oT", [P, 2, HQ, T], F32R)
        index = mem.sb("index", [P, 3, LCOL], I32)
        pick = mem.sb("pick", [P, 3, LCOL])
        found = mem.sb("found", [P, 2, 3, LCOL])
        psA = [mem.ps(f"psA{k}", [P, 512]) for k in range(2)]
        psB = [mem.ps(f"psB{k}", [P, 512]) for k in range(2)]
        psC = [mem.ps(f"psC{k}", [P, 512]) for k in range(2)]
        psD = mem.ps("psD", [P, 2, 512])

        names = ("x_here x_out_done xs_ok xacc_ok stats moments shifted rstd_ok ln_ok ln_ps lnT_ok norm_ok "
                 "v_ps v_ok q_ps q_ok k_ps k_ok g_ps th_ok tg_ok gs_ok s_ps sc_ok em_ok z_ps rz_ok et_ps et_ok "
                 "at_ps at_ok ok_ps okn_ok mx_ok sub_ok pe_ok sm_ok rsm_ok er_ok pz_ok pzt_ps pzt_ok bt_ps bt_ok "
                 "ov_ps sq_ok ss_ok ms_ok orstd_ok o1_ok o2_ok ot_ps ot_ok out_ps acc_ok "
                 "index_here picked looked looked_out lnTh_ok lnTl_ok otl_ok")
        (x_here, x_out_done, xs_ok, xacc_ok, stats, moments, shifted, rstd_ok, ln_ok, ln_ps, lnT_ok, norm_ok,
         v_ps, v_ok, q_ps, q_ok, k_ps, k_ok, g_ps, th_ok, tg_ok, gs_ok, s_ps, sc_ok, em_ok, z_ps, rz_ok, et_ps, et_ok,
         at_ps, at_ok, ok_ps, okn_ok, mx_ok, sub_ok, pe_ok, sm_ok, rsm_ok, er_ok, pz_ok, pzt_ps, pzt_ok, bt_ps, bt_ok,
         ov_ps, sq_ok, ss_ok, ms_ok, orstd_ok, o1_ok, o2_ok, ot_ps, ot_ok, out_ps, acc_ok,
         index_here, picked, looked, looked_out, lnTh_ok, lnTl_ok, otl_ok) = (
            mem.sem(n) for n in names.split())
        av = stream_a[0:NTOK, :].rearrange("(b t p) d -> b p t d", t=TT, p=P)
        bv = stream_b[0:NTOK, :].rearrange("(b t p) d -> b p t d", t=TT, p=P)
        ov = x_out.rearrange("(b t p) d -> b p t d", t=TT, p=P)

        def over_slots(stat):
            return stat[:, :].unsqueeze(2).to_broadcast([P, TT * HQ, M])

        with nc.Block() as block:
            @block.sync
            def _(sp):
                def load(b):
                    sp.dma_start(xab[:, 0, :, :], av[b]).then_inc(x_here, 16)
                    sp.dma_start(xab[:, 1, :, :], bv[b]).then_inc(x_here, 16)

                def load_index(b):
                    for k in range(3):
                        sp.dma_start(index[:, k, :], flat_rows(indices[k])[:, bass.ds(b * LCOL, LCOL)]).then_inc(index_here, 16)

                def store_looked_up(b):
                    sp.wait_ge(looked, NLUT * b + NLUT)
                    hold(sp)
                    for k in range(3):
                        sp.dma_start(flat_rows(looked_up[k])[:, bass.ds(b * LCOL, LCOL)], found[:, (NLUT - 1) % 2, k, :]).then_inc(looked_out, 16)

                def store(b):
                    sp.wait_ge(acc_ok, QPB * b + QPB + 1)
                    hold(sp)
                    sp.dma_start(ov[b], xacc[:, :, :]).then_inc(x_out_done, 16)

                load(0)
                load_index(0)
                def turn(b):
                    sp.wait_ge(xs_ok, b + 1)
                    hold(sp)
                    load(b + 1)
                    store_looked_up(b)
                    load_index(b + 1)
                    store(b)
                turn(0)
                with sp.Fori(1, B - 1) as b:
                    turn(b)
                store_looked_up(B - 1)
                store(B - 1)
                sp.wait_ge(x_out_done, 16 * B)
                sp.wait_ge(looked_out, 48 * B)

            @block.gpsimd
            def _(pool):
                def add_stream(b):
                    pool.wait_ge(x_here, 32 * b + 32)
                    pool.wait_ge(xacc_ok, b)
                    nc.gpsimd.tensor_tensor(out=xs[:, :, :], in0=xab[:, 0, :, :], in1=xab[:, 1, :, :], op=ALU.add).then_inc(xs_ok, 1)

                def rstd_of_stream(b):
                    pool.wait_ge(moments, TT * b + TT)
                    hold(pool)
                    nc.gpsimd.tensor_scalar(ve[:, :], mv[:, :, 1], EPS, None, ALU.add).then_inc(shifted, 1)
                    pool.wait_ge(shifted, b + 1)
                    nc.gpsimd.tensor_tensor(out=rstd[:, :], in0=ve[:, :], in1=cst["minus_half"][:, 0:TT], op=ALU.pow).then_inc(rstd_ok, 1)

                def gate(m):
                    for t in range(TT):
                        pool.wait_ge(tg_ok, TT * m + t + 1)
                        nc.gpsimd.tensor_tensor(out=gs[:, t, :].rearrange("p (h v) -> p h v", v=DV),
                                                in0=tg[:, t, :].rearrange("p (h v) -> p h v", v=DV),
                                                in1=norm_half[:, :].unsqueeze(1).to_broadcast([P, HQ, DV]),
                                                op=ALU.mult).then_inc(gs_ok, 1)

                def look_up(b, codes):
                    for c in codes:
                        pool.wait_ge(looked, NLUT * b + c)
                        if c == 0:
                            pool.wait_ge(index_here, 48 * b + 48)
                        if c == 1:
                            pool.wait_ge(looked_out, 48 * b)
                        hold(pool)
                        nc.gpsimd.tensor_scalar(found[:, 0, :, :] if c == 0 else pick[:, :, :], index[:, :, :], float(c),
                                                w["lut"][:, c:c + 1], ALU.is_equal, ALU.mult).then_inc(looked if c == 0 else picked, 1)
                        if c > 0:
                            pool.wait_ge(picked, (NLUT - 1) * b + c)
                            nc.gpsimd.tensor_tensor(out=found[:, c % 2, :, :], in0=found[:, 1 - c % 2, :, :], in1=pick[:, :, :],
                                                    op=ALU.add).then_inc(looked, 1)

                def slot(b, q, last):
                    n = QPB * b + q
                    ahead = not (last and q == QPB - 1)
                    look_up(b, range(4 * q, 4 * q + 1))
                    if q == 1 and not last:
                        add_stream(b + 1)
                    if q == 2 and not last:
                        rstd_of_stream(b + 1)
                    pool.wait_ge(mx_ok, n + 1)
                    nc.gpsimd.tensor_tensor(out=okn[:, :, :], in0=okn[:, :, :], in1=over_slots(mxs), op=ALU.subtract).then_inc(sub_ok, 1)
                    pool.wait_ge(pe_ok, n + 1)
                    nc.gpsimd.tensor_tensor(out=pz[:, :, :].rearrange("p t (h m) -> p (t h) m", m=M), in0=okn[:, :, :],
                                            in1=rz[:, :, :].rearrange("p t (h m) -> p (t h) m", m=M), op=ALU.mult).then_inc(er_ok, 1)
                    pool.wait_ge(er_ok, n + 1)
                    pool.wait_ge(rsm_ok, n + 1)
                    nc.gpsimd.tensor_tensor(out=pz[:, :, :].rearrange("p t (h m) -> p (t h) m", m=M),
                                            in0=pz[:, :, :].rearrange("p t (h m) -> p (t h) m", m=M),
                                            in1=over_slots(rsm), op=ALU.mult).then_inc(pz_ok, 1)
                    look_up(b, range(4 * q + 1, 4 * q + 4))
                    pool.wait_ge(ss_ok, n + 1)
                    hold(pool)
                    nc.gpsimd.tensor_scalar(ms[:, :], ss[:, :], 1.0 / DV, EPS, ALU.mult, ALU.add).then_inc(ms_ok, 1)
                    pool.wait_ge(ms_ok, n + 1)
                    nc.gpsimd.tensor_tensor(out=orstd[:, :], in0=ms[:, :], in1=cst["minus_half"][:, 0:TT * HQ], op=ALU.pow).then_inc(orstd_ok, 1)
                    pool.wait_ge(orstd_ok, n + 1)
                    pool.wait_ge(o1_ok, n + 1)
                    nc.gpsimd.tensor_tensor(out=o2[:, :, :].rearrange("p t (h v) -> p (t h) v", v=DV), in0=o1[:, :, :],
                                            in1=orstd[:, :].unsqueeze(2).to_broadcast([P, TT * HQ, DV]), op=ALU.mult).then_inc(o2_ok, 1)
                    if ahead:
                        gate(n + 1)
                    if q == 0:
                        pool.wait_ge(x_out_done, 16 * b)
                        pool.wait_ge(xs_ok, b + 1)
                        hold(pool)
                        nc.gpsimd.tensor_copy(xacc[:, :, :], xs[:, :, :]).then_inc(xacc_ok, 1)

                pool.wait_ge(w["here"], 16 * 5)
                hold(pool)
                nc.gpsimd.tensor_scalar(norm_half[:, :], w["norm"][:, :], 0.5, None, ALU.mult).then_inc(norm_ok, 1)
                pool.wait_ge(norm_ok, 1)
                add_stream(0)
                rstd_of_stream(0)
                gate(0)
                for q in range(QPB):
                    slot(0, q, False)
                with pool.Fori(1, B - 1) as b:
                    for q in range(QPB):
                        slot(b, q, False)
                for q in range(QPB):
                    slot(B - 1, q, True)

            @block.scalar
            def _(act):
                def copy(out, in_, done, scale=1.0):
                    nc.scalar.activation(out, in_, ACT.Copy, scale=scale).then_inc(done, 1)

                def turn_stream(b):
                    act.wait_ge(ln_ps, b + 1)
                    copy(lnT[:, :, :].rearrange("p c t -> p (c t)"), psC[1], lnT_ok)
                    copy(lnTp[:, 0, :, :].rearrange("p c t -> p (c t)"), psC[1], lnTh_ok)

                def value(m, par, t):
                    act.wait_ge(v_ps, TT * m + t + 1)
                    copy(v[:, par, t, :], psA[t], v_ok)

                def query(m):
                    act.wait_ge(q_ps, m + 1)
                    copy(qT[:, :, :].rearrange("p a t -> p (a t)"), psA[0], q_ok, scale=DK ** -0.5)

                def gate_tanh(m):
                    for t in range(TT):
                        act.wait_ge(g_ps, TT * m + t + 1)
                        act.wait_ge(gs_ok, TT * m)
                        nc.scalar.activation(tg[:, t, :], psA[t], ACT.Tanh, scale=0.5).then_inc(th_ok, 1)

                def exp_s(m):
                    act.wait_ge(sc_ok, m + 1)
                    nc.scalar.activation(em[:, :, :], em[:, :, :], ACT.Exp).then_inc(em_ok, 1)

                def slot(b, q, last):
                    n = QPB * b + q
                    ahead = not (last and q == QPB - 1)
                    if q == QPB - 1 and not last:
                        turn_stream(b + 1)
                    act.wait_ge(et_ps, n + 1)
                    copy(emT[:, :, :].rearrange("p a t -> p (a t)"), psC[1], et_ok)
                    if ahead:
                        value(n + 1, (q + 1) % 2, 0)
                    act.wait_ge(sub_ok, n + 1)
                    nc.scalar.activation(okn[:, :, :], okn[:, :, :], ACT.Exp).then_inc(pe_ok, 1)
                    if ahead:
                        value(n + 1, (q + 1) % 2, 1)
                        query(n + 1)
                    act.wait_ge(pzt_ps, n + 1)
                    copy(pzT[:, :, :].rearrange("p a t -> p (a t)"), psC[1], pzt_ok)
                    act.wait_ge(ov_ps, n + 1)
                    nc.scalar.activation(sq[:, :, :].rearrange("p (t h) v -> p t (h v)", t=TT), psD, ACT.Square).then_inc(sq_ok, 1)
                    if ahead:
                        gate_tanh(n + 1)
                        exp_s(n + 1)
                    for a in range(NH):
                        act.wait_ge(ot_ps, NH * n + a + 1)
                        copy(oT[:, 0, 2 * a:2 * a + 2, :].rearrange("p a t -> p (a t)"), psD[:, a, :], ot_ok)

                turn_stream(0)
                value(0, 0, 0)
                value(0, 0, 1)
                query(0)
                gate_tanh(0)
                exp_s(0)
                for q in range(QPB):
                    slot(0, q, False)
                with act.Fori(1, B - 1) as b:
                    for q in range(QPB):
                        slot(b, q, False)
                for q in range(QPB):
                    slot(B - 1, q, True)

            @block.vector
            def _(dve):
                def moments_of_stream(b):
                    dve.wait_ge(xs_ok, b + 1)
                    for t in range(TT):
                        nc.vector.bn_stats(bs[:, t, :], xs[:, t, :]).then_inc(stats, 1)
                    dve.wait_ge(stats, TT * b + TT)
                    hold(dve)
                    for t in range(TT):
                        nc.vector.bn_aggr(mv[:, t, :], bs[:, t, :]).then_inc(moments, 1)

                def normalise_stream(b):
                    dve.wait_ge(rstd_ok, b + 1)
                    for t in range(TT):
                        nc.vector.tensor_scalar(ln[:, t, :], xs[:, t, :], mv[:, t, 0:1], rstd[:, t:t + 1],
                                                ALU.subtract, ALU.mult).then_inc(ln_ok, 1)

                def low_part_of_stream(b):
                    dve.wait_ge(lnTh_ok, b + 1)
                    dve.wait_ge(lnT_ok, b + 1)
                    nc.vector.tensor_tensor(out=lnTp[:, 1, :, :], in0=lnT[:, :, :], in1=lnTp[:, 0, :, :], op=ALU.subtract).then_inc(lnTl_ok, 1)

                def low_part_of_output(n):
                    for a in range(NH):
                        dve.wait_ge(ot_ok, NH * n + a + 1)
                        nc.vector.tensor_tensor(out=oT[:, 1, 2 * a:2 * a + 2, :].rearrange("p a t -> p (a t)"), in0=psD[:, a, :],
                                                in1=oT[:, 0, 2 * a:2 * a + 2, :].rearrange("p a t -> p (a t)"),
                                                op=ALU.subtract).then_inc(otl_ok, 1)

                def add_output(b, n):
                    dve.wait_ge(out_ps, n + 1)
                    dve.wait_ge(xacc_ok, b + 1)
                    dve.wait_ge(acc_ok, n + 1)
                    nc.vector.tensor_tensor(out=xacc[:, :, :].rearrange("p t d -> p (t d)"), in0=psA[1],
                                            in1=xacc[:, :, :].rearrange("p t d -> p (t d)"), op=ALU.add).then_inc(acc_ok, 1)

                def key(m):
                    dve.wait_ge(k_ps, m + 1)
                    nc.vector.tensor_copy(kT[:, :, :].rearrange("p a t -> p (a t)"), psA[1]).then_inc(k_ok, 1)

                def gate(m):
                    for t in range(TT):
                        dve.wait_ge(th_ok, TT * m + t + 1)
                        nc.vector.scalar_tensor_tensor(out=tg[:, t, :], in0=tg[:, t, :], scalar=1.0, in1=psA[t],
                                                       op0=ALU.add, op1=ALU.mult).then_inc(tg_ok, 1)

                def clip(m):
                    dve.wait_ge(s_ps, m + 1)
                    nc.vector.tensor_scalar(em[:, :, :].rearrange("p t m -> p (t m)"), psA[0], -32.0, 32.0,
                                            ALU.max, ALU.min).then_inc(sc_ok, 1)

                def invert_z(m):
                    dve.wait_ge(z_ps, m + 1)
                    nc.vector.reciprocal(rz[:, :, :].rearrange("p t m -> p (t m)"), psC[0]).then_inc(rz_ok, 1)

                def masked(dst, n, ps_ready, done):
                    for h in range(HQ):
                        dve.wait_ge(ps_ready, HQ * n + h + 1)
                        nc.vector.tensor_tensor(out=dst[:, h, :], in0=psB[h % 2][:, 0:3 * P],
                                                in1=cst["causal"][:, :, :].rearrange("p a i -> p (a i)"), op=ALU.mult).then_inc(done, 1)

                def scores(m):
                    masked(at, m, at_ps, at_ok)
                    invert_z(m)

                def slot(b, q, last, first=False):
                    n = QPB * b + q
                    ahead = not (last and q == QPB - 1)
                    if q == QPB - 1 and not last:
                        low_part_of_stream(b + 1)
                    dve.wait_ge(ok_ps, n + 1)
                    dve.wait_ge(rz_ok, n + 1)
                    nc.vector.tensor_tensor(out=okn[:, :, :].rearrange("p a m -> p (a m)"), in0=psA[1],
                                            in1=rz[:, :, :].rearrange("p t m -> p (t m)"), op=ALU.mult).then_inc(okn_ok, 1)
                    dve.wait_ge(okn_ok, n + 1)
                    nc.vector.reduce_max(mxs[:, :], okn[:, :, :], axis=AX.X).then_inc(mx_ok, 1)
                    if not first:
                        low_part_of_output(n - 1)
                    dve.wait_ge(pe_ok, n + 1)
                    nc.vector.reduce_sum(sm[:, :], okn[:, :, :], axis=AX.X).then_inc(sm_ok, 1)
                    dve.wait_ge(sm_ok, n + 1)
                    nc.vector.reciprocal(rsm[:, :], sm[:, :]).then_inc(rsm_ok, 1)
                    if q == 1 and not last:
                        moments_of_stream(b + 1)
                    if q == 2 and not last:
                        normalise_stream(b + 1)
                    if not first:
                        add_output(b - 1 if q == 0 else b, n - 1)
                    if ahead:
                        key(n + 1)
                    masked(bt, n, bt_ps, bt_ok)
                    dve.wait_ge(sq_ok, n + 1)
                    dve.wait_ge(gs_ok, TT * n + TT)
                    nc.vector.tensor_tensor(out=o1[:, :, :].rearrange("p (t h) v -> p t (h v)", t=TT), in0=psD,
                                            in1=gs[:, :, :], op=ALU.mult).then_inc(o1_ok, 1)
                    nc.vector.reduce_sum(ss[:, :], sq[:, :, :], axis=AX.X).then_inc(ss_ok, 1)
                    if ahead:
                        gate(n + 1)
                        clip(n + 1)
                        scores(n + 1)

                nc.vector.memset(mxs[:, :], 0.0).then_inc(acc_ok, 1)
                moments_of_stream(0)
                normalise_stream(0)
                low_part_of_stream(0)
                key(0)
                gate(0)
                clip(0)
                scores(0)
                for q in range(QPB):
                    slot(0, q, False, q == 0)
                with dve.Fori(1, B - 1) as b:
                    for q in range(QPB):
                        slot(b, q, False)
                for q in range(QPB):
                    slot(B - 1, q, True)
                low_part_of_output(QPB * B - 1)
                add_output(B - 1, QPB * B - 1)

            @block.tensor
            def _(pe):
                ident = cst["ident"][:, :]
                tri, ones = cst["causal"][:, 0, :], cst["causal"][:, 1, :]

                def turn_stream(b):
                    pe.wait_ge(ln_ok, TT * b + TT)
                    for t in range(TT):
                        for c in range(DC):
                            mm = nc.tensor.transpose(psC[1][:, c * T + t * P:c * T + (t + 1) * P], ln[:, t, c * P:(c + 1) * P], ident)
                    mm.then_inc(ln_ps, 1)

                def wide(name, t, m, q, ready):
                    for c in range(DC):
                        mm = split_matmul(nc, psA[t], [lnTp[:, part, c, t * P:(t + 1) * P] for part in range(2)],
                                          [w[name][part][:, c, q * HQ * DV:(q + 1) * HQ * DV] for part in range(2)],
                                          c == 0, c == DC - 1)
                    mm.then_inc(ready, 1)

                def narrow(name, dst, q, ready):
                    for a in range(NH):
                        col = (q * NH + a) * 2 * DK
                        for c in range(DC):
                            mm = nc.tensor.matmul(dst[:, a * T:(a + 1) * T], w[name][:, c, col:col + 2 * DK], lnT[:, c, :],
                                                  start=(c == 0), stop=(c == DC - 1))
                    mm.then_inc(ready, 1)

                def value_query(b, m, q):
                    pe.wait_ge(lnTl_ok, b + 1)
                    pe.wait_ge(sc_ok, m)
                    wide("v", 0, m, q, v_ps)
                    pe.wait_ge(okn_ok, m)
                    wide("v", 1, m, q, v_ps)
                    pe.wait_ge(v_ok, TT * m + 1)
                    narrow("q", psA[0], q, q_ps)

                def key(m, q):
                    pe.wait_ge(v_ok, TT * m + 2)
                    pe.wait_ge(acc_ok, m)
                    narrow("k", psA[1], q, k_ps)

                def gate_slots(m, q):
                    pe.wait_ge(q_ok, m + 1)
                    wide("g", 0, m, q, g_ps)
                    pe.wait_ge(k_ok, m + 1)
                    wide("g", 1, m, q, g_ps)
                    pe.wait_ge(tg_ok, TT * m + 1)
                    for t in range(TT):
                        for c in range(DC):
                            mm = nc.tensor.matmul(psA[0][:, t * HQ * M:(t + 1) * HQ * M], lnT[:, c, t * P:(t + 1) * P],
                                                  w["s"][:, c, q * HQ * M:(q + 1) * HQ * M], start=(c == 0), stop=(c == DC - 1))
                    mm.then_inc(s_ps, 1)

                def z_sums(m):
                    pe.wait_ge(em_ok, m + 1)
                    pe.wait_ge(rz_ok, m)
                    nc.tensor.matmul(psC[0][:, 0:HQ * M], tri, em[:, 0, :], start=True, stop=True)
                    nc.tensor.matmul(psC[0][:, HQ * M:2 * HQ * M], ones, em[:, 0, :], start=True, stop=False)
                    nc.tensor.matmul(psC[0][:, HQ * M:2 * HQ * M], tri, em[:, 1, :], start=False, stop=True).then_inc(z_ps, 1)

                def causal_scores(lhs, rhs, n, ready, read):
                    for h in range(HQ):
                        a, r = h // 2, (h % 2) * DK
                        read(h)
                        nc.tensor.matmul(psB[h % 2][:, 0:2 * P], lhs[r:r + DK, a, 0:P], rhs[r:r + DK, a, 0:T], start=True, stop=True)
                        nc.tensor.matmul(psB[h % 2][:, 2 * P:3 * P], lhs[r:r + DK, a, P:T], rhs[r:r + DK, a, P:T],
                                         start=True, stop=True).then_inc(ready, 1)

                def over_j(dst, lhs, rhs, width, h):
                    nc.tensor.matmul(dst(0, h), lhs[:, h, 0:P], rhs(0, h), start=True, stop=True)
                    nc.tensor.matmul(dst(1, h), lhs[:, h, P:2 * P], rhs(0, h), start=True, stop=False)
                    return nc.tensor.matmul(dst(1, h), lhs[:, h, 2 * P:3 * P], rhs(1, h), start=False, stop=True)

                def output(n, q):
                    pe.wait_ge(otl_ok, NH * n + NH)
                    for t in range(TT):
                        for h in range(HQ):
                            mm = split_matmul(nc, psA[1][:, t * D:(t + 1) * D], [oT[:, part, h, t * P:(t + 1) * P] for part in range(2)],
                                              [w["o"][part][:, q * HQ + h, :] for part in range(2)], h == 0, h == HQ - 1)
                    mm.then_inc(out_ps, 1)

                def scores(m):
                    pe.wait_ge(q_ok, m + 1)
                    pe.wait_ge(k_ok, m + 1)

                    def b_free_a(h):
                        if h < 2:
                            pe.wait_ge(bt_ok, HQ * m)
                        else:
                            pe.wait_ge(at_ok, HQ * m + h - 1)
                    causal_scores(kT, qT, m, at_ps, b_free_a)

                def slot(b, q, last, first=False):
                    n = QPB * b + q
                    ahead = not (last and q == QPB - 1)
                    bn, qn = (b, q + 1) if q < QPB - 1 else (b + 1, 0)
                    pe.wait_ge(pzt_ok, n)
                    if q == QPB - 1 and not last:
                        turn_stream(b + 1)
                    pe.wait_ge(tg_ok, TT * n + TT)
                    for h in range(HQ):
                        pe.wait_ge(at_ok, HQ * n + h + 1)
                        mm = over_j(lambda t, h: psA[1][:, (t * HQ + h) * M:(t * HQ + h + 1) * M], at,
                                    lambda t, h: em[:, t, h * M:(h + 1) * M], M, h)
                    mm.then_inc(ok_ps, 1)
                    if q == QPB - 1 and not last:
                        pe.wait_ge(lnTh_ok, b + 2)
                    for t in range(TT):
                        for a in range(NH):
                            mm = nc.tensor.transpose(psC[1][:, a * T + t * P:a * T + (t + 1) * P], em[:, t, a * P:(a + 1) * P], ident)
                    mm.then_inc(et_ps, 1)
                    if ahead:
                        value_query(bn, n + 1, qn)
                    if not first:
                        if ahead:
                            pe.wait_ge(v_ok, TT * n + 2 * TT)
                        else:
                            pe.wait_ge(okn_ok, n + 1)
                        output(n - 1, (q - 1) % QPB)
                    pe.wait_ge(pz_ok, n + 1)
                    pe.wait_ge(et_ok, n + 1)
                    for t in range(TT):
                        for a in range(NH):
                            mm = nc.tensor.transpose(psC[1][:, a * T + t * P:a * T + (t + 1) * P], pz[:, t, a * P:(a + 1) * P], ident)
                    mm.then_inc(pzt_ps, 1)
                    if ahead:
                        key(n + 1, qn)
                    pe.wait_ge(pzt_ok, n + 1)

                    def b_free_b(h):
                        pe.wait_ge(at_ok if h < 2 else bt_ok, HQ * n + (4 if h < 2 else h - 1))
                    causal_scores(emT, pzT, n, bt_ps, b_free_b)
                    pe.wait_ge(v_ok, TT * n + TT)
                    pe.wait_ge(otl_ok, NH * n)
                    for h in range(HQ):
                        pe.wait_ge(bt_ok, HQ * n + h + 1)
                        mm = over_j(lambda t, h: psD[:, t, h * DV:(h + 1) * DV], bt,
                                    lambda t, h: v[:, q % 2, t, h * DV:(h + 1) * DV], DV, h)
                    mm.then_inc(ov_ps, 1)
                    if ahead:
                        gate_slots(n + 1, qn)
                        scores(n + 1)
                        z_sums(n + 1)
                    pe.wait_ge(o2_ok, n + 1)
                    for h in range(HQ):
                        for t in range(TT):
                            mm = nc.tensor.transpose(psD[:, h // 2, (h % 2) * T + t * P:(h % 2) * T + (t + 1) * P],
                                                     o2[:, t, h * DV:(h + 1) * DV], ident)
                        if h % 2:
                            mm.then_inc(ot_ps, 1)

                pe.wait_ge(w["here"], 16 * 5)
                turn_stream(0)
                value_query(0, 0, 0)
                key(0, 0)
                gate_slots(0, 0)
                scores(0)
                z_sums(0)
                for q in range(QPB):
                    slot(0, q, False, q == 0)
                with pe.Fori(1, B - 1) as b:
                    for q in range(QPB):
                        slot(b, q, False)
                for q in range(QPB):
                    slot(B - 1, q, True)
                pe.wait_ge(acc_ok, QPB * B)
                output(QPB * B - 1, QPB - 1)
        clear_semaphores(nc, mem)


def turn_matrices(nc, tag, cst, groups):
    NB = 4
    with ExitStack() as ctx:
        mem = Mem(nc, ctx, tag)
        ps = [mem.ps(f"ps{k}", [P, 512]) for k in range(NB)]
        turned, high_ok, left_ps = mem.sem("turned"), mem.sem("high_ok"), mem.sem("left_ps")
        with nc.Block() as block:
            @block.tensor
            def _(pe):
                for k, (high, low, srcs) in enumerate(groups):
                    if k >= NB:
                        pe.wait_ge(left_ps, k - NB + 1)
                    at = 0
                    for src in srcs:
                        rows, cols = src.shape
                        mm = nc.tensor.transpose(ps[k % NB][0:cols, at:at + rows], src, cst["ident"][0:rows, 0:rows])
                        at += rows
                    mm.then_inc(turned, 1)

            @block.scalar
            def _(act):
                for k, (high, low, srcs) in enumerate(groups):
                    if low is not None:
                        act.wait_ge(turned, k + 1)
                        nc.scalar.activation(high, ps[k % NB][0:high.shape[0], 0:high.shape[1]], ACT.Copy).then_inc(high_ok, 1)

            @block.vector
            def _(dve):
                split = 0
                for k, (high, low, srcs) in enumerate(groups):
                    whole = ps[k % NB][0:high.shape[0], 0:high.shape[1]]
                    if low is None:
                        dve.wait_ge(turned, k + 1)
                        nc.vector.tensor_copy(high, whole).then_inc(left_ps, 1)
                    else:
                        split += 1
                        dve.wait_ge(high_ok, split)
                        nc.vector.tensor_tensor(out=low, in0=whole, in1=high, op=ALU.subtract).then_inc(left_ps, 1)
        clear_semaphores(nc, mem)


def ffn_groups(w_gu, w_dn, wgT, wuT, wdT):
    groups = []
    for w, dst in ((w_gu[0], wgT), (w_gu[1], wuT)):
        for c in range(DC):
            for f0 in range(0, FT, 4):
                srcs = [w[0:(P if f < FT - 1 else FLAST), f, c * P:(c + 1) * P] for f in range(f0, min(f0 + 4, FT))]
                end = min((f0 + 4) * P, INTER)
                groups.append((dst[:, 0, c, f0 * P:end], dst[:, 1, c, f0 * P:end], srcs))
    for f in range(FT):
        n = P if f < FT - 1 else FLAST
        groups.append((wdT[0:n, 0, f, :], wdT[0:n, 1, f, :], [w_dn[:, c, f * P:f * P + n] for c in range(DC)]))
    return groups


def hgrn_groups(raw, turned):
    return [(turned[:, k, c, :], None, [raw[:, k, r, c * P:(c + 1) * P] for r in range(DC)])
            for k in range(4) for c in range(DC)]


def split_matmul(nc, out, lhs, rhs, first, last):
    nc.tensor.matmul(out, lhs[0], rhs[0], start=first, stop=False)
    nc.tensor.matmul(out, lhs[0], rhs[1], start=False, stop=False)
    return nc.tensor.matmul(out, lhs[1], rhs[0], start=False, stop=last)


def lut_ffn(nc, cst, tag, sources, x_out, wgT, wuT, wdT):
    G = 4
    NU = NTILE // G
    with ExitStack() as ctx:
        mem = Mem(nc, ctx, tag)
        two = len(sources) == 2
        xt = mem.sb("xt", [P, 2, G, D])
        xb = mem.sb("xb", [P, G, D])
        res = mem.sb("res", [P, 2, G, D])
        bs = mem.sb("bs", [P, G, 6])
        mv = mem.sb("mv", [P, G, 2])
        ve = mem.sb("ve", [P, G])
        rstd = mem.sb("rstd", [P, G])
        ln = mem.sb("ln", [P, G, D])
        lnT = mem.sb("lnT", [P, 2, 2, DC, G * P], F32R)
        sil = mem.sb("sil", [P, 2, G * P])
        hs = mem.sb("hs", [P, 2, G * P])
        hT = mem.sb("hT", [P, 2, 2, FT, G * P], F32R)
        y = mem.sb("y", [P, G, D])
        psT = [mem.ps(f"psT{c}", [P, G * P]) for c in range(DC)]
        psG = [mem.ps(f"psG{k}", [P, G * P]) for k in range(2)]
        psU = [mem.ps(f"psU{k}", [P, G * P]) for k in range(2)]
        psY = [mem.ps(f"psY{k}", [P, 2 * D]) for k in range(2)]
        names = ("x_here added res_ok stats moments shifted rstd_ok ln_ok ln_ps lnT_hi lnT_lo gate_ps up_ps sil_ok h_ok "
                 "h_hi h_lo down_ps y_ok y_out")
        (x_here, added, res_ok, stats, moments, shifted, rstd_ok, ln_ok, ln_ps, lnT_hi, lnT_lo, gate_ps, up_ps, sil_ok,
         h_ok, h_hi, h_lo, down_ps, y_ok, y_out) = (mem.sem(n) for n in names.split())
        sv = [s[0:NTOK, :].rearrange("(m g p) d -> m p g d", g=G, p=P) for s in sources]
        yv = x_out.rearrange("(m g p) d -> m p g d", g=G, p=P)

        def rows_of(f):
            return P if f < FT - 1 else FLAST

        def units(engine, body):
            body(0, 0, True, False)
            body(1, 1, True, True)
            with engine.Fori(1, NU // 2 - 1) as i:
                for u in range(2):
                    body(2 * i + u, u, True, True)
            body(NU - 2, 0, True, True)
            body(NU - 1, 1, False, True)

        with nc.Block() as block:
            @block.sync
            def _(sp):
                def load(m, u):
                    if two:
                        sp.dma_start(xb[:, :, :], sv[1][m]).then_inc(x_here, 16)
                    sp.dma_start(xt[:, u, :, :], sv[0][m]).then_inc(x_here, 16)

                def store(m):
                    sp.wait_ge(y_ok, 2 * m + 2)
                    hold(sp)
                    sp.dma_start(yv[m], y[:, :, :]).then_inc(y_out, 16)

                def unit(m, u, ahead, behind):
                    if ahead:
                        sp.wait_ge(moments, G * m + G)
                        hold(sp)
                        sp.wait_ge(res_ok, m + 1)
                        hold(sp)
                        sp.wait_ge(ln_ok, G * m)
                        hold(sp)
                        load(m + 1, 1 - u)
                    if behind:
                        store(m - 1)
                load(0, 0)
                units(sp, unit)
                store(NU - 1)
                sp.wait_ge(y_out, 16 * NU)

            @block.gpsimd
            def _(pool):
                def norm(m, u, used):
                    if two:
                        pool.wait_ge(x_here, 32 * m + 32)
                        nc.gpsimd.tensor_tensor(out=xt[:, u, :, :], in0=xt[:, u, :, :], in1=xb[:, :, :], op=ALU.add).then_inc(added, 1)
                    pool.wait_ge(moments, G * m + G)
                    hold(pool)
                    nc.gpsimd.tensor_scalar(ve[:, :], mv[:, :, 1], EPS, None, ALU.add).then_inc(shifted, 1)
                    pool.wait_ge(shifted, m + 1)
                    nc.gpsimd.tensor_tensor(out=rstd[:, :], in0=ve[:, :], in1=cst["minus_half"][:, 0:G], op=ALU.pow).then_inc(rstd_ok, 1)
                    if used:
                        pool.wait_ge(y_ok, 2 * m - 2)
                        hold(pool)
                    nc.gpsimd.tensor_copy(res[:, u, :, :], xt[:, u, :, :]).then_inc(res_ok, 1)

                def unit(m, u, ahead, behind):
                    if ahead:
                        norm(m + 1, 1 - u, behind)
                norm(0, 0, False)
                units(pool, unit)

            @block.scalar
            def _(act):
                def turn(m, u):
                    act.wait_ge(ln_ps, m + 1)
                    for c in range(DC):
                        nc.scalar.activation(lnT[:, u, 0, c, :], psT[c], ACT.Copy).then_inc(lnT_hi, 1)

                def high(m, u, f):
                    act.wait_ge(h_ok, FT * m + f + 1)
                    nc.scalar.activation(hT[0:rows_of(f), u, 0, f, :], hs[0:rows_of(f), f % 2, :], ACT.Copy).then_inc(h_hi, 1)

                def unit(m, u, ahead, behind):
                    for f in range(FT):
                        act.wait_ge(gate_ps, FT * m + f + 1)
                        nc.scalar.activation(sil[0:rows_of(f), f % 2, :], psG[f % 2][0:rows_of(f), :], ACT.Silu).then_inc(sil_ok, 1)
                        if f == 0 and behind:
                            act.wait_ge(down_ps, 2 * m - 2)
                        if f > 0:
                            high(m, u, f - 1)
                        if f == 4 and ahead:
                            turn(m + 1, 1 - u)
                    high(m, u, FT - 1)
                turn(0, 0)
                units(act, unit)

            @block.vector
            def _(dve):
                def moments_of(m, u):
                    if two:
                        dve.wait_ge(added, m + 1)
                    else:
                        dve.wait_ge(x_here, 16 * m + 16)
                    for g in range(G):
                        nc.vector.bn_stats(bs[:, g, :], xt[:, u, g, :]).then_inc(stats, 1)
                    dve.wait_ge(stats, G * m + G)
                    hold(dve)
                    for g in range(G):
                        nc.vector.bn_aggr(mv[:, g, :], bs[:, g, :]).then_inc(moments, 1)

                def normalise(m, u):
                    dve.wait_ge(rstd_ok, m + 1)
                    dve.wait_ge(ln_ps, m)
                    for g in range(G):
                        nc.vector.tensor_scalar(ln[:, g, :], xt[:, u, g, :], mv[:, g, 0:1], rstd[:, g:g + 1],
                                                ALU.subtract, ALU.mult).then_inc(ln_ok, 1)

                def turn(m, u):
                    for c in range(DC):
                        dve.wait_ge(lnT_hi, DC * m + c + 1)
                        nc.vector.tensor_tensor(out=lnT[:, u, 1, c, :], in0=psT[c], in1=lnT[:, u, 0, c, :], op=ALU.subtract).then_inc(lnT_lo, 1)

                def low(m, u, f):
                    dve.wait_ge(h_hi, FT * m + f + 1)
                    n = rows_of(f)
                    nc.vector.tensor_tensor(out=hT[0:n, u, 1, f, :], in0=hs[0:n, f % 2, :], in1=hT[0:n, u, 0, f, :],
                                            op=ALU.subtract).then_inc(h_lo, 1)

                def output(m, u):
                    dve.wait_ge(y_out, 16 * m)
                    dve.wait_ge(res_ok, m + 1)
                    for k in range(2):
                        dve.wait_ge(down_ps, 2 * m + k + 1)
                        nc.vector.scalar_tensor_tensor(out=y[:, 2 * k:2 * k + 2, :].rearrange("p g d -> p (g d)"), in0=psY[k], scalar=0.5,
                                                       in1=res[:, u, 2 * k:2 * k + 2, :].rearrange("p g d -> p (g d)"),
                                                       op0=ALU.mult, op1=ALU.add).then_inc(y_ok, 1)

                def unit(m, u, ahead, behind):
                    for f in range(FT):
                        n = rows_of(f)
                        dve.wait_ge(up_ps, FT * m + f + 1)
                        dve.wait_ge(sil_ok, FT * m + f + 1)
                        if behind or f > 1:
                            dve.wait_ge(h_lo, FT * m + f - 1)
                        nc.vector.tensor_tensor(out=hs[0:n, f % 2, :], in0=psU[f % 2][0:n, :], in1=sil[0:n, f % 2, :],
                                                op=ALU.mult).then_inc(h_ok, 1)
                        if f > 0:
                            low(m, u, f - 1)
                        if f == 0 and ahead:
                            moments_of(m + 1, 1 - u)
                        if f == 2 and ahead:
                            normalise(m + 1, 1 - u)
                        if f == 3 and behind:
                            output(m - 1, 1 - u)
                        if f == 4 and ahead:
                            turn(m + 1, 1 - u)
                    low(m, u, FT - 1)
                moments_of(0, 0)
                normalise(0, 0)
                turn(0, 0)
                units(dve, unit)
                output(NU - 1, 1)

            @block.tensor
            def _(pe):
                def turn(m):
                    pe.wait_ge(ln_ok, G * m + G)
                    pe.wait_ge(lnT_lo, DC * m)
                    for c in range(DC):
                        for g in range(G):
                            mm = nc.tensor.transpose(psT[c][:, g * P:(g + 1) * P], ln[:, g, c * P:(c + 1) * P], cst["ident"][:, :])
                    mm.then_inc(ln_ps, 1)

                def down(m, u):
                    pe.wait_ge(h_lo, FT * m + FT)
                    pe.wait_ge(y_ok, 2 * m)
                    for k in range(2):
                        for g in (2 * k, 2 * k + 1):
                            for f in range(FT):
                                n = rows_of(f)
                                mm = split_matmul(nc, psY[k][:, (g % 2) * D:(g % 2 + 1) * D],
                                                  [hT[0:n, u, part, f, g * P:(g + 1) * P] for part in range(2)],
                                                  [wdT[0:n, part, f, :] for part in range(2)], f == 0, f == FT - 1)
                        mm.then_inc(down_ps, 1)

                def unit(m, u, ahead, behind):
                    pe.wait_ge(lnT_lo, DC * m + DC)
                    for f in range(FT):
                        n = rows_of(f)
                        if behind or f > 1:
                            pe.wait_ge(h_ok, FT * m + f - 1)
                        for w, ps, ready in ((wgT, psG, gate_ps), (wuT, psU, up_ps)):
                            for c in range(DC):
                                mm = split_matmul(nc, ps[f % 2][0:n, :], [w[:, part, c, f * P:f * P + n] for part in range(2)],
                                                  [lnT[:, u, part, c, :] for part in range(2)], c == 0, c == DC - 1)
                            mm.then_inc(ready, 1)
                        if f == 1 and behind:
                            down(m - 1, 1 - u)
                        if f == 3 and ahead:
                            turn(m + 1)
                turn(0)
                units(pe, unit)
                down(NU - 1, 1)
        clear_semaphores(nc, mem)


def hgrn(nc, cst, tag, x_in, x_out, wT, norm_w):
    R = 4
    TT = T // P
    with ExitStack() as ctx:
        mem = Mem(nc, ctx, tag)
        xt = mem.sb("xt", [P, R, TT, D])
        nw = mem.sb("nw", [P, DC])
        nwh = mem.sb("nwh", [P, DC])
        bs = mem.sb("bs", [P, TT, 6])
        mv = mem.sb("mv", [P, TT, 2])
        ve = mem.sb("ve", [P, TT])
        rstd = mem.sb("rstd", [P, TT])
        ln = mem.sb("ln", [P, TT, D])
        lnT = mem.sb("lnT", [P, DC, T])
        ti, tf, tg, ai, ag, gate, rest, val, o, osq, pT = (
            mem.sb(n, [P, DC, T]) for n in "ti tf tg ai ag gate rest val o osq pT".split())
        ms = mem.sb("ms", [P, TT])
        orstd = mem.sb("orstd", [P, TT])
        y = mem.sb("y", [P, 2, TT, D])
        psI = mem.ps("psI", [P, DC * T])
        psF = mem.ps("psF", [P, DC * T])
        psG = mem.ps("psG", [P, DC * T])
        psI2 = mem.ps("psI2", [P, DC * T])
        psG2 = mem.ps("psG2", [P, DC * T])
        psT = mem.ps("psT", [P, DC * T])
        psS = mem.ps("psS", [P, TT])
        psY = mem.ps("psY", [P, TT * D])
        I, Gt = [psI, psI2], [psG, psG2]
        names = ("nw_here nw_ok stats moments shifted rstd_ok ln_ok ln_ps lnT_ok i_ps f_ps g_ps ti_ok tf_ok tg_ok "
                 "ai_ok ag_ok gate_ok rest_ok val_ok o_ok osq_ok ss_ps ms_ok orstd_ok pT_ok y_ps y_ok y_out")
        (nw_here, nw_ok, stats, moments, shifted, rstd_ok, ln_ok, ln_ps, lnT_ok, i_ps, f_ps, g_ps, ti_ok, tf_ok,
         tg_ok, ai_ok, ag_ok, gate_ok, rest_ok, val_ok, o_ok, osq_ok, ss_ps, ms_ok, orstd_ok, pT_ok, y_ps, y_ok, y_out) = (
            mem.sem(n) for n in names.split())
        x_here = mem.sem2("x_of_parity")
        xv = x_in.rearrange("(b t p) d -> b p t d", t=TT, p=P)
        yv = x_out.rearrange("(b t p) d -> b p t d", t=TT, p=P)

        def flat(a):
            return a.rearrange("p c t -> p (c t)")

        def slots(engine, body):
            for k in range(R):
                body(k, k, True, True)
            with engine.Fori(1, B // R - 1) as i:
                for k in range(R):
                    body(R * i + k, k, True, True)
            for k in range(R):
                body(B - R + k, k, k < R - 1, k < R - 2)

        with nc.Block() as block:
            @block.sync
            def _(sp):
                def load(b, k):
                    sp.dma_start(xt[:, k, :, :], xv[b]).then_inc(x_here[k % 2], 16)

                def slot(b, k, ahead, ahead2):
                    if ahead2:
                        sp.wait_ge(y_ok, 2 * b)
                        hold(sp)
                        sp.wait_ge(moments, TT * b + TT)
                        hold(sp)
                        load(b + 2, (k + 2) % R)
                    sp.wait_ge(y_ok, 2 * b + 2)
                    hold(sp)
                    sp.dma_start(yv[b], y[:, k % 2, :, :]).then_inc(y_out, 16)
                load(0, 0)
                load(1, 1)
                with nc.allow_non_contiguous_dma(reason="256 words, once"):
                    sp.dma_start(nw[:, :], norm_w.rearrange("(c p) -> p c", p=P)).then_inc(nw_here, 16)
                slots(sp, slot)
                sp.wait_ge(y_out, 16 * B)

            @block.gpsimd
            def _(pool):
                def norm(b):
                    pool.wait_ge(moments, TT * b + TT)
                    hold(pool)
                    nc.gpsimd.tensor_scalar(ve[:, :], mv[:, :, 1], EPS, None, ALU.add).then_inc(shifted, 1)
                    pool.wait_ge(shifted, b + 1)
                    nc.gpsimd.tensor_tensor(out=rstd[:, :], in0=ve[:, :], in1=cst["minus_half"][:, 0:TT], op=ALU.pow).then_inc(rstd_ok, 1)

                def slot(b, k, ahead, ahead2):
                    pool.wait_ge(tf_ok, b + 1)
                    pool.wait_ge(o_ok, DC * b)
                    hold(pool)
                    nc.gpsimd.tensor_scalar(gate[:, :, :], tf[:, :, :], 0.5, 0.5, ALU.mult, ALU.add).then_inc(gate_ok, 1)
                    nc.gpsimd.tensor_scalar(rest[:, :, :], tf[:, :, :], -0.25, 0.25, ALU.mult, ALU.add).then_inc(rest_ok, 1)
                    pool.wait_ge(rest_ok, b + 1)
                    pool.wait_ge(ai_ok, b + 1)
                    nc.gpsimd.tensor_tensor(out=val[:, :, :], in0=ai[:, :, :], in1=rest[:, :, :], op=ALU.mult).then_inc(val_ok, 1)
                    if ahead2:
                        norm(b + 2)
                    pool.wait_ge(ms_ok, b + 1)
                    nc.gpsimd.tensor_tensor(out=orstd[:, :], in0=ms[:, :], in1=cst["minus_half"][:, 0:TT], op=ALU.pow).then_inc(orstd_ok, 1)
                pool.wait_ge(nw_here, 16)
                hold(pool)
                nc.gpsimd.tensor_scalar(nwh[:, :], nw[:, :], 0.5, None, ALU.mult).then_inc(nw_ok, 1)
                norm(0)
                norm(1)
                slots(pool, slot)

            @block.scalar
            def _(act):
                def turn(b):
                    act.wait_ge(ln_ps, b + 1)
                    nc.scalar.activation(flat(lnT[:, :, :]), psT, ACT.Copy).then_inc(lnT_ok, 1)

                def tanhs(b, par):
                    act.wait_ge(rest_ok, b)
                    act.wait_ge(ag_ok, b)
                    for ps, dst, ready, done in ((psF, tf, f_ps, tf_ok), (I[par], ti, i_ps, ti_ok), (Gt[par], tg, g_ps, tg_ok)):
                        act.wait_ge(ready, b + 1)
                        nc.scalar.activation(flat(dst[:, :, :]), ps, ACT.Tanh, scale=0.5).then_inc(done, 1)

                def slot(b, k, ahead, ahead2):
                    act.wait_ge(o_ok, DC * b + DC)
                    nc.scalar.activation(osq[:, :, :], o[:, :, :], ACT.Square).then_inc(osq_ok, 1)
                    if ahead:
                        tanhs(b + 1, (k + 1) % 2)
                    if ahead2:
                        turn(b + 2)
                turn(0)
                tanhs(0, 0)
                turn(1)
                slots(act, slot)

            @block.vector
            def _(dve):
                def moments_of(b, k):
                    dve.wait_ge(x_here[k % 2], 8 * (b - k % 2) + 16)
                    for t in range(TT):
                        nc.vector.bn_stats(bs[:, t, :], xt[:, k, t, :]).then_inc(stats, 1)
                    dve.wait_ge(stats, TT * b + TT)
                    hold(dve)
                    for t in range(TT):
                        nc.vector.bn_aggr(mv[:, t, :], bs[:, t, :]).then_inc(moments, 1)

                def normalise(b, k):
                    dve.wait_ge(rstd_ok, b + 1)
                    dve.wait_ge(ln_ps, b)
                    for t in range(TT):
                        nc.vector.tensor_scalar(ln[:, t, :], xt[:, k, t, :], mv[:, t, 0:1], rstd[:, t:t + 1],
                                                ALU.subtract, ALU.mult).then_inc(ln_ok, 1)

                def slot(b, k, ahead, ahead2):
                    dve.wait_ge(ti_ok, b + 1)
                    dve.wait_ge(val_ok, b)
                    nc.vector.scalar_tensor_tensor(out=flat(ai[:, :, :]), in0=flat(ti[:, :, :]), scalar=1.0, in1=I[k % 2],
                                                   op0=ALU.add, op1=ALU.mult).then_inc(ai_ok, 1)
                    dve.wait_ge(tg_ok, b + 1)
                    dve.wait_ge(pT_ok, DC * b)
                    nc.vector.scalar_tensor_tensor(out=flat(ag[:, :, :]), in0=flat(tg[:, :, :]), scalar=1.0, in1=Gt[k % 2],
                                                   op0=ALU.add, op1=ALU.mult).then_inc(ag_ok, 1)
                    dve.wait_ge(gate_ok, b + 1)
                    dve.wait_ge(val_ok, b + 1)
                    dve.wait_ge(osq_ok, b)
                    for c in range(DC):
                        nc.vector.tensor_tensor_scan(o[:, c, :], gate[:, c, :], val[:, c, :], 0.0, ALU.mult, ALU.add).then_inc(o_ok, 1)
                    dve.wait_ge(o_ok, DC * b + DC)
                    dve.wait_ge(y_ps, b)
                    for c in range(DC):
                        nc.vector.scalar_tensor_tensor(out=pT[:, c, :], in0=ag[:, c, :], scalar=nwh[:, c:c + 1], in1=o[:, c, :],
                                                       op0=ALU.mult, op1=ALU.mult).then_inc(pT_ok, 1)
                    if ahead2:
                        moments_of(b + 2, (k + 2) % R)
                    dve.wait_ge(ss_ps, b + 1)
                    nc.vector.tensor_scalar(ms[:, :], psS, 1.0 / D, EPS, ALU.mult, ALU.add).then_inc(ms_ok, 1)
                    if ahead2:
                        normalise(b + 2, (k + 2) % R)
                    dve.wait_ge(orstd_ok, b + 1)
                    dve.wait_ge(y_ps, b + 1)
                    dve.wait_ge(y_out, 16 * b)
                    for t in range(TT):
                        nc.vector.scalar_tensor_tensor(out=y[:, k % 2, t, :], in0=psY[:, t * D:(t + 1) * D], scalar=orstd[:, t:t + 1],
                                                       in1=xt[:, k, t, :], op0=ALU.mult, op1=ALU.add).then_inc(y_ok, 1)
                for b in range(2):
                    moments_of(b, b)
                    normalise(b, b)
                dve.wait_ge(nw_ok, 1)
                slots(dve, slot)

            @block.tensor
            def _(pe):
                def turn(b):
                    pe.wait_ge(ln_ok, TT * b + TT)
                    pe.wait_ge(lnT_ok, b)
                    for c in range(DC):
                        for t in range(TT):
                            mm = nc.tensor.transpose(psT[:, c * T + t * P:c * T + (t + 1) * P], ln[:, t, c * P:(c + 1) * P], cst["ident"][:, :])
                    mm.then_inc(ln_ps, 1)

                def project(b, par):
                    pe.wait_ge(lnT_ok, b + 1)
                    pe.wait_ge(tf_ok, b)
                    for k, ps, ready in ((1, psF, f_ps), (0, I[par], i_ps), (2, Gt[par], g_ps)):
                        if k == 0:
                            pe.wait_ge(ai_ok, b if par else b)
                        for f in range(DC):
                            for c in range(DC):
                                mm = nc.tensor.matmul(ps[:, f * T:(f + 1) * T], wT[:, k, c, f * P:(f + 1) * P], lnT[:, c, :],
                                                      start=(c == 0), stop=(c == DC - 1))
                        mm.then_inc(ready, 1)

                def slot(b, k, ahead, ahead2):
                    if ahead:
                        project(b + 1, (k + 1) % 2)
                    pe.wait_ge(osq_ok, b + 1)
                    pe.wait_ge(ms_ok, b)
                    for t in range(TT):
                        for c in range(DC):
                            mm = nc.tensor.matmul(psS[:, t:t + 1], osq[:, c, t * P:(t + 1) * P], cst["causal"][:, 1, 0:1],
                                                  start=(c == 0), stop=(c == DC - 1))
                    mm.then_inc(ss_ps, 1)
                    pe.wait_ge(pT_ok, DC * b + DC)
                    pe.wait_ge(y_ok, 2 * b)
                    for t in range(TT):
                        for c in range(DC):
                            mm = nc.tensor.matmul(psY[:, t * D:(t + 1) * D], pT[:, c, t * P:(t + 1) * P], wT[:, 3, c, :],
                                                  start=(c == 0), stop=(c == DC - 1))
                    mm.then_inc(y_ps, 1)
                    if ahead2:
                        turn(b + 2)
                turn(0)
                project(0, 0)
                turn(1)
                slots(pe, slot)
        clear_semaphores(nc, mem)


def macaron(nc, x, Wq, Wk, Wv, Wg, Ws, Wo, g_norm, gate_w, w_gate, w_up, w_down,
            Wi1, Wf1, Wg1, Wo1, gnorm1, lut, gate_idx, up_idx, down_idx, out):
    rows = nc.dram_tensor("rows", [NTOK + P, ROW], F32, kind="Internal").ap()
    stream_a = nc.dram_tensor("stream_a", [NTOK + P, D], F32, kind="Internal").ap()
    stream_b = nc.dram_tensor("stream_b", [NTOK + P, D], F32, kind="Internal").ap()
    x_att = nc.dram_tensor("x_att", [NTOK, D], F32, kind="Internal").ap()
    x_ffn = nc.dram_tensor("x_ffn", [NTOK, D], F32, kind="Internal").ap()
    x_hgrn = nc.dram_tensor("x_hgrn", [NTOK, D], F32, kind="Internal").ap()
    looked_up = [nc.dram_tensor(f"looked_up{k}", idx.shape, F32, kind="Internal").ap()
                 for k, idx in enumerate((gate_idx, up_idx, down_idx))]
    with ExitStack() as ctx:
        mem = Mem(nc, ctx)
        slot_tok = mem.sb("slot_tok", [P, E], U32)
        pool_dma = [mem.sem(f"got{k}") for k in range(8)], mem.sem2("added")
        cst = constants(nc, mem)
        with ExitStack() as inner:
            wmem = Mem(nc, inner)
            w = attention_weights(nc, wmem, Wq, Wk, Ws, g_norm, lut)
            moe_router(nc, cst, "r1_", x, gate_w, rows, stream_a, stream_b, slot_tok)
            wide = [wmem.sb(f"wide_{part}", [P, 3, WIDE], F32R) for part in ("high", "low")]
            wide_src = [Wv.rearrange("(c p) n -> p c n", p=P), Wg.rearrange("(c p) n -> p c n", p=P),
                        Wo.rearrange("(h v) d -> v h d", v=DV)]
            moe_experts(nc, cst, "e1_", rows, w_gate, w_up, w_down, slot_tok, stream_a, stream_b, pool_dma, 0,
                        (wide_src, wide[0], wide[1]))
            w["v"], w["g"] = ([part[:, k, :].rearrange("p (c n) -> p c n", c=DC) for part in wide] for k in range(2))
            w["o"] = [part[:, 2, :].rearrange("p (h d) -> p h d", h=H) for part in wide]
            attention(nc, cst, w, "a_", stream_a, stream_b, x_att, (gate_idx, up_idx, down_idx), looked_up)
            clear_semaphores(nc, wmem)
        moe_router(nc, cst, "r2_", x_att, gate_w, rows, stream_a, stream_b, slot_tok)
        moe_experts(nc, cst, "e2_", rows, w_gate, w_up, w_down, slot_tok, stream_a, stream_b, pool_dma, 1)
        w_gu = [mem.sb(f"w_gu{k}", [P, FT, D]) for k in range(2)]
        w_dn = mem.sb("w_down", [P, DC, INTER])
        wgT = mem.sb("wgT", [P, 2, DC, INTER], F32R)
        wuT = mem.sb("wuT", [P, 2, DC, INTER], F32R)
        wdT = mem.sb("wdT", [P, 2, FT, D], F32R)
        h_raw = mem.sb("h_raw", [P, 4, DC, D])
        h_T = mem.sb("h_T", [P, 4, DC, D])
        h_here = mem.sem("h_here")
        with nc.Block() as block:
            @block.sync
            def _(sp):
                for k, src in enumerate((Wi1, Wf1, Wg1, Wo1)):
                    sp.dma_start(h_raw[:, k, :, :], src.rearrange("(r p) n -> p r n", p=P)).then_inc(h_here, 16)
                for k in range(2):
                    sp.dma_start(w_gu[k][:, 0:FT - 1, :], looked_up[k][0:(FT - 1) * P, :].rearrange("(f p) d -> p f d", p=P)).then_inc(h_here, 16)
                    sp.dma_start(w_gu[k][0:FLAST, FT - 1, :], looked_up[k][(FT - 1) * P:INTER, :]).then_inc(h_here, 16)
                sp.dma_start(w_dn[:, :, :], looked_up[2].rearrange("(c p) o -> p c o", p=P)).then_inc(h_here, 16)
                sp.wait_ge(h_here, 16 * 9)
        turn_matrices(nc, "t_", cst, ffn_groups(w_gu, w_dn, wgT, wuT, wdT) + hgrn_groups(h_raw, h_T))
        lut_ffn(nc, cst, "f1_", [stream_a, stream_b], x_ffn, wgT, wuT, wdT)
        hgrn(nc, cst, "h_", x_ffn, x_hgrn, h_T, gnorm1)
        lut_ffn(nc, cst, "f2_", [x_hgrn], out, wgT, wuT, wdT)


_INS = ['L0_attn_hidden_states', 'L0_attn_Wq', 'L0_attn_Wk', 'L0_attn_Wv', 'L0_attn_Wg', 'L0_attn_Ws', 'L0_attn_Wo',
        'L0_attn_g_norm_weight', 'L0_ffn_gate_w', 'L0_ffn_w_gate', 'L0_ffn_w_up', 'L0_ffn_w_down',
        'L1_attn_Wi', 'L1_attn_Wf', 'L1_attn_Wg', 'L1_attn_Wo', 'L1_attn_gnorm_w',
        'L1_ffn_lut', 'L1_ffn_gate_idx', 'L1_ffn_up_idx', 'L1_ffn_down_idx']


def kernel(**inputs):
    import numpy as _np
    import concourse.bacc as _bacc
    from concourse import mybir as _mybir
    from concourse.bass_utils import run_bass_kernel_spmd as _run

    nc = _bacc.Bacc("TRN2", target_bir_lowering=False, num_devices=1)
    arrays, args = {}, []
    for name in _INS:
        a = _np.ascontiguousarray(inputs[name])
        if name == 'L0_attn_hidden_states':
            a = a.reshape(NTOK, D)
        arrays[f"in_{name}"] = a
        args.append(nc.dram_tensor(f"in_{name}", a.shape, _mybir.dt.from_np(a.dtype), kind="ExternalInput").ap())
    out = nc.dram_tensor("out_stream", (NTOK, D), _mybir.dt.float32, kind="ExternalOutput").ap()
    macaron(nc, *args, out)
    r = _run(nc, [arrays], core_ids=[0])
    return r.results[0]["out_stream"].reshape(B, T, D)
```
